# Optimizing a Trainium2 kernel written in Bass

```python
import numpy as np
import jax
import jax.numpy as jnp

def _softmax(x, axis=-1):
    return jax.nn.softmax(x, axis=axis)

def _gelu(x):
    return jax.nn.gelu(x, approximate=True)

def _silu(x):
    return jax.nn.silu(x)

def _sigmoid(x):
    return jax.nn.sigmoid(x)

def _layernorm(x, axis=-1, eps=1e-05):
    m = jnp.mean(x, axis=axis, keepdims=True)
    v = jnp.var(x, axis=axis, keepdims=True)
    return (x - m) / jnp.sqrt(v + eps)

def _scatter_add(tgt, idx, src, axis=0):
    return tgt.at[idx].add(src)

def _segment_sum(src, seg, n):
    return jax.ops.segment_sum(src, seg, n)
kernel_name = 'mk_gnn_ffn_d1_gnn_r8_4c4149'

def setup_inputs(seed: int=0):
    np.random.seed(seed)
    _w = jnp.asarray

    def _rec_inputs():
        import jax
        import jax.numpy as jnp
        _gk = jax.random.key(seed)
        x = -0.0003713 + 1 * jax.random.normal(jax.random.fold_in(_gk, 1), (6250, 256), jnp.float32)
        src = jax.random.randint(jax.random.fold_in(_gk, 2), (100000,), 0, 6250, jnp.int32)
        dst = jnp.minimum((6250 * jax.random.uniform(jax.random.fold_in(_gk, 3), (100000,)) ** 2.0).astype(jnp.int32), 49999)
        _o = jnp.argsort(dst, stable=True)
        src = src[_o]
        dst = dst[_o]
        edge_weight1 = jax.random.uniform(jax.random.fold_in(_gk, 12), (100000, 1), jnp.float32, 0.0, 0.999998)
        return (x, src, dst, edge_weight1)
    x, src, dst, edge_weight1 = _rec_inputs()

    def _L0_gnn_setup():
        import jax, jax.numpy as jnp
        import numpy as np
        N_NODES = 6250
        DIM_H = 256
        N_EDGES = 100000
        LN_EPS = 1e-05

        def _layer_norm(x, g, b):
            mu = jnp.mean(x, axis=-1, keepdims=True)
            var = jnp.mean(jnp.square(x - mu), axis=-1, keepdims=True)
            return (x - mu) * jax.lax.rsqrt(var + LN_EPS) * g + b
        key = jax.random.key(seed)
        ks = jax.random.split(key, 12)
        d = DIM_H

        def lin(k, fan_in, fan_out):
            lim = 1.0 / np.sqrt(fan_in)
            kw, kb = jax.random.split(k)
            W = jax.random.uniform(kw, (fan_in, fan_out), jnp.float32, -lim, lim)
            b = jax.random.uniform(kb, (fan_out,), jnp.float32, -lim, lim)
            return (W, b)
        h = jax.random.normal(ks[0], (N_NODES, d), jnp.float32)
        e = jax.random.randint(ks[1], (2, N_EDGES), 0, N_NODES, jnp.int64)
        d2 = jax.random.uniform(ks[2], (N_EDGES, 1), jnp.float32)
        mW1, mb1 = lin(ks[3], 2 * d + 1, d)
        mW2, mb2 = lin(ks[4], d, d)
        ln_g = jnp.ones((d,), jnp.float32)
        ln_b = jnp.zeros((d,), jnp.float32)
        uW1, ub1 = lin(ks[5], 2 * d, d)
        uW2, ub2 = lin(ks[6], d, d)
        return {'h': h, 'e': e, 'd2': d2, 'mW1': mW1, 'mb1': mb1, 'ln_g': ln_g, 'ln_b': ln_b, 'mW2': mW2, 'mb2': mb2, 'uW1': uW1, 'ub1': ub1, 'uW2': uW2, 'ub2': ub2}
    _L0_gnn_all = _L0_gnn_setup()
    _L0_gnn_in = {k: v for k, v in _L0_gnn_all.items() if k in ('mW1', 'mb1', 'ln_g', 'ln_b', 'mW2', 'mb2', 'uW1', 'ub1', 'uW2', 'ub2')}
    del _L0_gnn_all

    def _L0_ffn_setup():
        import jax, jax.numpy as jnp
        import numpy as np
        NUM_EXPERTS = 8
        TOP_K = 2
        B, S, D = (8, 1024, 256)

        def _moe(tokens, router_w, w1, b1, w2, b2):
            N = tokens.shape[0]
            E = router_w.shape[0]
            logits = tokens.astype(jnp.float32) @ router_w.astype(jnp.float32).T
            probs = jax.nn.softmax(logits, axis=-1)
            rw, re = jax.lax.top_k(probs, TOP_K)
            if TOP_K > 1:
                rw = rw / jnp.maximum(rw.sum(-1, keepdims=True), 1e-12)
            rw = rw.astype(tokens.dtype)
            combine = jnp.zeros((N, E), tokens.dtype).at[jnp.arange(N)[:, None], re].set(rw)
            out = tokens
            for e in range(E):
                h = jax.nn.gelu(tokens @ w1[e] + b1[e], approximate=False)
                y = h @ w2[e] + b2[e]
                out = out + combine[:, e:e + 1] * y
            return out
        key = jax.random.key(seed)
        ks = jax.random.split(key, 4)
        scale = 1.0 / np.sqrt(D).astype(np.float32)
        return {'input_embeddings': jax.random.normal(ks[0], (B, S, D), jnp.float32), 'router_w': jax.random.normal(ks[1], (NUM_EXPERTS, D), jnp.float32) * scale, 'w1': jax.random.normal(ks[2], (NUM_EXPERTS, D, D), jnp.float32) * scale, 'b1': jnp.zeros((NUM_EXPERTS, D), jnp.float32), 'w2': jax.random.normal(ks[3], (NUM_EXPERTS, D, D), jnp.float32) * scale, 'b2': jnp.zeros((NUM_EXPERTS, D), jnp.float32)}
    _L0_ffn_all = _L0_ffn_setup()
    _L0_ffn_in = {k: v for k, v in _L0_ffn_all.items() if k in ('router_w', 'w1', 'b1', 'w2', 'b2')}
    del _L0_ffn_all
    return {'x': x, 'src': src, 'dst': dst, 'edge_weight1': edge_weight1, 'L0_gnn_mW1': _L0_gnn_in['mW1'], 'L0_gnn_mb1': _L0_gnn_in['mb1'], 'L0_gnn_ln_g': _L0_gnn_in['ln_g'], 'L0_gnn_ln_b': _L0_gnn_in['ln_b'], 'L0_gnn_mW2': _L0_gnn_in['mW2'], 'L0_gnn_mb2': _L0_gnn_in['mb2'], 'L0_gnn_uW1': _L0_gnn_in['uW1'], 'L0_gnn_ub1': _L0_gnn_in['ub1'], 'L0_gnn_uW2': _L0_gnn_in['uW2'], 'L0_gnn_ub2': _L0_gnn_in['ub2'], 'L0_ffn_router_w': _L0_ffn_in['router_w'], 'L0_ffn_w1': _L0_ffn_in['w1'], 'L0_ffn_b1': _L0_ffn_in['b1'], 'L0_ffn_w2': _L0_ffn_in['w2'], 'L0_ffn_b2': _L0_ffn_in['b2']}

def reference(x, src, dst, edge_weight1, L0_gnn_mW1, L0_gnn_mb1, L0_gnn_ln_g, L0_gnn_ln_b, L0_gnn_mW2, L0_gnn_mb2, L0_gnn_uW1, L0_gnn_ub1, L0_gnn_uW2, L0_gnn_ub2, L0_ffn_router_w, L0_ffn_w1, L0_ffn_b1, L0_ffn_w2, L0_ffn_b2):
    import jax
    import jax.numpy as jnp

    def _L0_gnn_ref(h, e, d2, mW1, mb1, ln_g, ln_b, mW2, mb2, uW1, ub1, uW2, ub2):
        import jax, jax.numpy as jnp
        import numpy as np
        N_NODES = 6250
        DIM_H = 256
        N_EDGES = 100000
        LN_EPS = 1e-05

        def _layer_norm(x, g, b):
            mu = jnp.mean(x, axis=-1, keepdims=True)
            var = jnp.mean(jnp.square(x - mu), axis=-1, keepdims=True)
            return (x - mu) * jax.lax.rsqrt(var + LN_EPS) * g + b
        ei, ej = (e[0], e[1])
        hi = h[ei]
        hj = h[ej]
        x = jnp.concatenate((hi, hj, d2), axis=-1)
        msg = jax.nn.silu(x @ mW1 + mb1)
        msg = _layer_norm(msg, ln_g, ln_b)
        msg = jax.nn.silu(msg @ mW2 + mb2)
        agg = jax.ops.segment_sum(msg, ei, num_segments=h.shape[0])
        y = jnp.concatenate((h, agg), axis=-1)
        y = jax.nn.silu(y @ uW1 + ub1) @ uW2 + ub2
        return h + y

    def _L0_ffn_ref(input_embeddings, router_w, w1, b1, w2, b2):
        import jax, jax.numpy as jnp
        import numpy as np
        NUM_EXPERTS = 8
        TOP_K = 2
        B, S, D = (8, 1024, 256)

        def _moe(tokens, router_w, w1, b1, w2, b2):
            N = tokens.shape[0]
            E = router_w.shape[0]
            logits = tokens.astype(jnp.float32) @ router_w.astype(jnp.float32).T
            probs = jax.nn.softmax(logits, axis=-1)
            rw, re = jax.lax.top_k(probs, TOP_K)
            if TOP_K > 1:
                rw = rw / jnp.maximum(rw.sum(-1, keepdims=True), 1e-12)
            rw = rw.astype(tokens.dtype)
            combine = jnp.zeros((N, E), tokens.dtype).at[jnp.arange(N)[:, None], re].set(rw)
            out = tokens
            for e in range(E):
                h = jax.nn.gelu(tokens @ w1[e] + b1[e], approximate=False)
                y = h @ w2[e] + b2[e]
                out = out + combine[:, e:e + 1] * y
            return out
        b, s, d = input_embeddings.shape
        tokens = input_embeddings.reshape(b * s, d)
        return _moe(tokens, router_w, w1, b1, w2, b2).reshape(b, s, d)
    edge_index = jnp.stack([src, dst])
    x = x + _L0_gnn_ref(_layernorm(x, axis=-1), edge_index, edge_weight1, L0_gnn_mW1, L0_gnn_mb1, L0_gnn_ln_g, L0_gnn_ln_b, L0_gnn_mW2, L0_gnn_mb2, L0_gnn_uW1, L0_gnn_ub1, L0_gnn_uW2, L0_gnn_ub2)
    x = x + _L0_ffn_ref(_layernorm(x, axis=-1)[None], L0_ffn_router_w, L0_ffn_w1, L0_ffn_b1, L0_ffn_w2, L0_ffn_b2)[0]
    return x

_drawn_inputs = setup_inputs


def setup_inputs(seed=0):
    import zlib

    import numpy as np

    out = dict(_drawn_inputs(seed))
    spreads = {'L0_gnn_ln_g': (1.0, 0.2),
     'L0_gnn_ln_b': (0.0, 0.1),
     'L0_ffn_b1': (0.0, 0.489),
     'L0_ffn_b2': (0.0, 0.333)}
    factors = {'edge_weight1': 28.568, 'L0_gnn_ub1': 6.794}
    for name, (base, spread) in spreads.items():
        noise = np.random.default_rng([zlib.crc32(name.encode()), seed]).standard_normal(out[name].shape)
        drawn = base * np.exp(spread * noise) if base else spread * noise
        out[name] = jnp.asarray(drawn.astype(out[name].dtype))
    for name, factor in factors.items():
        out[name] = (out[name] * factor).astype(out[name].dtype)
    return out
```

```python
from contextlib import ExitStack

import concourse.bass as bass
from concourse import mybir

F32 = mybir.dt.float32
F32R = mybir.dt.float32r
BF16 = mybir.dt.bfloat16
I32 = mybir.dt.int32
U32 = mybir.dt.uint32
ALU = mybir.AluOpType
ACT = mybir.ActivationFunctionType
AX_X = mybir.AxisListType.X
ds = bass.ds

P = 128
D = 256
KC = D // P
NODES = 6250
EDGES = 100000
EXPERTS = 8
LN_EPS = 1e-5

BIN = P - 2
BINS = -(-NODES // BIN)
LAST = NODES - (BINS - 1) * BIN

EP, EC = 125, 800
assert EP * EC == EDGES
GROUP = 2 * P
RING = 6
GROUPS = -(-(EDGES // GROUP + BINS) // RING) * RING
TILES = 2 * GROUPS
SLOTS = TILES * P
WORDS = 4
CHUNK = 200
SC = 20
ROUND = 1.5 * 2 ** 23

NAMES = ["x", "src", "dst", "edge_weight1", "L0_gnn_mW1", "L0_gnn_mb1", "L0_gnn_ln_g", "L0_gnn_ln_b", "L0_gnn_mW2",
         "L0_gnn_mb2", "L0_gnn_uW1", "L0_gnn_ub1", "L0_gnn_uW2", "L0_gnn_ub2", "L0_ffn_router_w", "L0_ffn_w1",
         "L0_ffn_b1", "L0_ffn_w2", "L0_ffn_b2"]


def hold(engine, semaphore, value):
    engine.wait_ge(semaphore, value)
    engine.nop(nofuse=True)


def by_chunks(w):
    return w.rearrange("(c p) n -> p c n", p=P)


def one_row(v):
    return v.rearrange("(o n) -> o n", o=1)


def gnn_ffn(nc, t, out):
    with ExitStack() as whole:
        whole.enter_context(nc.allow_non_contiguous_dma("small transposed parameters"))
        node_rows = whole.enter_context(nc.sbuf_tensor("node_rows", [P, BINS, D], F32))
        dram = {
            "b_rows": nc.dram_tensor("b_rows", (BINS * BIN, D), F32).ap(),
            "u_rows": nc.dram_tensor("u_rows", (BINS * BIN, D), F32).ap(),
            "xh_rows": nc.dram_tensor("xh_rows", (BINS * BIN, D), F32).ap(),
            "sorted_edges": nc.dram_tensor("sorted_edges", (SLOTS, WORDS), F32).ap(),
            "group_bins": nc.dram_tensor("group_bins", (4 * (P - 3),), I32).ap(),
        }
        ident = whole.enter_context(nc.sbuf_tensor("ident", [P, P], F32))
        with ExitStack() as edges:
            kept = {
                "a_at": nc.sbuf_base,
                "a_hi": edges.enter_context(nc.sbuf_tensor("a_hi", [P, BINS, D], F32R)),
                "a_lo": edges.enter_context(nc.sbuf_tensor("a_lo", [P, BINS, D], F32R)),
                "slots": edges.enter_context(nc.sbuf_tensor("slots", [P, TILES, WORDS], F32)),
                "w2_hi": edges.enter_context(nc.sbuf_tensor("w2_hi", [P, KC, D], F32R)),
                "w2_lo": edges.enter_context(nc.sbuf_tensor("w2_lo", [P, KC, D], F32R)),
                "c3": edges.enter_context(nc.sbuf_tensor("c3", [P, D], BF16)),
                "ones3": edges.enter_context(nc.sbuf_tensor("ones3", [P, P], BF16)),
                "iota": edges.enter_context(nc.sbuf_tensor("iota", [P, P], F32)),
            }
            nodes_and_sort(nc, t, dram, node_rows, ident, kept)
            messages(nc, dram, node_rows, ident, kept)
        with ExitStack() as rest:
            turned = rest.enter_context(nc.sbuf_tensor("tokens_t", [P, KC, BINS * BIN], F32))
            combine = rest.enter_context(nc.sbuf_tensor("combine", [P, BINS, EXPERTS], F32))
            update(nc, t, dram, node_rows, ident, turned, combine)
            route(nc, combine)
            experts(nc, t, node_rows, turned, combine, out)


def nodes_and_sort(nc, t, dram, node_rows, ident, kept):
    a_hi, a_lo, slots = kept["a_hi"], kept["a_lo"], kept["slots"]
    with ExitStack() as ctx:
        def sb(name, shape, dt=F32):
            return ctx.enter_context(nc.sbuf_tensor(name, shape, dt))

        def sem(name):
            return ctx.enter_context(nc.semaphore(name))

        def psum(name):
            return ctx.enter_context(nc.psum_tensor(name, [P, 512], F32))

        pay = sb("pay", [P, EC, WORDS])
        row_of = sb("row_of", [P, EC], I32)
        stage_row = sb("stage_row", [P, 2, SC], I32)
        stage_pay = sb("stage_pay", [P, 2, SC, WORDS])
        gbin = sb("gbin", [P, 4])
        gbin_i = sb("gbin_i", [P, 4], I32)
        gidx = sb("gidx", [P, 4])
        before = sb("before", [P, P])
        ones = sb("ones", [P, P])
        w1a = sb("w1a", [P, KC, D])
        w1b = sb("w1b", [P, KC, D])
        u1a = sb("u1a", [P, KC, D])
        b1_all = sb("b1_all", [P, D])
        ub1_all = sb("ub1_all", [P, D])
        ub2_all = sb("ub2_all", [P, D])
        gcol = sb("gcol", [P, KC])
        bcol = sb("bcol", [P, KC])
        mv = sb("mv", [P, BINS, 2])
        rstd = sb("rstd", [P, BINS])
        half = sb("half", [P, BINS])
        st6 = sb("st6", [P, 6])
        st2 = sb("st2", [P, 2])
        h = sb("h", [P, 2, D])
        ht = sb("ht", [P, 2, KC, BIN])
        u_out = sb("u_out", [P, 2, D])
        xh_out = sb("xh_out", [P, 2, D])
        with ExitStack() as early:
            w2 = early.enter_context(nc.sbuf_tensor("w2", [P, KC, D], F32))
        b_out = sb("b_out", [P, 2, D])

        at = [kept["a_at"]]

        def early_sb(name, shape, dt=F32):
            size = 4
            for n in shape[1:]:
                size *= n
            where = at[0]
            at[0] += -(-size // 32) * 32
            return nc.alloc_sbuf_tensor_at(name, shape, dt, offset=where)

        crow = early_sb("crow", [1, 3, D])
        cpart = early_sb("cpart", [1, 3, D], BF16)
        wc = early_sb("wc", [1, D])
        wc_hi = early_sb("wc_hi", [1, D], F32R)
        wc_lo = early_sb("wc_lo", [1, D], F32R)
        at[0] = kept["a_at"] + 4 * BINS * D
        bin_of = early_sb("bin_of", [EP, EC])
        slot_of = early_sb("slot_of", [EP, EC])
        srci = early_sb("srci", [EP, EC], I32)
        dsti = early_sb("dsti", [EP, EC], I32)
        wgt = early_sb("wgt", [EP, EC])
        mask = early_sb("mask", [EP, CHUNK])
        ranks = early_sb("ranks", [EP, CHUNK])
        run = early_sb("run", [EP, BINS])
        counts = early_sb("counts", [EP, BINS])
        groups = early_sb("groups", [P - 3, BINS])
        ends = early_sb("ends", [P - 3, BINS])
        gtmp = early_sb("gtmp", [P - 3, BINS])
        gtmp2 = early_sb("gtmp2", [P - 3, BINS])
        ahead = early_sb("ahead", [P - 3, 4, BINS])

        ps_t = [psum("ps_t0"), psum("ps_t1")]
        ps_a, ps_b, ps_u, ps_n, ps_c = (psum(f"ps_{x}") for x in "abunc")

        edges_in = sem("edges_in")
        x_in = sem("x_in")
        params_in = sem("params_in")
        last_clear = sem("last_clear")
        pool_consts = sem("pool_consts")
        masks_cut = sem("masks_cut")
        prep = sem("prep")
        mask_free = sem("mask_free")
        counted = sem("counted")
        summed = sem("summed")
        base_ready = sem("base_ready")
        ranked = sem("ranked")
        chunk_ready = sem("chunk_ready")
        staged = sem("staged")
        scattered = [sem("scattered0"), sem("scattered1")]
        filled = sem("filled")
        cleared = sem("cleared")
        sorted_in = sem("sorted_in")
        table_ready = sem("table_ready")
        table_out = sem("table_out")
        wc_ready = sem("wc_ready")
        wc_out = sem("wc_out")
        c_ready = sem("c_ready")
        c_out = sem("c_out")
        c_mul = sem("c_mul")
        w2_split = sem("w2_split")
        stats = sem("stats")
        var_ready = sem("var_ready")
        rstd_ready = sem("rstd_ready")
        h_ready = sem("h_ready")
        h_turned = sem("h_turned")
        ht_ready = sem("ht_ready")
        node_mul = sem("node_mul")
        a_hi_ready = sem("a_hi_ready")
        a_lo_ready = sem("a_lo_ready")
        xh_part = sem("xh_part")
        outs_ready = sem("outs_ready")
        outs_stored = [sem("outs_stored0"), sem("outs_stored1")]
        block = ctx.enter_context(nc.Block())
        n_params = 13
        NQ = P - 3
        STEPS = 5 * BINS + 6

        @block.sync
        def _(sp):
            for dst, name in ((srci, "src"), (dsti, "dst")):
                sp.dma_start(dst[:], t[name].rearrange("(p c) -> p c", p=EP)).then_inc(edges_in, 16)
            sp.dma_start(wgt[:], t["edge_weight1"].rearrange("(p c) o -> p (c o)", p=EP)).then_inc(edges_in, 16)
            sp.dma_start(node_rows[0:BIN, 0:BINS - 1, :],
                         t["x"][0:(BINS - 1) * BIN, :].rearrange("(b p) f -> p b f", p=BIN)).then_inc(x_in, 16)
            sp.wait_ge(last_clear, 1)
            sp.dma_start(node_rows[0:LAST, BINS - 1, :], t["x"][(BINS - 1) * BIN:, :]).then_inc(x_in, 16)
            sp.wait_ge(cleared, 1)
            sp.dma_start(dram["sorted_edges"].rearrange("(p t) w -> p t w", p=P), slots[:]).then_inc(filled, 16)
            sp.wait_ge(table_ready, 1)
            sp.dma_start(dram["group_bins"].rearrange("(p j) -> p j", p=NQ), gbin_i[0:NQ, :]).then_inc(table_out, 16)
            sp.wait_ge(wc_ready, 1)
            for table, row in ((a_hi, wc_hi), (a_lo, wc_lo)):
                for p in (BIN, BIN + 1):
                    sp.dma_start(table[p:p + 1, :, :].bitcast(F32),
                                 row[0:1, :].bitcast(F32).rearrange("p (o f) -> p o f", o=1)
                                 .broadcast_to([1, BINS, D])).then_inc(wc_out, 16)
            sp.wait_ge(c_ready, 1)
            for n in range(3):
                sp.dma_start(kept["c3"][n:n + 1, :], cpart[0:1, n, :]).then_inc(c_out, 16)

            with sp.Fori(0, BINS // 2) as j:
                for k in range(2):
                    i = 2 * j + k
                    sp.wait_ge(outs_ready, 3 * i + 3)
                    for buf, name in ((b_out, "b_rows"), (u_out, "u_rows"), (xh_out, "xh_rows")):
                        sp.dma_start(dram[name][ds(i * BIN, BIN), :], buf[0:BIN, k, :]).then_inc(outs_stored[k], 16)
            for k in range(2):
                sp.wait_ge(scattered[k], 16 * EC // 2)
            sp.dma_start(slots[:], dram["sorted_edges"].rearrange("(p t) w -> p t w", p=P)).then_inc(sorted_in, 16)
            sp.wait_ge(sorted_in, 16)
            for k in range(2):
                sp.wait_ge(outs_stored[k], 16 * 3 * BINS // 2)
            sp.wait_ge(wc_out, 16 * 4)
            sp.wait_ge(c_out, 16 * 3)
            sp.wait_ge(table_out, 16)

        @block.gpsimd
        def _(pool):
            nc.gpsimd.memset(ident[:], 0.0).then_inc(pool_consts, 1)
            nc.gpsimd.memset(before[:], 1.0).then_inc(pool_consts, 1)
            nc.gpsimd.memset(ones[:], 1.0).then_inc(pool_consts, 1)
            nc.gpsimd.memset(half[:], -0.5).then_inc(pool_consts, 1)
            nc.gpsimd.iota(kept["iota"][:], [[1, P]], base=0, channel_multiplier=0,
                           allow_small_or_imprecise_dtypes=True).then_inc(pool_consts, 1)
            nc.gpsimd.iota(gidx[:], [[1, 4]], base=0, channel_multiplier=4,
                           allow_small_or_imprecise_dtypes=True).then_inc(pool_consts, 1)
            pool.wait_ge(pool_consts, 6)
            nc.gpsimd.affine_select(out=ident[:], in_=ident[:], compare_op=ALU.not_equal, fill=1.0, base=0,
                                    pattern=[[-1, P]], channel_multiplier=1).then_inc(masks_cut, 1)
            nc.gpsimd.affine_select(out=before[:], in_=before[:], compare_op=ALU.is_ge, fill=0.0, base=-1,
                                    pattern=[[1, P]], channel_multiplier=-1).then_inc(masks_cut, 1)

            def stage_and_scatter(j, k, first):
                s = 2 * j + k
                if not first:
                    hold(pool, scattered[k], 16 * SC * j)
                nc.gpsimd.tensor_copy(stage_row[0:EP, k, :], row_of[0:EP, ds(s * SC, SC)]).then_inc(staged, 1)
                nc.gpsimd.tensor_copy(stage_pay[0:EP, k], pay[0:EP, ds(s * SC, SC), :]).then_inc(staged, 1)
                hold(pool, staged, 2 * s + 2)
                for c in range(SC):
                    nc.gpsimd.indirect_dma_start(
                        dram["sorted_edges"], bass.IndirectOffsetOnAxis(ap=stage_row[0:EP, k, c:c + 1], axis=0),
                        stage_pay[0:EP, k, c, :], None).then_inc(scattered[k], 16)

            pool.wait_ge(filled, 16)
            pool.wait_ge(chunk_ready, 1)
            stage_and_scatter(0, 0, True)
            stage_and_scatter(0, 1, True)
            with pool.Fori(1, CHUNK // SC // 2) as j:
                for k in range(2):
                    stage_and_scatter(j, k, False)
            pool.wait_ge(var_ready, 1)
            nc.gpsimd.tensor_tensor(rstd[0:BIN, :], mv[0:BIN, :, 1], half[0:BIN, :], ALU.pow).then_inc(rstd_ready, 1)
            for n in range(1, EC // CHUNK):
                pool.wait_ge(chunk_ready, n + 1)
                with pool.Fori(n * CHUNK // SC // 2, (n + 1) * CHUNK // SC // 2) as j:
                    for k in range(2):
                        stage_and_scatter(j, k, False)

        @block.scalar
        def _(act):
            mw1, uw1 = t["L0_gnn_mW1"], t["L0_gnn_uW1"]
            for dst, src in ((w1a, by_chunks(mw1[0:D, :])), (w1b, by_chunks(mw1[D:2 * D, :])),
                             (u1a, by_chunks(uw1[0:D, :])), (w2, by_chunks(t["L0_gnn_mW2"]))):
                act.dma_start(dst[:], src).then_inc(params_in, 16)
            for dst, name in ((b1_all, "L0_gnn_mb1"), (ub1_all, "L0_gnn_ub1"), (ub2_all, "L0_gnn_ub2")):
                act.dma_start(dst[:], one_row(t[name]).broadcast_to([P, D])).then_inc(params_in, 16)
            act.dma_start(wc[:], mw1[2 * D:2 * D + 1, :]).then_inc(params_in, 16)
            act.dma_start(crow[0:1, 0, :], one_row(t["L0_gnn_mb2"])).then_inc(params_in, 16)
            for dst, name in ((gcol, "L0_gnn_ln_g"), (bcol, "L0_gnn_ln_b")):
                for c in range(KC):
                    act.dma_start(dst[:, c:c + 1], t[name][c * P:(c + 1) * P].rearrange("(p o) -> p o", o=1)
                                  ).then_inc(params_in, 16)

            def copies(i, k, first):
                act.wait_ge(h_turned, i + 1)
                if not first:
                    act.wait_ge(node_mul, i - 1)
                nc.scalar.activation(ht[:, k], ps_t[k][:, 0:KC * BIN].rearrange("p (c n) -> p c n", c=KC),
                                     ACT.Copy).then_inc(ht_ready, 1)
                hold(act, node_mul, i + 1)
                nc.scalar.activation(a_hi[0:BIN, ds(i, 1), :], ps_a[0:BIN, 0:D].rearrange("p (o f) -> p o f", o=1),
                                     ACT.Copy).then_inc(a_hi_ready, 1)

            copies(0, 0, True)
            copies(1, 1, True)
            with act.Fori(1, BINS // 2) as j:
                for k in range(2):
                    copies(2 * j + k, k, False)

        @block.tensor
        def _(pe):
            pe.wait_ge(masks_cut, 2)
            pe.wait_ge(counted, BINS)
            pe.matmul(ps_n[:, 0:BINS], before[0:EP, :], counts[:], start=True, stop=True)
            pe.matmul(ps_n[:, BINS:2 * BINS], ones[0:EP, :], counts[:], start=True, stop=True).then_inc(summed, 1)
            pe.wait_ge(params_in, 16 * n_params)
            for c in range(KC):
                mm = pe.matmul(ps_c[0:1, 0:D], bcol[:, c:c + 1], w2[:, c, :], start=(c == 0), stop=(c == KC - 1))
            mm.then_inc(c_mul, 1)

            def products(i, k, first):
                pe.wait_ge(h_ready, i + 1)
                for c in range(KC):
                    tr = pe.transpose(ps_t[k][:, c * BIN:(c + 1) * BIN], h[0:BIN, k, c * P:(c + 1) * P],
                                      ident[0:BIN, 0:BIN])
                tr.then_inc(h_turned, 1)
                pe.wait_ge(ht_ready, i + 1)
                if not first:
                    pe.wait_ge(outs_ready, 3 * i)
                    pe.wait_ge(a_lo_ready, i)
                for ps, w in ((ps_a, w1a), (ps_b, w1b), (ps_u, u1a)):
                    for c in range(KC):
                        mm = pe.matmul(ps[0:BIN, 0:D], ht[:, k, c, :], w[:, c, :], start=(c == 0),
                                       stop=(c == KC - 1))
                mm.then_inc(node_mul, 1)

            products(0, 0, True)
            products(1, 1, False)
            with pe.Fori(1, BINS // 2) as j:
                for k in range(2):
                    products(2 * j + k, k, False)

        @block.vector
        def _(dve):
            nc.vector.memset(node_rows[:, BINS - 1, :], 0.0).then_inc(last_clear, 1)
            nc.vector.memset(slots[:], 0.0).then_inc(prep, 1)
            nc.vector.memset(kept["c3"][:], 0.0)
            nc.vector.memset(kept["ones3"][:], 1.0).then_inc(prep, 1)
            dve.wait_ge(prep, 2)
            nc.vector.memset(slots[:, :, 1:2], -1.0).then_inc(cleared, 1)
            dve.wait_ge(edges_in, 16 * 3)
            nc.vector.tensor_copy(pay[0:EP, :, 0].bitcast(I32), dsti[:]).then_inc(prep, 1)
            nc.vector.tensor_copy(pay[0:EP, :, 2].bitcast(F32R), wgt[:]).then_inc(prep, 1)
            nc.vector.tensor_copy(slot_of[:], srci[:]).then_inc(prep, 1)
            dve.wait_ge(prep, 5)
            nc.vector.tensor_tensor(pay[0:EP, :, 3].bitcast(F32R), wgt[:], pay[0:EP, :, 2],
                                    ALU.subtract).then_inc(prep, 1)
            nc.vector.tensor_scalar(bin_of[:], slot_of[:], 1.0 / BIN, 0.5 / BIN - 0.5, ALU.mult,
                                    ALU.add).then_inc(prep, 1)
            dve.wait_ge(prep, 7)
            nc.vector.tensor_scalar(wgt[:], bin_of[:], ROUND, None, ALU.add).then_inc(prep, 1)
            dve.wait_ge(prep, 8)
            nc.vector.tensor_scalar(bin_of[:], wgt[:], -ROUND, None, ALU.add).then_inc(prep, 1)
            dve.wait_ge(prep, 9)
            nc.vector.scalar_tensor_tensor(out=pay[0:EP, :, 1], in0=bin_of[:], scalar=-float(BIN),
                                           in1=slot_of[:], op0=ALU.mult, op1=ALU.add).then_inc(prep, 1)
            dve.wait_ge(pool_consts, 6)
            nc.vector.memset(wgt[:], 0.0).then_inc(mask_free, 1)
            with dve.Fori(0, BINS) as b:
                dve.wait_ge(mask_free, b + 1)
                nc.vector.tensor_scalar(wgt[:], bin_of[:], kept["iota"][0:EP, ds(b, 1)], 0.0,
                                        ALU.is_equal, ALU.add, accum_out=counts[:, ds(b, 1)]).then_inc(counted, 1)
                dve.wait_ge(counted, b + 1)
                nc.vector.memset(gbin[:, 0:1], 0.0).then_inc(mask_free, 1)
            dve.wait_ge(summed, 1)
            nc.vector.tensor_scalar(gtmp[:], ps_n[0:NQ, BINS:2 * BINS], 1.0 / GROUP,
                                    (GROUP - 1.0) / GROUP - 0.5 + 0.5 / GROUP, ALU.mult, ALU.add
                                    ).then_inc(base_ready, 1)
            dve.wait_ge(base_ready, 1)
            nc.vector.tensor_scalar(gtmp2[:], gtmp[:], ROUND, None, ALU.add).then_inc(base_ready, 1)
            dve.wait_ge(base_ready, 2)
            nc.vector.tensor_scalar(groups[:], gtmp2[:], -ROUND, None, ALU.add).then_inc(base_ready, 1)
            dve.wait_ge(base_ready, 3)
            nc.vector.tensor_tensor_scan(ends[:], groups[:], groups[:], 0.0, ALU.add, ALU.max
                                         ).then_inc(base_ready, 1)
            dve.wait_ge(base_ready, 4)
            nc.vector.tensor_tensor(gtmp[:], ends[:], groups[:], ALU.subtract).then_inc(base_ready, 1)
            dve.wait_ge(base_ready, 5)
            nc.vector.scalar_tensor_tensor(out=run[:], in0=gtmp[:], scalar=float(GROUP),
                                           in1=ps_n[0:EP, 0:BINS], op0=ALU.mult, op1=ALU.add).then_inc(base_ready, 1)
            nc.vector.tensor_tensor(ahead[:], ends[:].rearrange("p (o b) -> p o b", o=1).broadcast_to([NQ, 4, BINS]),
                                    gidx[0:NQ, :].rearrange("p (j o) -> p j o", o=1).broadcast_to([NQ, 4, BINS]),
                                    ALU.is_le).then_inc(base_ready, 1)
            dve.wait_ge(base_ready, 7)
            dve.wait_ge(mask_free, BINS + 1)
            nc.vector.tensor_reduce(gbin[0:NQ, :], ahead[:], AX_X, ALU.add).then_inc(base_ready, 1)
            dve.wait_ge(base_ready, 8)
            nc.vector.tensor_scalar(gbin_i[0:NQ, :], gbin[0:NQ, :], float(BINS - 1), None, ALU.min
                                    ).then_inc(table_ready, 1)

            def rank(n):
                cols = slice(n * CHUNK, (n + 1) * CHUNK)
                if n:
                    dve.wait_ge(chunk_ready, n)
                nc.vector.memset(slot_of[:, cols], 0.0).then_inc(ranked, 1)
                with dve.Fori(0, BINS) as b:
                    step = 5 * b + n * STEPS
                    dve.wait_ge(ranked, step + 1)
                    nc.vector.tensor_scalar(mask[:], bin_of[:, cols], kept["iota"][0:EP, ds(b, 1)], None,
                                            ALU.is_equal).then_inc(ranked, 1)
                    dve.wait_ge(ranked, step + 2)
                    nc.vector.tensor_tensor_scan(ranks[:], mask[:], mask[:], run[:, ds(b, 1)], ALU.add,
                                                 ALU.max).then_inc(ranked, 1)
                    dve.wait_ge(ranked, step + 3)
                    nc.vector.tensor_scalar(run[:, ds(b, 1)], ranks[:, CHUNK - 1:CHUNK], 0.0, None, ALU.add
                                            ).then_inc(ranked, 1)
                    nc.vector.tensor_tensor(mask[:], mask[:], ranks[:], ALU.mult).then_inc(ranked, 1)
                    dve.wait_ge(ranked, step + 5)
                    nc.vector.tensor_tensor(slot_of[:, cols], slot_of[:, cols], mask[:], ALU.add
                                            ).then_inc(ranked, 1)
                at = 5 * BINS + n * STEPS
                dve.wait_ge(ranked, at + 1)
                nc.vector.tensor_scalar(mask[:], slot_of[:, cols], 1.0 / P, -1.0 / P - 0.5 + 0.5 / P, ALU.mult,
                                        ALU.add).then_inc(ranked, 1)
                dve.wait_ge(ranked, at + 2)
                nc.vector.tensor_scalar(ranks[:], mask[:], ROUND, None, ALU.add).then_inc(ranked, 1)
                dve.wait_ge(ranked, at + 3)
                nc.vector.tensor_scalar(mask[:], ranks[:], -ROUND, None, ALU.add).then_inc(ranked, 1)
                dve.wait_ge(ranked, at + 4)
                nc.vector.scalar_tensor_tensor(out=ranks[:], in0=mask[:], scalar=-float(P), in1=slot_of[:, cols],
                                               op0=ALU.mult, op1=ALU.add).then_inc(ranked, 1)
                dve.wait_ge(ranked, at + 5)
                nc.vector.tensor_scalar(ranks[:], ranks[:], float(TILES), -float(TILES), ALU.mult, ALU.add
                                        ).then_inc(ranked, 1)
                dve.wait_ge(ranked, at + 6)
                nc.vector.tensor_tensor(row_of[0:EP, cols], ranks[:], mask[:], ALU.add).then_inc(chunk_ready, 1)

            rank(0)
            dve.wait_ge(x_in, 32)
            with dve.Fori(0, BINS) as i:
                nc.vector.bn_stats(st6[0:BIN, :], node_rows[0:BIN, ds(i, 1), :].rearrange("p o f -> p (o f)")
                                   ).then_inc(stats, 1)
                hold(dve, stats, 3 * i + 1)
                nc.vector.bn_aggr(st2[0:BIN, :], st6[0:BIN, :]).then_inc(stats, 1)
                dve.wait_ge(stats, 3 * i + 2)
                nc.vector.tensor_scalar(mv[0:BIN, ds(i, 1), :], st2[0:BIN, :].rearrange("p (o f) -> p o f", o=1),
                                        0.0, None, ALU.add).then_inc(stats, 1)
                hold(dve, stats, 3 * i + 3)
            nc.vector.tensor_scalar(mv[0:BIN, :, 1], mv[0:BIN, :, 1], LN_EPS, None, ALU.add).then_inc(var_ready, 1)
            dve.wait_ge(params_in, 16 * n_params)
            nc.vector.tensor_copy(wc_hi[:], wc[:]).then_inc(w2_split, 1)
            dve.wait_ge(c_mul, 1)
            for c in range(KC):
                nc.vector.tensor_scalar(w2[:, c, :], w2[:, c, :], gcol[:, c:c + 1], None, ALU.mult
                                        ).then_inc(w2_split, 1)
            nc.vector.tensor_tensor(crow[0:1, 0, :], crow[0:1, 0, :], ps_c[0:1, 0:D], ALU.add).then_inc(w2_split, 1)
            dve.wait_ge(w2_split, 4)
            nc.vector.tensor_tensor(wc_lo[:], wc[:], wc_hi[:].bitcast(F32), ALU.subtract).then_inc(wc_ready, 1)
            nc.vector.tensor_copy(kept["w2_hi"][:], w2[:]).then_inc(w2_split, 1)
            nc.vector.tensor_copy(cpart[0:1, 0, :], crow[0:1, 0, :]).then_inc(w2_split, 1)
            dve.wait_ge(w2_split, 6)
            nc.vector.tensor_tensor(kept["w2_lo"][:], w2[:], kept["w2_hi"][:].bitcast(F32), ALU.subtract
                                    ).then_inc(w2_split, 1)
            nc.vector.tensor_tensor(crow[0:1, 1, :], crow[0:1, 0, :], cpart[0:1, 0, :], ALU.subtract
                                    ).then_inc(w2_split, 1)
            dve.wait_ge(w2_split, 8)
            nc.vector.tensor_copy(cpart[0:1, 1, :], crow[0:1, 1, :]).then_inc(w2_split, 1)
            dve.wait_ge(w2_split, 9)
            nc.vector.tensor_tensor(crow[0:1, 2, :], crow[0:1, 1, :], cpart[0:1, 1, :], ALU.subtract
                                    ).then_inc(w2_split, 1)
            dve.wait_ge(w2_split, 10)
            nc.vector.tensor_copy(cpart[0:1, 2, :], crow[0:1, 2, :]).then_inc(c_ready, 1)
            for n in range(1, EC // CHUNK):
                rank(n)

            def node(j, k, first):
                i = 2 * j + k
                row = node_rows[0:BIN, ds(i, 1), :].rearrange("p o f -> p (o f)")
                if not first:
                    dve.wait_ge(h_turned, i - 1)
                    dve.wait_ge(outs_stored[k], 16 * 3 * j)
                nc.vector.tensor_scalar(h[0:BIN, k, :], row, mv[0:BIN, ds(i, 1), 0:1].rearrange("p o f -> p (o f)"),
                                        rstd[0:BIN, ds(i, 1)], ALU.subtract, ALU.mult).then_inc(h_ready, 1)
                dve.wait_ge(h_ready, i + 1)
                nc.vector.tensor_tensor(xh_out[0:BIN, k, :], h[0:BIN, k, :], row, ALU.add).then_inc(xh_part, 1)
                dve.wait_ge(xh_part, i + 1)
                nc.vector.tensor_tensor(xh_out[0:BIN, k, :], xh_out[0:BIN, k, :], ub2_all[0:BIN, :], ALU.add
                                        ).then_inc(outs_ready, 1)
                dve.wait_ge(node_mul, i + 1)
                nc.vector.tensor_tensor(b_out[0:BIN, k, :], ps_b[0:BIN, 0:D], b1_all[0:BIN, :], ALU.add
                                        ).then_inc(outs_ready, 1)
                nc.vector.tensor_tensor(u_out[0:BIN, k, :], ps_u[0:BIN, 0:D], ub1_all[0:BIN, :], ALU.add
                                        ).then_inc(outs_ready, 1)
                dve.wait_ge(a_hi_ready, i + 1)
                nc.vector.tensor_tensor(a_lo[0:BIN, ds(i, 1), :],
                                        ps_a[0:BIN, 0:D].rearrange("p (o f) -> p o f", o=1),
                                        a_hi[0:BIN, ds(i, 1), :].bitcast(F32), ALU.subtract).then_inc(a_lo_ready, 1)

            dve.wait_ge(rstd_ready, 1)
            dve.wait_ge(chunk_ready, EC // CHUNK)
            dve.wait_ge(wc_out, 16 * 4)
            dve.wait_ge(c_out, 16 * 3)
            node(0, 0, True)
            node(0, 1, True)
            with dve.Fori(1, BINS // 2) as j:
                for k in range(2):
                    node(j, k, False)

def messages(nc, dram, node_rows, ident, kept):
    a_hi, a_lo, slots, iota = kept["a_hi"], kept["a_lo"], kept["slots"], kept["iota"]
    w2_hi, w2_lo, c3, ones3 = kept["w2_hi"], kept["w2_lo"], kept["c3"], kept["ones3"]
    with ExitStack() as ctx:
        def sb(name, shape, dt=F32):
            return ctx.enter_context(nc.sbuf_tensor(name, shape, dt))

        def sem(name):
            return ctx.enter_context(nc.semaphore(name))

        group_bin = sb("group_bin", [1, 4 * (P - 3)], I32)
        dst_row = sb("dst_row", [P, RING, 2], I32)
        onehot = sb("onehot", [P, RING, 2, P])
        onehot_t = sb("onehot_t", [P, 2, 2, P], F32R)
        rows = [sb(f"rows{r}", [P, 2, D]) for r in range(RING)]
        st6 = sb("st6_m", [P, 2, 6])
        mv = sb("mv_m", [P, RING, 2, 2])
        rstd = sb("rstd_m", [P, RING, 2])
        half = sb("half_m", [P, 2])
        shift = sb("shift", [P, RING, 2])
        t_hi = sb("t_hi", [P, 2, 2, KC, P], F32R)
        t_lo = sb("t_lo", [P, 2, 2, KC, P], F32R)
        msg = sb("msg", [P, 2, 2, D])

        def psum(name, n=2, width=512):
            return [ctx.enter_context(nc.psum_tensor(f"{name}{k}", [P, width], F32)) for k in range(n)]

        ps_oh = ctx.enter_context(nc.psum_tensor("ps_oh", [P, 512], F32))
        ps_pre = psum("ps_pre")
        ps_rt = psum("ps_rt")
        ps_z = psum("ps_z")
        ps_agg = ctx.enter_context(nc.psum_tensor("ps_agg", [P, 512], F32))

        table_in = sem("table_in")
        start = sem("start")
        dst_ready = sem("dst_ready")
        b_landed = [sem(f"b_landed{r}") for r in range(RING)]
        onehot_ready = sem("onehot_ready")
        onehot_turned = sem("onehot_turned")
        onehot_t_ready = sem("onehot_t_ready")
        a_gathered = sem("a_gathered")
        pre_ready = sem("pre_ready")
        silu_ready = sem("silu_ready")
        tile_stats = sem("tile_stats")
        stats_ready = sem("stats_ready")
        eps_added = sem("eps_added")
        shift_ready = sem("shift_ready")
        rstd_ready = sem("rstd_ready")
        norm_ready = sem("norm_ready")
        rows_turned = sem("rows_turned")
        hi_ready = sem("hi_ready")
        lo_ready = sem("lo_ready")
        z_ready = sem("z_ready")
        msg_ready = sem("msg_ready")
        part_ready = sem("part_ready")
        added = sem("added")
        block = ctx.enter_context(nc.Block())

        def pipeline(engine, step, last):
            for n in range(2 * RING):
                step(n // RING, n % RING, lambda d: n - d >= 0)
            with engine.Fori(2, GROUPS // RING) as j:
                for r in range(RING):
                    step(j, r, lambda d: True)
            for n in range(GROUPS, GROUPS + last):
                step(n // RING, n % RING, lambda d: n - d < GROUPS)

        @block.sync
        def _(sp):
            sp.dma_start(group_bin[:], one_row(dram["group_bins"])).then_inc(table_in, 16)
            sp.wait_ge(table_in, 16)

        @block.gpsimd
        def _(pool):
            nc.gpsimd.memset(half[:], -0.5).then_inc(start, 1)
            pool.wait_ge(start, 1)

            def step(j, r, live):
                n = RING * j + r
                if live(0):
                    if live(RING):
                        hold(pool, rows_turned, n - RING + 1)
                    nc.gpsimd.tensor_copy(dst_row[:, r, :], slots[:, ds(2 * n, 2), 0].bitcast(I32)
                                          ).then_inc(dst_ready, 1)
                    hold(pool, dst_ready, n + 1)
                    for i in range(2):
                        nc.gpsimd.indirect_dma_start(
                            rows[r][:, i, :], None, dram["b_rows"],
                            bass.IndirectOffsetOnAxis(ap=dst_row[:, r, i:i + 1], axis=0)).then_inc(b_landed[r], 16)
                if live(2):
                    g, q = n - 2, (r - 2) % RING
                    hold(pool, stats_ready, g + 1)
                    nc.gpsimd.tensor_scalar(mv[:, q, :, 1], mv[:, q, :, 1], LN_EPS, None, ALU.add
                                            ).then_inc(eps_added, 1)
                    pool.wait_ge(eps_added, g + 1)
                    nc.gpsimd.tensor_tensor(rstd[:, q, :], mv[:, q, :, 1], half[:], ALU.pow).then_inc(rstd_ready, 1)

            pipeline(pool, step, 2)

        @block.scalar
        def _(act):
            def step(j, r, live):
                n = RING * j + r
                if live(3):
                    g, q = n - 3, (r - 3) % RING
                    act.wait_ge(shift_ready, g + 1)
                    for i in range(2):
                        nm = nc.scalar.activation(rows[q][:, i, :], rows[q][:, i, :], ACT.Identity,
                                                  bias=shift[:, q, i:i + 1], scale=rstd[:, q, i:i + 1])
                    nm.then_inc(norm_ready, 1)
                if live(5):
                    g, k = n - 5, (r - 5) % 2
                    act.wait_ge(z_ready, g + 1)
                    if live(5 + 2):
                        act.wait_ge(part_ready, g - 1)
                    nc.scalar.activation(msg[:, k], ps_z[k][:].rearrange("p (i n) -> p i n", i=2), ACT.Silu
                                         ).then_inc(msg_ready, 1)
                if live(0):
                    k = r % 2
                    act.wait_ge(onehot_turned, n + 1)
                    if live(2):
                        act.wait_ge(a_gathered, n - 1)
                    nc.scalar.activation(onehot_t[:, k], ps_oh[:, 0:2 * P].rearrange("p (i n) -> p i n", i=2),
                                         ACT.Copy).then_inc(onehot_t_ready, 1)
                if live(3):
                    g, k = n - 3, (r - 3) % 2
                    act.wait_ge(rows_turned, g + 1)
                    if live(3 + 2):
                        act.wait_ge(z_ready, g - 1)
                    nc.scalar.activation(t_hi[:, k].rearrange("p i c e -> p (i c e)"), ps_rt[k][:], ACT.Copy
                                         ).then_inc(hi_ready, 1)
                if live(1):
                    g, x = n - 1, rows[(r - 1) % RING]
                    act.wait_ge(pre_ready, g + 1)
                    nc.scalar.activation(x[:], x[:], ACT.Silu).then_inc(silu_ready, 1)

            pipeline(act, step, 5)

        @block.tensor
        def _(pe):
            pe.wait_ge(table_in, 16)

            def step(j, r, live):
                n = RING * j + r
                if live(1):
                    b = pe.value_load(group_bin[0:1, ds(n - 1, 1)], min_val=0, max_val=BINS - 1)
                if live(1):
                    g, k = n - 1, (r - 1) % 2
                    pe.wait_ge(onehot_t_ready, g + 1)
                    if live(1 + 2):
                        pe.wait_ge(pre_ready, g - 1)
                    for i in range(2):
                        pre = ps_pre[k][:, i * D:(i + 1) * D]
                        pe.matmul(pre, onehot_t[:, k, i, :], a_hi[:, ds(b, 1), :].rearrange("p o f -> p (o f)"),
                                  start=True, stop=False)
                        mm = pe.matmul(pre, onehot_t[:, k, i, :],
                                       a_lo[:, ds(b, 1), :].rearrange("p o f -> p (o f)"), start=False, stop=True)
                    mm.then_inc(a_gathered, 1)
                if live(0):
                    pe.wait_ge(onehot_ready, n + 1)
                    if live(1):
                        pe.wait_ge(onehot_t_ready, n)
                    for i in range(2):
                        tr = pe.transpose(ps_oh[:, i * P:(i + 1) * P], onehot[:, r, i, :], ident[:])
                    tr.then_inc(onehot_turned, 1)
                if live(3):
                    g, k, q = n - 3, (r - 3) % 2, (r - 3) % RING
                    pe.wait_ge(norm_ready, g + 1)
                    if live(3 + 2):
                        pe.wait_ge(lo_ready, g - 1)
                    for i in range(2):
                        for c in range(KC):
                            tr = pe.transpose(ps_rt[k][:, (i * KC + c) * P:(i * KC + c + 1) * P],
                                              rows[q][:, i, c * P:(c + 1) * P], ident[:])
                    tr.then_inc(rows_turned, 1)
                if live(5):
                    g, k, q = n - 5, (r - 5) % 2, (r - 5) % RING
                    pe.wait_ge(msg_ready, g + 1)
                    if live(5 + 1):
                        pe.wait_ge(added, g + 1)
                    for i in range(2):
                        mm = pe.matmul(ps_agg[0:BIN, 0:D], onehot[:, q, i, 0:BIN], msg[:, k, i, :],
                                       start=(i == 0), stop=(i == 1))
                    mm.then_inc(part_ready, 1)
                if live(4):
                    g, k = n - 4, (r - 4) % 2
                    pe.wait_ge(lo_ready, g + 1)
                    if live(4 + 2):
                        pe.wait_ge(msg_ready, g - 1)
                    for i in range(2):
                        z = ps_z[k][:, i * D:(i + 1) * D]
                        pe.matmul(z, ones3[:], c3[:], start=True, stop=False)
                        for c in range(KC):
                            pe.matmul(z, t_hi[:, k, i, c, :], w2_hi[:, c, :], start=False, stop=False)
                            pe.matmul(z, t_hi[:, k, i, c, :], w2_lo[:, c, :], start=False, stop=False)
                            mm = pe.matmul(z, t_lo[:, k, i, c, :], w2_hi[:, c, :], start=False, stop=(c == KC - 1))
                    mm.then_inc(z_ready, 1)

            pipeline(pe, step, 5)

        @block.vector
        def _(dve):
            nc.vector.memset(node_rows[:], 0.0).then_inc(added, 1)
            dve.wait_ge(table_in, 16)

            def step(j, r, live):
                n = RING * j + r
                if live(6):
                    b = dve.value_load(group_bin[0:1, ds(n - 6, 1)], min_val=0, max_val=BINS - 1)
                if live(3):
                    g, q = n - 3, (r - 3) % RING
                    dve.wait_ge(rstd_ready, g + 1)
                    nc.vector.scalar_tensor_tensor(out=shift[:, q, :], in0=mv[:, q, :, 0], scalar=-1.0,
                                                   in1=rstd[:, q, :], op0=ALU.mult, op1=ALU.mult
                                                   ).then_inc(shift_ready, 1)
                if live(0):
                    if live(RING):
                        dve.wait_ge(part_ready, n - RING + 1)
                    tiles = slots[:, ds(2 * n, 2), :]
                    nc.vector.tensor_tensor(
                        onehot[:, r, :, 0:BIN],
                        iota[:, 0:BIN].rearrange("p (o n) -> p o n", o=1).broadcast_to([P, 2, BIN]),
                        tiles[:, :, 1:2].broadcast_to([P, 2, BIN]), ALU.is_equal)
                    nc.vector.tensor_copy(onehot[:, r, :, BIN:P], tiles[:, :, 2:4]).then_inc(onehot_ready, 1)
                if live(6):
                    g = n - 6
                    dve.wait_ge(part_ready, g + 1)
                    dve.wait_ge(added, g + 1)
                    agg = node_rows[0:BIN, ds(b, 1), :]
                    nc.vector.tensor_tensor(agg, agg, ps_agg[0:BIN, 0:D].rearrange("p (o f) -> p o f", o=1),
                                            ALU.add).then_inc(added, 1)
                if live(2):
                    g, q = n - 2, (r - 2) % RING
                    dve.wait_ge(silu_ready, g + 1)
                    for i in range(2):
                        nc.vector.bn_stats(st6[:, i, :], rows[q][:, i, :]).then_inc(tile_stats, 1)
                if live(4):
                    g, k = n - 4, (r - 4) % 2
                    dve.wait_ge(hi_ready, g + 1)
                    if live(2):
                        dve.wait_ge(tile_stats, 2 * (n - 2) + 2)
                    nc.vector.tensor_tensor(t_lo[:, k].rearrange("p i c e -> p (i c e)"), ps_rt[k][:],
                                            t_hi[:, k].rearrange("p i c e -> p (i c e)").bitcast(F32),
                                            ALU.subtract).then_inc(lo_ready, 1)
                if live(2):
                    g, q = n - 2, (r - 2) % RING
                    if not live(4):
                        dve.wait_ge(tile_stats, 2 * g + 2)
                    for i in range(2):
                        ag = nc.vector.bn_aggr(mv[:, q, i, :], st6[:, i, :])
                    ag.then_inc(stats_ready, 1)
                if live(1):
                    g, q = n - 1, (r - 1) % RING
                    dve.wait_ge(a_gathered, g + 1)
                    dve.wait_ge(b_landed[q], 32 * (j + (r >= 1)))
                    x = rows[q][:].rearrange("p i f -> p (i f)")
                    nc.vector.tensor_tensor(x, x, ps_pre[q % 2][:], ALU.add).then_inc(pre_ready, 1)

            pipeline(dve, step, 6)

def update(nc, t, dram, node_rows, ident, tokens_t, logits):
    with ExitStack() as ctx:
        def sb(name, shape, dt=F32):
            return ctx.enter_context(nc.sbuf_tensor(name, shape, dt))

        def sem(name):
            return ctx.enter_context(nc.semaphore(name))

        def psum(name):
            return ctx.enter_context(nc.psum_tensor(name, [P, 512], F32))

        u1b = sb("u1b", [P, KC, D])
        u2 = sb("u2", [P, KC, D])
        rw = sb("rw", [P, KC, EXPERTS])
        u_row = sb("u_row", [P, 2, D])
        xh_row = sb("xh_row", [P, 2, D])
        agg = sb("agg", [P, 2, D])
        agg_t = sb("agg_t", [P, 2, KC, BIN])
        act1 = sb("act1", [P, 2, D])
        act1_t = sb("act1_t", [P, 2, KC, BIN])
        x1 = sb("x1", [P, 2, D])
        h2 = sb("h2", [P, 2, D])
        h2_t = sb("h2_t", [P, 2, KC, BIN])
        st6 = sb("st6_u", [P, 6])
        mv = sb("mv_u", [P, 2, 2])
        rstd = sb("rstd_u", [P, 2, 1])
        half = sb("half_u", [P, 1])
        ps_at, ps_v, ps_st, ps_y, ps_ht, ps_l = (psum(f"ps_{x}") for x in ("at", "v", "st", "y", "ht", "l"))

        weights_in = sem("weights_in")
        u_in = [sem("u_in0"), sem("u_in1")]
        xh_in = [sem("xh_in0"), sem("xh_in1")]
        agg_ready = sem("agg_ready")
        agg_turned = sem("agg_turned")
        agg_t_ready = sem("agg_t_ready")
        v_ready = sem("v_ready")
        v_added = sem("v_added")
        silu_ready = sem("silu_ready")
        act_turned = sem("act_turned")
        act_t_ready = sem("act_t_ready")
        y_ready = sem("y_ready")
        x1_ready = sem("x1_ready")
        stats_part = sem("stats_part")
        stats_ready = sem("stats_ready")
        half_ready = sem("half_ready")
        rstd_ready = sem("rstd_ready")
        h2_ready = sem("h2_ready")
        sum_ready = sem("sum_ready")
        h2_turned = sem("h2_turned")
        h2_t_ready = sem("h2_t_ready")
        tokens_ready = sem("tokens_ready")
        l_ready = sem("l_ready")
        l_copied = sem("l_copied")
        block = ctx.enter_context(nc.Block())

        def run(engine, step, delays=2):
            for n in range(6):
                step(n // 2, n % 2, lambda d: n - d >= 0)
            with engine.Fori(3, BINS // 2) as j:
                for k in range(2):
                    step(j, k, lambda d: True)
            for n in range(BINS, BINS + delays):
                step(n // 2, n % 2, lambda d: n - d < BINS)

        @block.sync
        def _(sp):
            for dst, src in ((u1b, by_chunks(t["L0_gnn_uW1"][D:2 * D, :])), (u2, by_chunks(t["L0_gnn_uW2"]))):
                sp.dma_start(dst[:], src).then_inc(weights_in, 16)
            for c in range(KC):
                sp.dma_start(rw[:, c, :], t["L0_ffn_router_w"][:, c * P:(c + 1) * P].rearrange("e p -> p e")
                             ).then_inc(weights_in, 16)

            def step(j, k, live):
                n = 2 * j + k
                if live(2):
                    sp.wait_ge(v_added, n - 1)
                sp.dma_start(u_row[0:BIN, k, :], dram["u_rows"][ds(n * BIN, BIN), :]).then_inc(u_in[k], 16)
                if live(2):
                    sp.wait_ge(x1_ready, n - 1)
                sp.dma_start(xh_row[0:BIN, k, :], dram["xh_rows"][ds(n * BIN, BIN), :]).then_inc(xh_in[k], 16)

            run(sp, step, 0)

        @block.gpsimd
        def _(pool):
            nc.gpsimd.memset(half[:], -0.5).then_inc(half_ready, 1)
            pool.wait_ge(half_ready, 1)

            def step(j, k, live):
                n = 2 * j + k
                if live(2):
                    hold(pool, h2_t_ready, n - 1)
                    nc.gpsimd.tensor_copy(tokens_t[:, :, ds((n - 2) * BIN, BIN)], h2_t[:, k]).then_inc(tokens_ready, 1)
                if live(1):
                    pool.wait_ge(stats_ready, n)
                    nc.gpsimd.tensor_tensor(rstd[0:BIN, 1 - k, :], mv[0:BIN, 1 - k, 1:2], half[0:BIN, :], ALU.pow
                                            ).then_inc(rstd_ready, 1)

            run(pool, step)

        @block.scalar
        def _(act):
            def step(j, k, live):
                n = 2 * j + k
                if live(2):
                    act.wait_ge(h2_turned, n - 1)
                    if live(4):
                        act.wait_ge(tokens_ready, n - 3)
                        act.wait_ge(l_ready, n - 3)
                    nc.scalar.activation(h2_t[:, k], ps_ht[:, 0:KC * BIN].rearrange("p (c n) -> p c n", c=KC),
                                         ACT.Copy).then_inc(h2_t_ready, 1)
                if live(0):
                    if live(2):
                        hold(act, agg_turned, n - 1)
                    nc.scalar.activation(agg[0:BIN, k, :], node_rows[0:BIN, ds(n, 1), :].rearrange("p o f -> p (o f)"),
                                         ACT.Copy).then_inc(agg_ready, 1)
                if live(1):
                    act.wait_ge(act_turned, n)
                    if live(3):
                        act.wait_ge(y_ready, n - 2)
                    nc.scalar.activation(act1_t[:, 1 - k], ps_st[:, 0:KC * BIN].rearrange("p (c n) -> p c n", c=KC),
                                         ACT.Copy).then_inc(act_t_ready, 1)
                if live(0):
                    act.wait_ge(v_added, n + 1)
                    nc.scalar.activation(act1[0:BIN, k, :], act1[0:BIN, k, :], ACT.Silu).then_inc(silu_ready, 1)

            run(act, step)

        @block.tensor
        def _(pe):
            pe.wait_ge(weights_in, 16 * 4)

            def turn(ps, rows):
                for c in range(KC):
                    tr = pe.transpose(ps[:, c * BIN:(c + 1) * BIN], rows[:, c * P:(c + 1) * P], ident[0:BIN, 0:BIN])
                return tr

            def product(ps, rows_t, w):
                for c in range(KC):
                    mm = pe.matmul(ps, rows_t[:, c, :], w[:, c, :], start=(c == 0), stop=(c == KC - 1))
                return mm

            def step(j, k, live):
                n = 2 * j + k
                if live(2):
                    pe.wait_ge(h2_ready, n - 1)
                    if live(3):
                        pe.wait_ge(h2_t_ready, n - 2)
                    turn(ps_ht, h2[0:BIN, k, :]).then_inc(h2_turned, 1)
                if live(1):
                    pe.wait_ge(silu_ready, n)
                    if live(2):
                        pe.wait_ge(act_t_ready, n - 1)
                    turn(ps_st, act1[0:BIN, 1 - k, :]).then_inc(act_turned, 1)
                if live(0):
                    pe.wait_ge(agg_ready, n + 1)
                    if live(1):
                        pe.wait_ge(agg_t_ready, n)
                    turn(ps_at, agg[0:BIN, k, :]).then_inc(agg_turned, 1)
                if live(1):
                    pe.wait_ge(act_t_ready, n)
                    if live(2):
                        pe.wait_ge(x1_ready, n - 1)
                    product(ps_y[0:BIN, 0:D], act1_t[:, 1 - k], u2).then_inc(y_ready, 1)
                if live(0):
                    pe.wait_ge(agg_t_ready, n + 1)
                    if live(1):
                        pe.wait_ge(v_added, n)
                    product(ps_v[0:BIN, 0:D], agg_t[:, k], u1b).then_inc(v_ready, 1)
                if live(2):
                    pe.wait_ge(h2_t_ready, n - 1)
                    if live(3):
                        pe.wait_ge(l_copied, n - 2)
                    product(ps_l[0:BIN, 0:EXPERTS], h2_t[:, k], rw).then_inc(l_ready, 1)

            run(pe, step)

        @block.vector
        def _(dve):
            def step(j, k, live):
                n = 2 * j + k
                if live(2):
                    dve.wait_ge(rstd_ready, n - 1)
                    if live(4):
                        dve.wait_ge(h2_turned, n - 3)
                    nc.vector.tensor_scalar(h2[0:BIN, k, :], x1[0:BIN, k, :], mv[0:BIN, k, 0:1], rstd[0:BIN, k, :],
                                            ALU.subtract, ALU.mult).then_inc(h2_ready, 1)
                if live(0):
                    dve.wait_ge(agg_turned, n + 1)
                    if live(2):
                        dve.wait_ge(v_ready, n - 1)
                    nc.vector.tensor_copy(agg_t[:, k], ps_at[:, 0:KC * BIN].rearrange("p (c n) -> p c n", c=KC)
                                          ).then_inc(agg_t_ready, 1)
                if live(2):
                    dve.wait_ge(h2_ready, n - 1)
                    nc.vector.tensor_tensor(node_rows[0:BIN, ds(n - 2, 1), :],
                                            h2[0:BIN, k, :].rearrange("p (o f) -> p o f", o=1),
                                            x1[0:BIN, k, :].rearrange("p (o f) -> p o f", o=1), ALU.add
                                            ).then_inc(sum_ready, 1)
                if live(1):
                    q = 1 - k
                    dve.wait_ge(y_ready, n)
                    dve.wait_ge(xh_in[q], 16 * (j + 1 if k else j))
                    nc.vector.tensor_tensor(x1[0:BIN, q, :], ps_y[0:BIN, 0:D], xh_row[0:BIN, q, :], ALU.add
                                            ).then_inc(x1_ready, 1)
                    dve.wait_ge(x1_ready, n)
                    nc.vector.bn_stats(st6[0:BIN, :], x1[0:BIN, q, :]).then_inc(stats_part, 1)
                    hold(dve, stats_part, 2 * (n - 1) + 1)
                    nc.vector.bn_aggr(mv[0:BIN, q, :], st6[0:BIN, :]).then_inc(stats_part, 1)
                    dve.wait_ge(stats_part, 2 * (n - 1) + 2)
                    nc.vector.tensor_scalar(mv[0:BIN, q, 1:2], mv[0:BIN, q, 1:2], LN_EPS, None, ALU.add
                                            ).then_inc(stats_ready, 1)
                if live(0):
                    dve.wait_ge(v_ready, n + 1)
                    if live(2):
                        dve.wait_ge(act_turned, n - 1)
                    dve.wait_ge(u_in[k], 16 * (j + 1))
                    nc.vector.tensor_tensor(act1[0:BIN, k, :], ps_v[0:BIN, 0:D], u_row[0:BIN, k, :], ALU.add
                                            ).then_inc(v_added, 1)
                if live(2):
                    hold(dve, l_ready, n - 1)
                    nc.vector.tensor_copy(logits[0:BIN, ds(n - 2, 1), :],
                                          ps_l[0:BIN, 0:EXPERTS].rearrange("p (o e) -> p o e", o=1)
                                          ).then_inc(l_copied, 1)

            run(dve, step)


def route(nc, combine):
    with ExitStack() as ctx:
        def sb(name, shape):
            return ctx.enter_context(nc.sbuf_tensor(name, shape, F32))

        prob = sb("prob", [P, BINS, EXPERTS])
        index = sb("index", [P, BINS, EXPERTS])
        work = sb("work_r", [P, BINS, EXPERTS])
        hot = [sb("hot0", [P, BINS, EXPERTS]), sb("hot1", [P, BINS, EXPERTS])]
        low = sb("low", [P, BINS])
        best = [sb("best0", [P, BINS]), sb("best1", [P, BINS])]
        first = sb("first", [P, BINS])
        total = sb("total", [P, BINS])
        index_ready = ctx.enter_context(nc.semaphore("index_ready"))
        shifted = ctx.enter_context(nc.semaphore("shifted"))
        exp_ready = ctx.enter_context(nc.semaphore("exp_ready"))
        done = ctx.enter_context(nc.semaphore("route_step"))
        block = ctx.enter_context(nc.Block())
        full = [BIN, BINS, EXPERTS]

        def wide(a):
            return a[0:BIN, :].rearrange("p (b o) -> p b o", o=1).broadcast_to(full)

        @block.gpsimd
        def _(pool):
            nc.gpsimd.iota(index[:], [[0, BINS], [1, EXPERTS]], base=0, channel_multiplier=0,
                           allow_small_or_imprecise_dtypes=True).then_inc(index_ready, 1)

        @block.scalar
        def _(act):
            act.wait_ge(shifted, 1)
            nc.scalar.activation(prob[0:BIN], prob[0:BIN], ACT.Exp).then_inc(exp_ready, 1)

        @block.vector
        def _(dve):
            steps = [0]

            def then(ins):
                steps[0] += 1
                ins.then_inc(done, 1)
                dve.wait_ge(done, steps[0])

            c, p, w, idx = combine[0:BIN], prob[0:BIN], work[0:BIN], index[0:BIN]
            then(nc.vector.tensor_reduce(low[0:BIN, :], c, AX_X, ALU.max))
            nc.vector.tensor_tensor(p, c, wide(low), ALU.subtract).then_inc(shifted, 1)
            dve.wait_ge(exp_ready, 1)
            then(nc.vector.tensor_reduce(low[0:BIN, :], p, AX_X, ALU.add))
            then(nc.vector.reciprocal(total[0:BIN, :], low[0:BIN, :]))
            then(nc.vector.tensor_tensor(p, p, wide(total), ALU.mult))
            dve.wait_ge(index_ready, 1)
            for k in range(2):
                then(nc.vector.tensor_reduce(best[k][0:BIN, :], p, AX_X, ALU.max))
                then(nc.vector.tensor_tensor(w, p, wide(best[k]), ALU.is_lt))
                then(nc.vector.scalar_tensor_tensor(out=w, in0=w, scalar=float(EXPERTS), in1=idx, op0=ALU.mult,
                                                    op1=ALU.add))
                then(nc.vector.tensor_reduce(first[0:BIN, :], w, AX_X, ALU.min))
                then(nc.vector.tensor_tensor(hot[k][0:BIN], idx, wide(first), ALU.is_equal))
                if k == 0:
                    then(nc.vector.scalar_tensor_tensor(out=p, in0=hot[0][0:BIN], scalar=-2.0, in1=p, op0=ALU.mult,
                                                        op1=ALU.add))
                then(nc.vector.tensor_tensor(hot[k][0:BIN], hot[k][0:BIN], wide(best[k]), ALU.mult))
            then(nc.vector.tensor_tensor(total[0:BIN, :], best[0][0:BIN, :], best[1][0:BIN, :], ALU.add))
            then(nc.vector.tensor_scalar(total[0:BIN, :], total[0:BIN, :], 1e-12, None, ALU.max))
            then(nc.vector.reciprocal(low[0:BIN, :], total[0:BIN, :]))
            then(nc.vector.tensor_tensor(w, hot[0][0:BIN], hot[1][0:BIN], ALU.add))
            then(nc.vector.tensor_tensor(c, w, wide(low), ALU.mult))


def experts(nc, t, node_rows, tokens_t, combine, out):
    PAIR = 2 * BIN
    with ExitStack() as ctx:
        def sb(name, shape, dt=F32):
            return ctx.enter_context(nc.sbuf_tensor(name, shape, dt))

        def sem(name):
            return ctx.enter_context(nc.semaphore(name))

        raw = sb("raw", [P, EXPERTS, KC, D])
        w_hi = [sb(f"w{n}_hi_e", [P, EXPERTS, KC, D], F32R) for n in (1, 2)]
        w_lo = [sb(f"w{n}_lo_e", [P, EXPERTS, KC, D], F32R) for n in (1, 2)]
        b1 = sb("b1", [P, KC, EXPERTS])
        b2 = sb("b2", [EXPERTS, 2, D])
        b2_part = sb("b2_part", [EXPERTS, 3, D], BF16)
        b2x = sb("b2x", [P, EXPERTS, D], BF16)
        ones_e = sb("ones_e", [P, P], BF16)
        tk_hi = sb("tk_hi", [P, KC, PAIR], F32R)
        tk_lo = sb("tk_lo", [P, KC, PAIR], F32R)
        g = sb("g", [P, 2, KC, PAIR])
        g_hi = sb("g_hi", [P, 2, KC, PAIR], F32R)
        g_lo = sb("g_lo", [P, 2, KC, PAIR], F32R)
        ps_h = [ctx.enter_context(nc.psum_tensor(f"ps_h{k}", [P, 512], F32)) for k in range(2)]
        ps_y = [ctx.enter_context(nc.psum_tensor(f"ps_ye{k}", [P, 512], F32)) for k in range(2)]
        b2_dram = nc.dram_tensor("b2_dram", (3, EXPERTS, D), BF16).ap()

        w_in = [sem("w1_in"), sem("w2_in")]
        small_in = sem("small_in")
        w_split = sem("w_split")
        w_ready = sem("w_ready")
        b2_step = sem("b2_step")
        b2_ready = sem("b2_ready")
        b2_out = sem("b2_out")
        b2_in = sem("b2_in")
        tk_split = sem("tk_split")
        tk_ready = sem("tk_ready")
        h_ready = sem("h_ready_e")
        g_ready = sem("g_ready")
        g_hi_ready = sem("g_hi_ready")
        g_lo_ready = sem("g_lo_ready")
        y_ready = sem("y_ready_e")
        added = sem("added_e")
        stored = sem("stored")
        block = ctx.enter_context(nc.Block())
        CHUNKS = BINS // 2
        E = EXPERTS

        def loop(engine, chunk):
            chunk(0, True)
            with engine.Fori(1, CHUNKS) as c:
                chunk(c, False)

        @block.sync
        def _(sp):
            sp.dma_start(raw[:], t["L0_ffn_w1"].rearrange("e (c p) n -> p e c n", p=P)).then_inc(w_in[0], 16)
            for c in range(KC):
                sp.dma_start(b1[:, c, :], t["L0_ffn_b1"][:, c * P:(c + 1) * P].rearrange("e p -> p e")
                             ).then_inc(small_in, 16)
            sp.dma_start(b2[:, 0, :], t["L0_ffn_b2"]).then_inc(small_in, 16)
            sp.wait_ge(w_ready, 1)
            sp.dma_start(raw[:], t["L0_ffn_w2"].rearrange("e (c p) n -> p e c n", p=P)).then_inc(w_in[1], 16)
            sp.wait_ge(b2_ready, 1)
            sp.dma_start(b2_dram.rearrange("n e f -> e n f"), b2_part[:]).then_inc(b2_out, 16)
            sp.wait_ge(b2_out, 16)
            sp.dma_start(b2x[0:3, :, :], b2_dram).then_inc(b2_in, 16)
            with sp.Fori(0, CHUNKS - 1) as c:
                sp.wait_ge(added, 2 * E * (c + 1))
                for i in range(2):
                    sp.dma_start(out[ds((2 * c + i) * BIN, BIN), :],
                                 node_rows[0:BIN, ds(2 * c + i, 1), :].rearrange("p o f -> p (o f)")
                                 ).then_inc(stored, 16)
            sp.wait_ge(added, 2 * E * CHUNKS)
            sp.dma_start(out[(BINS - 2) * BIN:(BINS - 1) * BIN, :], node_rows[0:BIN, BINS - 2, :]).then_inc(stored, 16)
            sp.dma_start(out[(BINS - 1) * BIN:NODES, :], node_rows[0:LAST, BINS - 1, :]).then_inc(stored, 16)
            sp.wait_ge(stored, 16 * BINS)

        @block.scalar
        def _(act):
            for n in range(2):
                act.wait_ge(w_in[n], 16)
                nc.scalar.activation(w_hi[n][:], raw[:], ACT.Copy).then_inc(w_split, 1)
            act.wait_ge(small_in, 16 * 3)

            def chunk(c, first):
                if not first:
                    hold(act, h_ready, E * c)
                nc.scalar.activation(tk_hi[:], tokens_t[:, :, ds(c * PAIR, PAIR)], ACT.Copy).then_inc(tk_split, 1)
                for e in range(E):
                    k = e % 2
                    act.wait_ge(h_ready, E * c + e + 1)
                    if not first or e >= 2:
                        act.wait_ge(g_lo_ready, E * c + e - 1)
                    for m in range(KC):
                        gl = nc.scalar.activation(g[:, k, m, :], ps_h[k][:, m * PAIR:(m + 1) * PAIR], ACT.Gelu,
                                                  bias=b1[:, m, e:e + 1])
                    gl.then_inc(g_ready, 1)
                    act.wait_ge(g_ready, E * c + e + 1)
                    if not first or e >= 2:
                        act.wait_ge(y_ready, E * c + e - 1)
                    nc.scalar.activation(g_hi[:, k], g[:, k], ACT.Copy).then_inc(g_hi_ready, 1)

            loop(act, chunk)

        @block.tensor
        def _(pe):
            pe.wait_ge(w_ready, 2)
            pe.wait_ge(b2_in, 16)

            def chunk(c, first):
                for e in range(E + 1):
                    if e < E:
                        k = e % 2
                        if e == 0:
                            pe.wait_ge(tk_ready, c + 1)
                        if not first or e >= 2:
                            pe.wait_ge(g_ready, E * c + e - 1)
                        for m in range(KC):
                            h = ps_h[k][:, m * PAIR:(m + 1) * PAIR]
                            n = 0
                            for w, tk in ((w_hi, tk_hi), (w_lo, tk_hi), (w_hi, tk_lo)):
                                for q in range(KC):
                                    mm = pe.matmul(h, w[0][:, e, q, m * P:(m + 1) * P], tk[:, q, :], start=(n == 0),
                                                   stop=(n == 3 * KC - 1))
                                    n += 1
                        mm.then_inc(h_ready, 1)
                    if e > 0:
                        d, k = e - 1, (e - 1) % 2
                        pe.wait_ge(g_lo_ready, E * c + d + 1)
                        if not first or d >= 2:
                            pe.wait_ge(added, 2 * (E * c + d - 1))
                        for i in range(2):
                            y = ps_y[k][0:BIN, i * D:(i + 1) * D]
                            rows = slice(i * BIN, (i + 1) * BIN)
                            for q in range(KC):
                                pe.matmul(y, g_hi[:, k, q, rows], w_hi[1][:, d, q, :], start=(q == 0), stop=False)
                                pe.matmul(y, g_hi[:, k, q, rows], w_lo[1][:, d, q, :], start=False, stop=False)
                                pe.matmul(y, g_lo[:, k, q, rows], w_hi[1][:, d, q, :], start=False, stop=False)
                            mm = pe.matmul(y, ones_e[:, 0:BIN], b2x[:, d, :], start=False, stop=True)
                        mm.then_inc(y_ready, 1)

            loop(pe, chunk)

        @block.vector
        def _(dve):
            nc.vector.memset(ones_e[:], 1.0)
            nc.vector.memset(b2x[:], 0.0).then_inc(b2_step, 1)
            for n in range(2):
                dve.wait_ge(w_split, n + 1)
                nc.vector.tensor_tensor(w_lo[n][:], raw[:], w_hi[n][:].bitcast(F32), ALU.subtract).then_inc(w_ready, 1)
                if n == 0:
                    dve.wait_ge(small_in, 16 * 3)
                    for m in range(3):
                        a, b = b2[:, m % 2, :], b2[:, (m + 1) % 2, :]
                        dve.wait_ge(b2_step, 2 * m + 1)
                        part = nc.vector.tensor_copy(b2_part[:, m, :], a)
                        if m == 2:
                            part.then_inc(b2_ready, 1)
                        else:
                            part.then_inc(b2_step, 1)
                            dve.wait_ge(b2_step, 2 * m + 2)
                            nc.vector.tensor_tensor(b, a, b2_part[:, m, :], ALU.subtract).then_inc(b2_step, 1)

            def add(c, d, first):
                k = d % 2
                dve.wait_ge(y_ready, E * c + d + 1)
                for i in range(2):
                    row = node_rows[0:BIN, ds(2 * c + i, 1), :]
                    if d:
                        dve.wait_ge(added, 2 * (E * c + d - 1) + i + 1)
                    nc.vector.scalar_tensor_tensor(
                        out=row, in0=ps_y[k][0:BIN, i * D:(i + 1) * D].rearrange("p (o f) -> p o f", o=1),
                        scalar=combine[0:BIN, ds(2 * c + i, 1), d:d + 1].rearrange("p o e -> p (o e)"), in1=row,
                        op0=ALU.mult, op1=ALU.add).then_inc(added, 1)

            def chunk(c, first):
                dve.wait_ge(tk_split, c + 1)
                nc.vector.tensor_tensor(tk_lo[:], tokens_t[:, :, ds(c * PAIR, PAIR)], tk_hi[:].bitcast(F32),
                                        ALU.subtract).then_inc(tk_ready, 1)
                for e in range(E + 1):
                    if e < E:
                        k = e % 2
                        dve.wait_ge(g_hi_ready, E * c + e + 1)
                        nc.vector.tensor_tensor(g_lo[:, k], g[:, k], g_hi[:, k].bitcast(F32), ALU.subtract
                                                ).then_inc(g_lo_ready, 1)
                    if e > 0:
                        add(c, e - 1, first)

            loop(dve, chunk)


_OUT = (NODES, D)


def kernel(**inputs):
    import numpy as _np
    import concourse.bacc as _bacc
    from concourse import mybir as _mybir
    from concourse.bass_utils import run_bass_kernel_spmd as _run

    nc = _bacc.Bacc("TRN2", target_bir_lowering=False, num_devices=1)
    arrays, t = {}, {}
    for name in NAMES:
        a = _np.ascontiguousarray(inputs[name])
        arrays[f"in_{name}"] = a
        t[name] = nc.dram_tensor(f"in_{name}", a.shape, _mybir.dt.from_np(a.dtype), kind="ExternalInput").ap()
    out = nc.dram_tensor("out_rows", _OUT, F32, kind="ExternalOutput").ap()
    gnn_ffn(nc, t, out)
    r = _run(nc, [arrays], core_ids=[0])
    return r.results[0]["out_rows"]
```

```python
from contextlib import ExitStack

import concourse.bass as bass
from concourse import mybir

F32 = mybir.dt.float32
F32R = mybir.dt.float32r
BF16 = mybir.dt.bfloat16
I32 = mybir.dt.int32
U32 = mybir.dt.uint32
ALU = mybir.AluOpType
ACT = mybir.ActivationFunctionType
AX_X = mybir.AxisListType.X
ds = bass.ds

P = 128
D = 256
KC = D // P
NODES = 6250
EDGES = 100000
EXPERTS = 8
LN_EPS = 1e-5

BIN = P - 2
BINS = -(-NODES // BIN)
LAST = NODES - (BINS - 1) * BIN

EP, EC = 125, 800
assert EP * EC == EDGES
TILES = (EDGES + (P - 1) * BINS) // P
GROUPS = -(-TILES // 2)
TILES = 2 * GROUPS
RING = 6
TABLE_P = P - 3
TABLE_C = -(-TILES // TABLE_P)
SLOTS = TILES * P
WORDS = 4
CHUNK = 40
ROUND = 1.5 * 2 ** 23

NAMES = ["x", "src", "dst", "edge_weight1", "L0_gnn_mW1", "L0_gnn_mb1", "L0_gnn_ln_g", "L0_gnn_ln_b", "L0_gnn_mW2",
         "L0_gnn_mb2", "L0_gnn_uW1", "L0_gnn_ub1", "L0_gnn_uW2", "L0_gnn_ub2", "L0_ffn_router_w", "L0_ffn_w1",
         "L0_ffn_b1", "L0_ffn_w2", "L0_ffn_b2"]


def hold(engine, semaphore, value):
    engine.wait_ge(semaphore, value)
    engine.nop(nofuse=True)


def by_chunks(w):
    return w.rearrange("(c p) n -> p c n", p=P)


def one_row(v):
    return v.rearrange("(o n) -> o n", o=1)


def gnn_ffn(nc, t, out):
    with ExitStack() as whole:
        whole.enter_context(nc.allow_non_contiguous_dma("small transposed parameters"))
        node_rows = whole.enter_context(nc.sbuf_tensor("node_rows", [P, BINS, D], F32))
        dram = {
            "b_rows": nc.dram_tensor("b_rows", (BINS * BIN, D), F32).ap(),
            "u_rows": nc.dram_tensor("u_rows", (BINS * BIN, D), F32).ap(),
            "xh_rows": nc.dram_tensor("xh_rows", (BINS * BIN, D), F32).ap(),
            "sorted_edges": nc.dram_tensor("sorted_edges", (SLOTS, WORDS), F32).ap(),
            "tile_bins": nc.dram_tensor("tile_bins", (TABLE_P * TABLE_C,), I32).ap(),
        }
        ident = whole.enter_context(nc.sbuf_tensor("ident", [P, P], F32))
        with ExitStack() as edges:
            kept = {
                "a_at": nc.sbuf_base,
                "a_hi": edges.enter_context(nc.sbuf_tensor("a_hi", [P, BINS, D], F32R)),
                "a_lo": edges.enter_context(nc.sbuf_tensor("a_lo", [P, BINS, D], F32R)),
                "slots": edges.enter_context(nc.sbuf_tensor("slots", [P, TILES, WORDS], F32)),
                "w2_hi": edges.enter_context(nc.sbuf_tensor("w2_hi", [P, KC, D], F32R)),
                "w2_lo": edges.enter_context(nc.sbuf_tensor("w2_lo", [P, KC, D], F32R)),
                "c3": edges.enter_context(nc.sbuf_tensor("c3", [P, D], BF16)),
                "ones3": edges.enter_context(nc.sbuf_tensor("ones3", [P, P], BF16)),
                "iota": edges.enter_context(nc.sbuf_tensor("iota", [P, P], F32)),
            }
            nodes_and_sort(nc, t, dram, node_rows, ident, kept)
            messages(nc, dram, node_rows, ident, kept)
        with ExitStack() as rest:
            turned = rest.enter_context(nc.sbuf_tensor("tokens_t", [P, KC, BINS * BIN], F32))
            combine = rest.enter_context(nc.sbuf_tensor("combine", [P, BINS, EXPERTS], F32))
            w = {"hi": [], "lo": [], "raw": [], "in": rest.enter_context(nc.semaphore("expert_weights_in"))}
            for m in (1, 2):
                shape = [P, EXPERTS, KC, D]
                w["hi"].append(rest.enter_context(nc.sbuf_tensor(f"w{m}_hi_e", shape, F32R)))
                at = nc.sbuf_base
                w["lo"].append(rest.enter_context(nc.sbuf_tensor(f"w{m}_lo_e", shape, F32R)))
                w["raw"].append(nc.alloc_sbuf_tensor_at(f"w{m}_raw", shape, F32, offset=at))
            with nc.psum_tensor("ps_logits", [P, 512], F32) as ps_logits:
                update(nc, t, dram, node_rows, ident, turned, ps_logits, w)
                w["b1"] = rest.enter_context(nc.sbuf_tensor("b1", [P, KC, EXPERTS], F32))
                w["b2_rows"] = rest.enter_context(nc.sbuf_tensor("b2_rows", [P, EXPERTS, D], BF16))
                w["ones3"] = rest.enter_context(nc.sbuf_tensor("ones3_e", [P, P], BF16))
                route(nc, t, ps_logits, combine, w)
            experts(nc, node_rows, turned, combine, w, out)
def nodes_and_sort(nc, t, dram, node_rows, ident, kept):
    a_hi, a_lo, slots = kept["a_hi"], kept["a_lo"], kept["slots"]
    with ExitStack() as ctx:
        def sb(name, shape, dt=F32):
            return ctx.enter_context(nc.sbuf_tensor(name, shape, dt))

        def sem(name):
            return ctx.enter_context(nc.semaphore(name))

        def psum(name):
            return ctx.enter_context(nc.psum_tensor(name, [P, 512], F32))

        pay = sb("pay", [P, EC, WORDS])
        row_of = sb("row_of", [P, EC], I32)
        stage_row = sb("stage_row", [P, 2, CHUNK], I32)
        stage_pay = sb("stage_pay", [P, 2, CHUNK, WORDS])
        bins_f = sb("bins_f", [P, TABLE_C])
        bins_i = sb("bins_i", [P, TABLE_C], I32)
        tile_no = sb("tile_no", [P, TABLE_C])
        before = sb("before", [P, P])
        ones = sb("ones", [P, P])
        w1a = sb("w1a", [P, KC, D])
        w1b = sb("w1b", [P, KC, D])
        u1a = sb("u1a", [P, KC, D])
        b1_all = sb("b1_all", [P, D])
        ub1_all = sb("ub1_all", [P, D])
        ub2_all = sb("ub2_all", [P, D])
        gcol = sb("gcol", [P, KC])
        bcol = sb("bcol", [P, KC])
        mv = sb("mv", [P, BINS, 2])
        rstd = sb("rstd", [P, BINS])
        half = sb("half", [P, BINS])
        st6 = sb("st6", [P, 6])
        st2 = sb("st2", [P, 2])
        h = sb("h", [P, 2, D])
        ht = sb("ht", [P, 2, KC, BIN])
        u_out = sb("u_out", [P, 2, D])
        xh_out = sb("xh_out", [P, 2, D])
        with ExitStack() as early:
            w2 = early.enter_context(nc.sbuf_tensor("w2", [P, KC, D], F32))
        b_out = sb("b_out", [P, 2, D])

        at = [kept["a_at"]]

        def early_sb(name, shape, dt=F32):
            size = 4
            for n in shape[1:]:
                size *= n
            where = at[0]
            at[0] += -(-size // 32) * 32
            return nc.alloc_sbuf_tensor_at(name, shape, dt, offset=where)

        crow = early_sb("crow", [1, 3, D])
        cpart = early_sb("cpart", [1, 3, D], BF16)
        wc = early_sb("wc", [1, D])
        wc_hi = early_sb("wc_hi", [1, D], F32R)
        wc_lo = early_sb("wc_lo", [1, D], F32R)
        at[0] = kept["a_at"] + 4 * BINS * D
        bin_of = early_sb("bin_of", [EP, EC])
        src_f = early_sb("src_f", [EP, EC])
        srci = early_sb("srci", [EP, EC], I32)
        dsti = early_sb("dsti", [EP, EC], I32)
        wgt = early_sb("wgt", [EP, EC])
        waste = [early_sb(f"waste{k}", [EP, EC], BF16) for k in range(2)]
        marks = early_sb("marks", [EP, BINS, CHUNK + 1])
        ranks = early_sb("ranks", [EP, BINS, CHUNK + 1])
        carry = early_sb("carry", [EP, BINS, CHUNK + 1])
        slot = early_sb("slot", [EP, CHUNK])
        tile_of = early_sb("tile_of", [EP, CHUNK])
        rounded = early_sb("rounded", [EP, CHUNK])
        counts = early_sb("counts", [EP, BINS])
        tiles = early_sb("tiles", [TABLE_P, BINS])
        ends = early_sb("ends", [TABLE_P, BINS])
        gtmp = early_sb("gtmp", [TABLE_P, BINS])
        gtmp2 = early_sb("gtmp2", [TABLE_P, BINS])
        ahead = early_sb("ahead", [TABLE_P, TABLE_C, BINS])

        ps_t = [psum("ps_t0"), psum("ps_t1")]
        ps_a, ps_b, ps_u, ps_n, ps_c = (psum(f"ps_{x}") for x in "abunc")

        edges_in = sem("edges_in")
        x_in = sem("x_in")
        params_in = sem("params_in")
        last_clear = sem("last_clear")
        pool_consts = sem("pool_consts")
        masks_cut = sem("masks_cut")
        prep = sem("prep")
        counted = sem("counted")
        summed = sem("summed")
        base_ready = sem("base_ready")
        ranked = sem("ranked")
        chunk_ready = sem("chunk_ready")
        staged = sem("staged")
        scattered = [sem("scattered0"), sem("scattered1")]
        filled = sem("filled")
        cleared = sem("cleared")
        sorted_in = sem("sorted_in")
        table_ready = sem("table_ready")
        table_out = sem("table_out")
        wc_ready = sem("wc_ready")
        wc_out = sem("wc_out")
        c_ready = sem("c_ready")
        c_out = sem("c_out")
        c_mul = sem("c_mul")
        w2_centred = sem("w2_centred")
        w2_split = sem("w2_split")
        stats = sem("stats")
        var_ready = sem("var_ready")
        rstd_ready = sem("rstd_ready")
        h_ready = sem("h_ready")
        h_turned = sem("h_turned")
        ht_ready = sem("ht_ready")
        node_mul = sem("node_mul")
        a_hi_ready = sem("a_hi_ready")
        a_lo_ready = sem("a_lo_ready")
        xh_part = sem("xh_part")
        outs_ready = sem("outs_ready")
        outs_stored = [sem("outs_stored0"), sem("outs_stored1")]
        block = ctx.enter_context(nc.Block())
        n_params = 13
        STEPS = 10
        CHUNKS = EC // CHUNK
        FIRST = 9 * CHUNKS // 20

        @block.sync
        def _(sp):
            for dst, name in ((srci, "src"), (dsti, "dst")):
                sp.dma_start(dst[:], t[name].rearrange("(p c) -> p c", p=EP)).then_inc(edges_in, 16)
            sp.dma_start(wgt[:], t["edge_weight1"].rearrange("(p c) o -> p (c o)", p=EP)).then_inc(edges_in, 16)
            sp.dma_start(node_rows[0:BIN, 0:BINS - 1, :],
                         t["x"][0:(BINS - 1) * BIN, :].rearrange("(b p) f -> p b f", p=BIN)).then_inc(x_in, 16)
            sp.wait_ge(last_clear, 1)
            sp.dma_start(node_rows[0:LAST, BINS - 1, :], t["x"][(BINS - 1) * BIN:, :]).then_inc(x_in, 16)
            sp.wait_ge(cleared, 1)
            sp.dma_start(dram["sorted_edges"].rearrange("(p t) w -> p t w", p=P), slots[:]).then_inc(filled, 16)
            sp.wait_ge(table_ready, 1)
            sp.dma_start(dram["tile_bins"].rearrange("(p j) -> p j", p=TABLE_P), bins_i[0:TABLE_P, :]).then_inc(table_out, 16)
            sp.wait_ge(wc_ready, 1)
            for table, row in ((a_hi, wc_hi), (a_lo, wc_lo)):
                for p in (BIN, BIN + 1):
                    sp.dma_start(table[p:p + 1, :, :].bitcast(F32),
                                 row[0:1, :].bitcast(F32).rearrange("p (o f) -> p o f", o=1)
                                 .broadcast_to([1, BINS, D])).then_inc(wc_out, 16)
            sp.wait_ge(c_ready, 1)
            for n in range(3):
                sp.dma_start(kept["c3"][n:n + 1, :], cpart[0:1, n, :]).then_inc(c_out, 16)

            with sp.Fori(0, BINS // 2) as j:
                for k in range(2):
                    i = 2 * j + k
                    sp.wait_ge(outs_ready, 3 * i + 3)
                    for buf, name in ((b_out, "b_rows"), (u_out, "u_rows"), (xh_out, "xh_rows")):
                        sp.dma_start(dram[name][ds(i * BIN, BIN), :], buf[0:BIN, k, :]).then_inc(outs_stored[k], 16)
            for k in range(2):
                sp.wait_ge(scattered[k], 16 * EC // 2)
            sp.dma_start(slots[:], dram["sorted_edges"].rearrange("(p t) w -> p t w", p=P)).then_inc(sorted_in, 16)
            sp.wait_ge(sorted_in, 16)
            for k in range(2):
                sp.wait_ge(outs_stored[k], 16 * 3 * BINS // 2)
            sp.wait_ge(wc_out, 16 * 4)
            sp.wait_ge(c_out, 16 * 3)
            sp.wait_ge(table_out, 16)

        @block.gpsimd
        def _(pool):
            nc.gpsimd.memset(ident[:], 0.0).then_inc(pool_consts, 1)
            nc.gpsimd.memset(before[:], 1.0).then_inc(pool_consts, 1)
            nc.gpsimd.memset(ones[:], 1.0).then_inc(pool_consts, 1)
            nc.gpsimd.memset(half[:], -0.5).then_inc(pool_consts, 1)
            nc.gpsimd.iota(kept["iota"][:], [[1, P]], base=0, channel_multiplier=0,
                           allow_small_or_imprecise_dtypes=True).then_inc(pool_consts, 1)
            nc.gpsimd.iota(tile_no[:], [[1, TABLE_C]], base=0, channel_multiplier=TABLE_C,
                           allow_small_or_imprecise_dtypes=True).then_inc(pool_consts, 1)
            pool.wait_ge(pool_consts, 6)
            nc.gpsimd.affine_select(out=ident[:], in_=ident[:], compare_op=ALU.not_equal, fill=1.0, base=0,
                                    pattern=[[-1, P]], channel_multiplier=1).then_inc(masks_cut, 1)
            nc.gpsimd.affine_select(out=before[:], in_=before[:], compare_op=ALU.is_ge, fill=0.0, base=-1,
                                    pattern=[[1, P]], channel_multiplier=-1).then_inc(masks_cut, 1)

            def stage_and_scatter(j, k, first):
                s = 2 * j + k
                if not first:
                    hold(pool, scattered[k], 16 * CHUNK * j)
                nc.gpsimd.tensor_copy(stage_row[0:EP, k, :], row_of[0:EP, ds(s * CHUNK, CHUNK)]).then_inc(staged, 1)
                nc.gpsimd.tensor_copy(stage_pay[0:EP, k], pay[0:EP, ds(s * CHUNK, CHUNK), :]).then_inc(staged, 1)
                hold(pool, staged, 2 * s + 2)
                for c in range(CHUNK):
                    nc.gpsimd.indirect_dma_start(
                        dram["sorted_edges"], bass.IndirectOffsetOnAxis(ap=stage_row[0:EP, k, c:c + 1], axis=0),
                        stage_pay[0:EP, k, c, :], None).then_inc(scattered[k], 16)

            pool.wait_ge(filled, 16)
            pool.wait_ge(chunk_ready, 1)
            stage_and_scatter(0, 0, True)
            pool.wait_ge(chunk_ready, 2)
            stage_and_scatter(0, 1, True)

            def scatter(first, last):
                with pool.Fori(first, last) as j:
                    for k in range(2):
                        hold(pool, chunk_ready, 2 * j + k + 1)
                        stage_and_scatter(j, k, False)

            scatter(1, FIRST // 2)
            pool.wait_ge(var_ready, 1)
            nc.gpsimd.tensor_tensor(rstd[0:BIN, :], mv[0:BIN, :, 1], half[0:BIN, :], ALU.pow).then_inc(rstd_ready, 1)
            scatter(FIRST // 2, CHUNKS // 2)

        @block.scalar
        def _(act):
            mw1, uw1 = t["L0_gnn_mW1"], t["L0_gnn_uW1"]
            for dst, src in ((w1a, by_chunks(mw1[0:D, :])), (w1b, by_chunks(mw1[D:2 * D, :])),
                             (u1a, by_chunks(uw1[0:D, :])), (w2, by_chunks(t["L0_gnn_mW2"]))):
                act.dma_start(dst[:], src).then_inc(params_in, 16)
            for dst, name in ((b1_all, "L0_gnn_mb1"), (ub1_all, "L0_gnn_ub1"), (ub2_all, "L0_gnn_ub2")):
                act.dma_start(dst[:], one_row(t[name]).broadcast_to([P, D])).then_inc(params_in, 16)
            act.dma_start(wc[:], mw1[2 * D:2 * D + 1, :]).then_inc(params_in, 16)
            act.dma_start(crow[0:1, 0, :], one_row(t["L0_gnn_mb2"])).then_inc(params_in, 16)
            for dst, name in ((gcol, "L0_gnn_ln_g"), (bcol, "L0_gnn_ln_b")):
                for c in range(KC):
                    act.dma_start(dst[:, c:c + 1], t[name][c * P:(c + 1) * P].rearrange("(p o) -> p o", o=1)
                                  ).then_inc(params_in, 16)

            def copies(i, k, first):
                act.wait_ge(h_turned, i + 1)
                if not first:
                    act.wait_ge(node_mul, i - 1)
                nc.scalar.activation(ht[:, k], ps_t[k][:, 0:KC * BIN].rearrange("p (c n) -> p c n", c=KC),
                                     ACT.Copy).then_inc(ht_ready, 1)
                hold(act, node_mul, i + 1)
                nc.scalar.activation(a_hi[0:BIN, ds(i, 1), :], ps_a[0:BIN, 0:D].rearrange("p (o f) -> p o f", o=1),
                                     ACT.Copy).then_inc(a_hi_ready, 1)

            copies(0, 0, True)
            copies(1, 1, True)
            with act.Fori(1, BINS // 2) as j:
                for k in range(2):
                    copies(2 * j + k, k, False)

        @block.tensor
        def _(pe):
            pe.wait_ge(masks_cut, 2)
            pe.wait_ge(counted, BINS)
            pe.matmul(ps_n[:, 0:BINS], before[0:EP, :], counts[:], start=True, stop=True)
            pe.matmul(ps_n[:, BINS:2 * BINS], ones[0:EP, :], counts[:], start=True, stop=True).then_inc(summed, 1)
            pe.wait_ge(params_in, 16 * n_params)
            for c in range(KC):
                mm = pe.matmul(ps_c[0:1, 0:D], bcol[:, c:c + 1], w2[:, c, :], start=(c == 0), stop=(c == KC - 1))
            mm.then_inc(c_mul, 1)
            pe.wait_ge(w2_split, 3)
            for c in range(KC):
                mm = pe.matmul(ps_n[:, 0:D], ones[:], w2[:, c, :], start=(c == 0), stop=(c == KC - 1))
            mm.then_inc(c_mul, 1)

            def products(i, k, first):
                pe.wait_ge(h_ready, i + 1)
                for c in range(KC):
                    tr = pe.transpose(ps_t[k][:, c * BIN:(c + 1) * BIN], h[0:BIN, k, c * P:(c + 1) * P],
                                      ident[0:BIN, 0:BIN])
                tr.then_inc(h_turned, 1)
                pe.wait_ge(ht_ready, i + 1)
                if not first:
                    pe.wait_ge(outs_ready, 3 * i)
                    pe.wait_ge(a_lo_ready, i)
                for ps, w in ((ps_a, w1a), (ps_b, w1b), (ps_u, u1a)):
                    for c in range(KC):
                        mm = pe.matmul(ps[0:BIN, 0:D], ht[:, k, c, :], w[:, c, :], start=(c == 0),
                                       stop=(c == KC - 1))
                mm.then_inc(node_mul, 1)

            products(0, 0, True)
            products(1, 1, False)
            with pe.Fori(1, BINS // 2) as j:
                for k in range(2):
                    products(2 * j + k, k, False)

        @block.vector
        def _(dve):
            nc.vector.memset(node_rows[:, BINS - 1, :], 0.0).then_inc(last_clear, 1)
            nc.vector.memset(slots[:], 0.0).then_inc(prep, 1)
            nc.vector.memset(kept["c3"][:], 0.0)
            nc.vector.memset(kept["ones3"][:], 1.0).then_inc(prep, 1)
            dve.wait_ge(prep, 2)
            nc.vector.memset(slots[:, :, 1:2], -1.0).then_inc(cleared, 1)
            dve.wait_ge(edges_in, 16 * 3)
            nc.vector.tensor_copy(pay[0:EP, :, 0].bitcast(I32), dsti[:]).then_inc(prep, 1)
            nc.vector.tensor_copy(pay[0:EP, :, 2].bitcast(F32R), wgt[:]).then_inc(prep, 1)
            nc.vector.tensor_copy(src_f[:], srci[:]).then_inc(prep, 1)
            dve.wait_ge(prep, 5)
            nc.vector.tensor_tensor(pay[0:EP, :, 3].bitcast(F32R), wgt[:], pay[0:EP, :, 2],
                                    ALU.subtract).then_inc(prep, 1)
            nc.vector.tensor_scalar(bin_of[:], src_f[:], 1.0 / BIN, 0.5 / BIN - 0.5, ALU.mult,
                                    ALU.add).then_inc(prep, 1)
            dve.wait_ge(prep, 7)
            nc.vector.tensor_scalar(wgt[:], bin_of[:], ROUND, None, ALU.add).then_inc(prep, 1)
            dve.wait_ge(prep, 8)
            nc.vector.tensor_scalar(bin_of[:], wgt[:], -ROUND, None, ALU.add).then_inc(prep, 1)
            dve.wait_ge(prep, 9)
            nc.vector.scalar_tensor_tensor(out=pay[0:EP, :, 1], in0=bin_of[:], scalar=-float(BIN),
                                           in1=src_f[:], op0=ALU.mult, op1=ALU.add).then_inc(prep, 1)
            nc.vector.memset(carry[:], 1.0).then_inc(prep, 1)
            dve.wait_ge(prep, 11)
            nc.vector.memset(carry[:, :, 0:1], 0.0).then_inc(ranked, 1)
            dve.wait_ge(pool_consts, 6)
            dve.wait_ge(prep, 10)

            def count(j, k, first):
                b = 2 * j + k
                if not first:
                    dve.wait_ge(counted, b - 1)
                nc.vector.tensor_scalar(waste[k][:], bin_of[:], kept["iota"][0:EP, ds(b, 1)], 0.0,
                                        ALU.is_equal, ALU.add, accum_out=counts[:, ds(b, 1)]).then_inc(counted, 1)

            count(0, 0, True)
            count(0, 1, True)
            with dve.Fori(1, BINS // 2) as j:
                for k in range(2):
                    count(j, k, False)
            dve.wait_ge(summed, 1)
            nc.vector.tensor_scalar(gtmp[:], ps_n[0:TABLE_P, BINS:2 * BINS], 1.0 / P,
                                    (P - 1.0) / P - 0.5 + 0.5 / P, ALU.mult, ALU.add
                                    ).then_inc(base_ready, 1)
            dve.wait_ge(base_ready, 1)
            nc.vector.tensor_scalar(gtmp2[:], gtmp[:], ROUND, None, ALU.add).then_inc(base_ready, 1)
            dve.wait_ge(base_ready, 2)
            nc.vector.tensor_scalar(tiles[:], gtmp2[:], -ROUND, None, ALU.add).then_inc(base_ready, 1)
            dve.wait_ge(base_ready, 3)
            nc.vector.tensor_tensor_scan(ends[:], tiles[:], tiles[:], 0.0, ALU.add, ALU.max
                                         ).then_inc(base_ready, 1)
            dve.wait_ge(base_ready, 4)
            nc.vector.tensor_tensor(gtmp[:], ends[:], tiles[:], ALU.subtract).then_inc(base_ready, 1)
            dve.wait_ge(base_ready, 5)
            nc.vector.scalar_tensor_tensor(out=ranks[:, :, CHUNK:CHUNK + 1],
                                           in0=gtmp[0:EP, :].rearrange("p (b o) -> p b o", o=1), scalar=float(P),
                                           in1=ps_n[0:EP, 0:BINS].rearrange("p (b o) -> p b o", o=1), op0=ALU.mult,
                                           op1=ALU.add).then_inc(base_ready, 1)
            nc.vector.tensor_tensor(ahead[:], ends[:].rearrange("p (o b) -> p o b", o=1).broadcast_to([TABLE_P, TABLE_C, BINS]),
                                    tile_no[0:TABLE_P, :].rearrange("p (j o) -> p j o", o=1).broadcast_to([TABLE_P, TABLE_C, BINS]),
                                    ALU.is_le).then_inc(base_ready, 1)
            dve.wait_ge(base_ready, 7)
            nc.vector.tensor_reduce(bins_f[0:TABLE_P, :], ahead[:], AX_X, ALU.add).then_inc(base_ready, 1)
            dve.wait_ge(base_ready, 8)
            nc.vector.tensor_scalar(bins_i[0:TABLE_P, :], bins_f[0:TABLE_P, :], float(BINS - 1), None, ALU.min
                                    ).then_inc(table_ready, 1)

            with dve.Fori(0, CHUNKS) as n:
                cols = ds(n * CHUNK, CHUNK)
                step = STEPS * n + 1
                dve.wait_ge(ranked, step)
                nc.vector.tensor_tensor(
                    marks[:, :, 1:], bin_of[:, cols].rearrange("p (o c) -> p o c", o=1).broadcast_to([EP, BINS, CHUNK]),
                    kept["iota"][0:EP, 0:BINS].rearrange("p (b o) -> p b o", o=1).broadcast_to([EP, BINS, CHUNK]),
                    ALU.is_equal).then_inc(ranked, 1)
                nc.vector.tensor_scalar(marks[:, :, 0:1], ranks[:, :, CHUNK:], 0.0, None, ALU.add).then_inc(ranked, 1)
                dve.wait_ge(ranked, step + 2)
                nc.vector.tensor_tensor_scan(ranks[:].rearrange("p b c -> p (b c)"),
                                             carry[:].rearrange("p b c -> p (b c)"),
                                             marks[:].rearrange("p b c -> p (b c)"), 0.0, ALU.mult, ALU.add
                                             ).then_inc(ranked, 1)
                dve.wait_ge(ranked, step + 3)
                nc.vector.tensor_tensor(marks[:, :, 1:], marks[:, :, 1:], ranks[:, :, 1:], ALU.mult
                                        ).then_inc(ranked, 1)
                hold(dve, ranked, step + 4)
                nc.vector.tensor_reduce(slot[:], marks[:, :, 1:].rearrange("p b c -> p c b"), AX_X, ALU.add
                                        ).then_inc(ranked, 1)
                dve.wait_ge(ranked, step + 5)
                nc.vector.tensor_scalar(tile_of[:], slot[:], 1.0 / P, -1.0 / P - 0.5 + 0.5 / P, ALU.mult,
                                        ALU.add).then_inc(ranked, 1)
                dve.wait_ge(ranked, step + 6)
                nc.vector.tensor_scalar(rounded[:], tile_of[:], ROUND, None, ALU.add).then_inc(ranked, 1)
                dve.wait_ge(ranked, step + 7)
                nc.vector.tensor_scalar(tile_of[:], rounded[:], -ROUND, None, ALU.add).then_inc(ranked, 1)
                dve.wait_ge(ranked, step + 8)
                nc.vector.scalar_tensor_tensor(out=rounded[:], in0=tile_of[:], scalar=-float(P), in1=slot[:],
                                               op0=ALU.mult, op1=ALU.add).then_inc(ranked, 1)
                dve.wait_ge(ranked, step + 9)
                nc.vector.tensor_scalar(slot[:], rounded[:], float(TILES), -float(TILES), ALU.mult, ALU.add
                                        ).then_inc(ranked, 1)
                dve.wait_ge(ranked, step + 10)
                nc.vector.tensor_tensor(row_of[0:EP, cols], slot[:], tile_of[:], ALU.add).then_inc(chunk_ready, 1)

            dve.wait_ge(x_in, 32)
            with dve.Fori(0, BINS) as i:
                nc.vector.bn_stats(st6[0:BIN, :], node_rows[0:BIN, ds(i, 1), :].rearrange("p o f -> p (o f)")
                                   ).then_inc(stats, 1)
                hold(dve, stats, 3 * i + 1)
                nc.vector.bn_aggr(st2[0:BIN, :], st6[0:BIN, :]).then_inc(stats, 1)
                dve.wait_ge(stats, 3 * i + 2)
                nc.vector.tensor_scalar(mv[0:BIN, ds(i, 1), :], st2[0:BIN, :].rearrange("p (o f) -> p o f", o=1),
                                        0.0, None, ALU.add).then_inc(stats, 1)
                hold(dve, stats, 3 * i + 3)
            nc.vector.tensor_scalar(mv[0:BIN, :, 1], mv[0:BIN, :, 1], LN_EPS, None, ALU.add).then_inc(var_ready, 1)
            dve.wait_ge(params_in, 16 * n_params)
            nc.vector.tensor_copy(wc_hi[:], wc[:]).then_inc(w2_split, 1)
            dve.wait_ge(c_mul, 1)
            for c in range(KC):
                nc.vector.tensor_scalar(w2[:, c, :], w2[:, c, :], gcol[:, c:c + 1], None, ALU.mult
                                        ).then_inc(w2_split, 1)
            nc.vector.tensor_tensor(crow[0:1, 0, :], crow[0:1, 0, :], ps_c[0:1, 0:D], ALU.add).then_inc(w2_split, 1)
            dve.wait_ge(w2_split, 4)
            nc.vector.tensor_tensor(wc_lo[:], wc[:], wc_hi[:].bitcast(F32), ALU.subtract).then_inc(wc_ready, 1)
            dve.wait_ge(c_mul, 2)
            for c in range(KC):
                centred = nc.vector.scalar_tensor_tensor(out=w2[:, c, :], in0=ps_n[:, 0:D], scalar=-1.0 / D,
                                                         in1=w2[:, c, :], op0=ALU.mult, op1=ALU.add)
            centred.then_inc(w2_centred, 1)
            dve.wait_ge(w2_centred, 1)
            nc.vector.tensor_copy(kept["w2_hi"][:], w2[:]).then_inc(w2_split, 1)
            nc.vector.tensor_copy(cpart[0:1, 0, :], crow[0:1, 0, :]).then_inc(w2_split, 1)
            dve.wait_ge(w2_split, 6)
            nc.vector.tensor_tensor(kept["w2_lo"][:], w2[:], kept["w2_hi"][:].bitcast(F32), ALU.subtract
                                    ).then_inc(w2_split, 1)
            nc.vector.tensor_tensor(crow[0:1, 1, :], crow[0:1, 0, :], cpart[0:1, 0, :], ALU.subtract
                                    ).then_inc(w2_split, 1)
            dve.wait_ge(w2_split, 8)
            nc.vector.tensor_copy(cpart[0:1, 1, :], crow[0:1, 1, :]).then_inc(w2_split, 1)
            dve.wait_ge(w2_split, 9)
            nc.vector.tensor_tensor(crow[0:1, 2, :], crow[0:1, 1, :], cpart[0:1, 1, :], ALU.subtract
                                    ).then_inc(w2_split, 1)
            dve.wait_ge(w2_split, 10)
            nc.vector.tensor_copy(cpart[0:1, 2, :], crow[0:1, 2, :]).then_inc(c_ready, 1)

            def node(j, k, first):
                i = 2 * j + k
                row = node_rows[0:BIN, ds(i, 1), :].rearrange("p o f -> p (o f)")
                if not first:
                    dve.wait_ge(h_turned, i - 1)
                    dve.wait_ge(outs_stored[k], 16 * 3 * j)
                nc.vector.tensor_scalar(h[0:BIN, k, :], row, mv[0:BIN, ds(i, 1), 0:1].rearrange("p o f -> p (o f)"),
                                        rstd[0:BIN, ds(i, 1)], ALU.subtract, ALU.mult).then_inc(h_ready, 1)
                dve.wait_ge(h_ready, i + 1)
                nc.vector.tensor_tensor(xh_out[0:BIN, k, :], h[0:BIN, k, :], row, ALU.add).then_inc(xh_part, 1)
                dve.wait_ge(xh_part, i + 1)
                nc.vector.tensor_tensor(xh_out[0:BIN, k, :], xh_out[0:BIN, k, :], ub2_all[0:BIN, :], ALU.add
                                        ).then_inc(outs_ready, 1)
                dve.wait_ge(node_mul, i + 1)
                nc.vector.tensor_tensor(b_out[0:BIN, k, :], ps_b[0:BIN, 0:D], b1_all[0:BIN, :], ALU.add
                                        ).then_inc(outs_ready, 1)
                nc.vector.tensor_tensor(u_out[0:BIN, k, :], ps_u[0:BIN, 0:D], ub1_all[0:BIN, :], ALU.add
                                        ).then_inc(outs_ready, 1)
                dve.wait_ge(a_hi_ready, i + 1)
                nc.vector.tensor_tensor(a_lo[0:BIN, ds(i, 1), :],
                                        ps_a[0:BIN, 0:D].rearrange("p (o f) -> p o f", o=1),
                                        a_hi[0:BIN, ds(i, 1), :].bitcast(F32), ALU.subtract).then_inc(a_lo_ready, 1)

            dve.wait_ge(rstd_ready, 1)
            dve.wait_ge(chunk_ready, CHUNKS)
            dve.wait_ge(wc_out, 16 * 4)
            dve.wait_ge(c_out, 16 * 3)
            node(0, 0, True)
            node(0, 1, True)
            with dve.Fori(1, BINS // 2) as j:
                for k in range(2):
                    node(j, k, False)

def messages(nc, dram, node_rows, ident, kept):
    a_hi, a_lo, slots, iota = kept["a_hi"], kept["a_lo"], kept["slots"], kept["iota"]
    w2_hi, w2_lo, c3, ones3 = kept["w2_hi"], kept["w2_lo"], kept["c3"], kept["ones3"]
    with ExitStack() as ctx:
        def sb(name, shape, dt=F32):
            return ctx.enter_context(nc.sbuf_tensor(name, shape, dt))

        def sem(name):
            return ctx.enter_context(nc.semaphore(name))

        tile_bin = sb("tile_bin", [1, TABLE_P * TABLE_C], I32)
        dst_row = sb("dst_row", [P, RING, 2], I32)
        onehot = sb("onehot", [P, RING, 2, P])
        onehot_t = sb("onehot_t", [P, 2, 2, P], F32R)
        rows = [sb(f"rows{r}", [P, 2, D]) for r in range(RING)]
        st6 = sb("st6_m", [P, 2, 6])
        mv = sb("mv_m", [P, RING, 2, 2])
        rstd = sb("rstd_m", [P, RING, 2])
        half = sb("half_m", [P, 2])
        t_hi = sb("t_hi", [P, 2, 2, KC, P], F32R)
        t_lo = sb("t_lo", [P, 2, 2, KC, P], F32R)
        msg = sb("msg", [P, 2, 2, D])

        def psum(name, n=2, width=512):
            return [ctx.enter_context(nc.psum_tensor(f"{name}{k}", [P, width], F32)) for k in range(n)]

        ps_oh = ctx.enter_context(nc.psum_tensor("ps_oh", [P, 512], F32))
        ps_pre = psum("ps_pre")
        ps_rt = psum("ps_rt")
        ps_z = psum("ps_z")
        ps_agg = ctx.enter_context(nc.psum_tensor("ps_agg", [P, 512], F32))

        table_in = sem("table_in")
        start = sem("start")
        dst_ready = sem("dst_ready")
        b_landed = [sem(f"b_landed{r}") for r in range(RING)]
        onehot_ready = sem("onehot_ready")
        onehot_turned = sem("onehot_turned")
        onehot_t_ready = sem("onehot_t_ready")
        a_gathered = sem("a_gathered")
        pre_ready = sem("pre_ready")
        silu_ready = sem("silu_ready")
        tile_stats = sem("tile_stats")
        stats_ready = sem("stats_ready")
        eps_added = sem("eps_added")
        rstd_ready = sem("rstd_ready")
        norm_ready = sem("norm_ready")
        rows_turned = sem("rows_turned")
        hi_ready = sem("hi_ready")
        lo_ready = sem("lo_ready")
        z_ready = sem("z_ready")
        msg_ready = sem("msg_ready")
        part_ready = sem("part_ready")
        added = sem("added")
        block = ctx.enter_context(nc.Block())

        def pipeline(engine, step, last):
            for n in range(2 * RING):
                step(n // RING, n % RING, lambda d: n - d >= 0)
            with engine.Fori(2, GROUPS // RING) as j:
                for r in range(RING):
                    step(j, r, lambda d: True)
            for n in range(GROUPS // RING * RING, GROUPS + last):
                step(n // RING, n % RING, lambda d: n - d < GROUPS)

        @block.sync
        def _(sp):
            sp.dma_start(tile_bin[:], one_row(dram["tile_bins"])).then_inc(table_in, 16)
            sp.wait_ge(table_in, 16)

        @block.gpsimd
        def _(pool):
            nc.gpsimd.memset(half[:], -0.5).then_inc(start, 1)
            pool.wait_ge(start, 1)

            def step(j, r, live):
                n = RING * j + r
                if live(0):
                    if live(RING):
                        hold(pool, rows_turned, n - RING + 1)
                    nc.gpsimd.tensor_copy(dst_row[:, r, :], slots[:, ds(2 * n, 2), 0].bitcast(I32)
                                          ).then_inc(dst_ready, 1)
                    hold(pool, dst_ready, n + 1)
                    for i in range(2):
                        nc.gpsimd.indirect_dma_start(
                            rows[r][:, i, :], None, dram["b_rows"],
                            bass.IndirectOffsetOnAxis(ap=dst_row[:, r, i:i + 1], axis=0)).then_inc(b_landed[r], 16)
                if live(2):
                    g, q = n - 2, (r - 2) % RING
                    hold(pool, stats_ready, g + 1)
                    nc.gpsimd.tensor_scalar(mv[:, q, :, 1], mv[:, q, :, 1], LN_EPS, None, ALU.add
                                            ).then_inc(eps_added, 1)
                    pool.wait_ge(eps_added, g + 1)
                    nc.gpsimd.tensor_tensor(rstd[:, q, :], mv[:, q, :, 1], half[:], ALU.pow).then_inc(rstd_ready, 1)

            pipeline(pool, step, 2)

        @block.scalar
        def _(act):
            def step(j, r, live):
                n = RING * j + r
                if live(3):
                    g, q = n - 3, (r - 3) % RING
                    act.wait_ge(rstd_ready, g + 1)
                    for i in range(2):
                        nm = nc.scalar.activation(rows[q][:, i, :], rows[q][:, i, :], ACT.Copy,
                                                  scale=rstd[:, q, i:i + 1])
                    nm.then_inc(norm_ready, 1)
                if live(5):
                    g, k = n - 5, (r - 5) % 2
                    act.wait_ge(z_ready, g + 1)
                    if live(5 + 2):
                        act.wait_ge(part_ready, g - 1)
                    nc.scalar.activation(msg[:, k], ps_z[k][:].rearrange("p (i n) -> p i n", i=2), ACT.Silu
                                         ).then_inc(msg_ready, 1)
                if live(0):
                    k = r % 2
                    act.wait_ge(onehot_turned, n + 1)
                    if live(2):
                        act.wait_ge(a_gathered, n - 1)
                    nc.scalar.activation(onehot_t[:, k], ps_oh[:, 0:2 * P].rearrange("p (i n) -> p i n", i=2),
                                         ACT.Copy).then_inc(onehot_t_ready, 1)
                if live(3):
                    g, k = n - 3, (r - 3) % 2
                    act.wait_ge(rows_turned, g + 1)
                    if live(3 + 2):
                        act.wait_ge(z_ready, g - 1)
                    nc.scalar.activation(t_hi[:, k].rearrange("p i c e -> p (i c e)"), ps_rt[k][:], ACT.Copy
                                         ).then_inc(hi_ready, 1)
                if live(1):
                    g, x = n - 1, rows[(r - 1) % RING]
                    act.wait_ge(pre_ready, g + 1)
                    nc.scalar.activation(x[:], x[:], ACT.Silu).then_inc(silu_ready, 1)

            pipeline(act, step, 5)

        @block.tensor
        def _(pe):
            pe.wait_ge(table_in, 16)

            def step(j, r, live):
                n = RING * j + r
                if live(1):
                    b = [pe.value_load(tile_bin[0:1, ds(2 * (n - 1) + i, 1)], min_val=0, max_val=BINS - 1)
                         for i in range(2)]
                if live(1):
                    g, k = n - 1, (r - 1) % 2
                    pe.wait_ge(onehot_t_ready, g + 1)
                    if live(1 + 2):
                        pe.wait_ge(pre_ready, g - 1)
                    for i in range(2):
                        pre = ps_pre[k][:, i * D:(i + 1) * D]
                        pe.matmul(pre, onehot_t[:, k, i, :], a_hi[:, ds(b[i], 1), :].rearrange("p o f -> p (o f)"),
                                  start=True, stop=False)
                        mm = pe.matmul(pre, onehot_t[:, k, i, :],
                                       a_lo[:, ds(b[i], 1), :].rearrange("p o f -> p (o f)"), start=False, stop=True)
                    mm.then_inc(a_gathered, 1)
                if live(0):
                    pe.wait_ge(onehot_ready, n + 1)
                    if live(1):
                        pe.wait_ge(onehot_t_ready, n)
                    for i in range(2):
                        tr = pe.transpose(ps_oh[:, i * P:(i + 1) * P], onehot[:, r, i, :], ident[:])
                    tr.then_inc(onehot_turned, 1)
                if live(3):
                    g, k, q = n - 3, (r - 3) % 2, (r - 3) % RING
                    pe.wait_ge(norm_ready, g + 1)
                    if live(3 + 2):
                        pe.wait_ge(lo_ready, g - 1)
                    for i in range(2):
                        for c in range(KC):
                            tr = pe.transpose(ps_rt[k][:, (i * KC + c) * P:(i * KC + c + 1) * P],
                                              rows[q][:, i, c * P:(c + 1) * P], ident[:])
                    tr.then_inc(rows_turned, 1)
                if live(5):
                    g, k, q = n - 5, (r - 5) % 2, (r - 5) % RING
                    pe.wait_ge(msg_ready, g + 1)
                    if live(5 + 1):
                        pe.wait_ge(added, 2 * g + 1)
                    for i in range(2):
                        mm = pe.matmul(ps_agg[0:BIN, i * D:(i + 1) * D], onehot[:, q, i, 0:BIN], msg[:, k, i, :],
                                       start=True, stop=True)
                    mm.then_inc(part_ready, 1)
                if live(4):
                    g, k = n - 4, (r - 4) % 2
                    pe.wait_ge(lo_ready, g + 1)
                    if live(4 + 2):
                        pe.wait_ge(msg_ready, g - 1)
                    for i in range(2):
                        z = ps_z[k][:, i * D:(i + 1) * D]
                        pe.matmul(z, ones3[:], c3[:], start=True, stop=False)
                        for c in range(KC):
                            pe.matmul(z, t_hi[:, k, i, c, :], w2_hi[:, c, :], start=False, stop=False)
                            pe.matmul(z, t_hi[:, k, i, c, :], w2_lo[:, c, :], start=False, stop=False)
                            mm = pe.matmul(z, t_lo[:, k, i, c, :], w2_hi[:, c, :], start=False, stop=(c == KC - 1))
                    mm.then_inc(z_ready, 1)

            pipeline(pe, step, 5)

        @block.vector
        def _(dve):
            nc.vector.memset(node_rows[:], 0.0).then_inc(added, 1)
            dve.wait_ge(table_in, 16)

            def step(j, r, live):
                n = RING * j + r
                if live(6):
                    b = [dve.value_load(tile_bin[0:1, ds(2 * (n - 6) + i, 1)], min_val=0, max_val=BINS - 1)
                         for i in range(2)]

                def add_sums(i):
                    g = n - 6
                    dve.wait_ge(part_ready, g + 1)
                    dve.wait_ge(added, 2 * g + i + 1)
                    sums = node_rows[0:BIN, ds(b[i], 1), :]
                    nc.vector.tensor_tensor(sums, sums, ps_agg[0:BIN, i * D:(i + 1) * D]
                                            .rearrange("p (o f) -> p o f", o=1), ALU.add).then_inc(added, 1)

                if live(0):
                    if live(RING):
                        dve.wait_ge(part_ready, n - RING + 1)
                    tiles = slots[:, ds(2 * n, 2), :]
                    nc.vector.tensor_tensor(
                        onehot[:, r, :, 0:BIN],
                        iota[:, 0:BIN].rearrange("p (o n) -> p o n", o=1).broadcast_to([P, 2, BIN]),
                        tiles[:, :, 1:2].broadcast_to([P, 2, BIN]), ALU.is_equal)
                    nc.vector.tensor_copy(onehot[:, r, :, BIN:P], tiles[:, :, 2:4]).then_inc(onehot_ready, 1)
                if live(6):
                    add_sums(0)
                if live(2):
                    g, q = n - 2, (r - 2) % RING
                    dve.wait_ge(silu_ready, g + 1)
                    for i in range(2):
                        nc.vector.bn_stats(st6[:, i, :], rows[q][:, i, :]).then_inc(tile_stats, 1)
                if live(6):
                    add_sums(1)
                if live(4):
                    g, k = n - 4, (r - 4) % 2
                    dve.wait_ge(hi_ready, g + 1)
                    if live(2):
                        dve.wait_ge(tile_stats, 2 * (n - 2) + 2)
                    nc.vector.tensor_tensor(t_lo[:, k].rearrange("p i c e -> p (i c e)"), ps_rt[k][:],
                                            t_hi[:, k].rearrange("p i c e -> p (i c e)").bitcast(F32),
                                            ALU.subtract).then_inc(lo_ready, 1)
                if live(2):
                    g, q = n - 2, (r - 2) % RING
                    if not live(4):
                        dve.wait_ge(tile_stats, 2 * g + 2)
                    for i in range(2):
                        ag = nc.vector.bn_aggr(mv[:, q, i, :], st6[:, i, :])
                    ag.then_inc(stats_ready, 1)
                if live(1):
                    g, q = n - 1, (r - 1) % RING
                    dve.wait_ge(a_gathered, g + 1)
                    dve.wait_ge(b_landed[q], 32 * (j + (r >= 1)))
                    x = rows[q][:].rearrange("p i f -> p (i f)")
                    nc.vector.tensor_tensor(x, x, ps_pre[q % 2][:], ALU.add).then_inc(pre_ready, 1)

            pipeline(dve, step, 6)

def update(nc, t, dram, node_rows, ident, tokens_t, ps_logits, w):
    R = 4
    with ExitStack() as ctx:
        def sb(name, shape, dt=F32):
            return ctx.enter_context(nc.sbuf_tensor(name, shape, dt))

        def sem(name):
            return ctx.enter_context(nc.semaphore(name))

        def psum(name):
            return ctx.enter_context(nc.psum_tensor(name, [P, 512], F32))

        u1b = sb("u1b", [P, KC, D])
        u2 = sb("u2", [P, KC, D])
        rw = sb("rw", [P, KC, EXPERTS])
        u_row = sb("u_row", [P, R, D])
        xh_row = sb("xh_row", [P, R, D])
        agg = sb("agg", [P, R, D])
        agg_t = sb("agg_t", [P, R, KC, BIN])
        act1 = sb("act1", [P, R, D])
        act1_t = sb("act1_t", [P, R, KC, BIN])
        x1 = sb("x1", [P, R, D])
        h2 = sb("h2", [P, R, D])
        h2_t = sb("h2_t", [P, R, KC, BIN])
        st6 = sb("st6_u", [P, R, 6])
        mv = sb("mv_u", [P, R, 2])
        rstd = sb("rstd_u", [P, R, 1])
        half = sb("half_u", [P, 1])
        ps_at, ps_st, ps_ht = (psum(f"ps_{x}") for x in ("at", "st", "ht"))
        ps_v = [psum("ps_v0"), psum("ps_v1")]
        ps_y = [psum("ps_y0"), psum("ps_y1")]

        weights_in = sem("weights_in")
        u_in = [sem(f"u_in{r}") for r in range(R)]
        xh_in = [sem(f"xh_in{r}") for r in range(R)]
        agg_ready = sem("agg_ready")
        agg_turned = sem("agg_turned")
        agg_t_ready = sem("agg_t_ready")
        v_ready = sem("v_ready")
        v_added = sem("v_added")
        silu_ready = sem("silu_ready")
        act_turned = sem("act_turned")
        act_t_ready = sem("act_t_ready")
        y_ready = sem("y_ready")
        x1_ready = sem("x1_ready")
        stats_part = sem("stats_part")
        stats_ready = sem("stats_ready")
        eps_added = sem("eps_added")
        half_ready = sem("half_ready")
        rstd_ready = sem("rstd_ready")
        h2_ready = sem("h2_ready")
        sum_ready = sem("sum_ready")
        h2_turned = sem("h2_turned")
        h2_t_ready = sem("h2_t_ready")
        tokens_ready = sem("tokens_ready")
        l_ready = sem("l_ready")
        block = ctx.enter_context(nc.Block())

        def pipeline(engine, step, last=7):
            for n in range(3 * R):
                step(n // R, n % R, lambda d: n - d >= 0)
            with engine.Fori(3, BINS // R) as j:
                for r in range(R):
                    step(j, r, lambda d: True)
            for n in range(BINS // R * R, BINS + last):
                step(n // R, n % R, lambda d: n - d < BINS)

        def turned_view(ps):
            return ps[:, 0:KC * BIN].rearrange("p (c n) -> p c n", c=KC)

        @block.sync
        def _(sp):
            for dst, src in ((u1b, by_chunks(t["L0_gnn_uW1"][D:2 * D, :])), (u2, by_chunks(t["L0_gnn_uW2"]))):
                sp.dma_start(dst[:], src).then_inc(weights_in, 16)
            for c in range(KC):
                sp.dma_start(rw[:, c, :], t["L0_ffn_router_w"][:, c * P:(c + 1) * P].rearrange("e p -> p e")
                             ).then_inc(weights_in, 16)
            for m, name in enumerate(("L0_ffn_w1", "L0_ffn_w2")):
                sp.dma_start(w["raw"][m][:], t[name].rearrange("e (c p) n -> p e c n", p=P)).then_inc(w["in"], 16)

            def step(j, r, live):
                n = R * j + r
                if live(0):
                    if live(R):
                        sp.wait_ge(v_added, n - R + 1)
                    sp.dma_start(u_row[0:BIN, r, :], dram["u_rows"][ds(n * BIN, BIN), :]).then_inc(u_in[r], 16)
                    if live(R):
                        sp.wait_ge(x1_ready, n - R + 1)
                    sp.dma_start(xh_row[0:BIN, r, :], dram["xh_rows"][ds(n * BIN, BIN), :]).then_inc(xh_in[r], 16)

            pipeline(sp, step, 0)

        @block.gpsimd
        def _(pool):
            nc.gpsimd.memset(half[:], -0.5).then_inc(half_ready, 1)
            pool.wait_ge(half_ready, 1)

            def step(j, r, live):
                n = R * j + r
                if live(6):
                    g, q = n - 6, (r - 6) % R
                    hold(pool, h2_ready, g + 1)
                    nc.gpsimd.tensor_tensor(node_rows[0:BIN, ds(g, 1), :],
                                            h2[0:BIN, q, :].rearrange("p (o f) -> p o f", o=1),
                                            x1[0:BIN, q, :].rearrange("p (o f) -> p o f", o=1), ALU.add
                                            ).then_inc(sum_ready, 1)
                if live(5):
                    q = (r - 5) % R
                    hold(pool, stats_ready, n - 4)
                    nc.gpsimd.tensor_scalar(mv[0:BIN, q, 1:2], mv[0:BIN, q, 1:2], LN_EPS, None, ALU.add
                                            ).then_inc(eps_added, 1)
                if live(7):
                    g, q = n - 7, (r - 7) % R
                    hold(pool, h2_t_ready, g + 1)
                    nc.gpsimd.tensor_copy(tokens_t[:, :, ds(g * BIN, BIN)], h2_t[:, q]).then_inc(tokens_ready, 1)
                if live(5):
                    q = (r - 5) % R
                    pool.wait_ge(eps_added, n - 4)
                    nc.gpsimd.tensor_tensor(rstd[0:BIN, q, :], mv[0:BIN, q, 1:2], half[0:BIN, :], ALU.pow
                                            ).then_inc(rstd_ready, 1)

            pipeline(pool, step)

        @block.scalar
        def _(act):
            def step(j, r, live):
                n = R * j + r
                if live(4):
                    g, q = n - 4, (r - 4) % R
                    act.wait_ge(act_turned, g + 1)
                    if live(4 + R):
                        act.wait_ge(y_ready, g - R + 1)
                    nc.scalar.activation(act1_t[:, q], turned_view(ps_st), ACT.Copy).then_inc(act_t_ready, 1)
                if live(0):
                    if live(R):
                        hold(act, agg_turned, n - R + 1)
                    nc.scalar.activation(agg[0:BIN, r, :], node_rows[0:BIN, ds(n, 1), :].rearrange("p o f -> p (o f)"),
                                         ACT.Copy).then_inc(agg_ready, 1)
                if live(7):
                    g, q = n - 7, (r - 7) % R
                    act.wait_ge(h2_turned, g + 1)
                    if live(7 + R):
                        act.wait_ge(tokens_ready, g - R + 1)
                        act.wait_ge(l_ready, g - R + 1)
                    nc.scalar.activation(h2_t[:, q], turned_view(ps_ht), ACT.Copy).then_inc(h2_t_ready, 1)
                if live(2):
                    g, q = n - 2, (r - 2) % R
                    act.wait_ge(v_added, g + 1)
                    nc.scalar.activation(act1[0:BIN, q, :], act1[0:BIN, q, :], ACT.Silu).then_inc(silu_ready, 1)

            pipeline(act, step)

        @block.tensor
        def _(pe):
            pe.wait_ge(weights_in, 16 * 4)

            def turn(ps, rows):
                for c in range(KC):
                    tr = pe.transpose(ps[:, c * BIN:(c + 1) * BIN], rows[:, c * P:(c + 1) * P], ident[0:BIN, 0:BIN])
                return tr

            def product(ps, rows_t, w):
                for c in range(KC):
                    mm = pe.matmul(ps, rows_t[:, c, :], w[:, c, :], start=(c == 0), stop=(c == KC - 1))
                return mm

            def step(j, r, live):
                n = R * j + r
                if live(2):
                    g, q = n - 2, (r - 2) % R
                    pe.wait_ge(agg_t_ready, g + 1)
                    if live(2 + 2):
                        pe.wait_ge(v_added, g - 1)
                    product(ps_v[r % 2][0:BIN, 0:D], agg_t[:, q], u1b).then_inc(v_ready, 1)
                if live(3):
                    g, q = n - 3, (r - 3) % R
                    pe.wait_ge(silu_ready, g + 1)
                    if live(3 + 1):
                        pe.wait_ge(act_t_ready, g)
                    turn(ps_st, act1[0:BIN, q, :]).then_inc(act_turned, 1)
                if live(4):
                    g, q = n - 4, (r - 4) % R
                    pe.wait_ge(act_t_ready, g + 1)
                    if live(4 + 2):
                        pe.wait_ge(x1_ready, g - 1)
                    product(ps_y[r % 2][0:BIN, 0:D], act1_t[:, q], u2).then_inc(y_ready, 1)
                if live(7):
                    g, q = n - 7, (r - 7) % R
                    pe.wait_ge(h2_t_ready, g + 1)
                    product(ps_logits[0:BIN, ds(g * EXPERTS, EXPERTS)], h2_t[:, q], rw).then_inc(l_ready, 1)
                if live(6):
                    g, q = n - 6, (r - 6) % R
                    pe.wait_ge(h2_ready, g + 1)
                    if live(6 + 1):
                        pe.wait_ge(h2_t_ready, g)
                    turn(ps_ht, h2[0:BIN, q, :]).then_inc(h2_turned, 1)
                if live(0):
                    pe.wait_ge(agg_ready, n + 1)
                    if live(1):
                        pe.wait_ge(agg_t_ready, n)
                    turn(ps_at, agg[0:BIN, r, :]).then_inc(agg_turned, 1)

            pipeline(pe, step)

        @block.vector
        def _(dve):
            def step(j, r, live):
                n = R * j + r
                if live(1):
                    g, q = n - 1, (r - 1) % R
                    dve.wait_ge(agg_turned, g + 1)
                    if live(1 + R):
                        dve.wait_ge(v_ready, g - R + 1)
                    nc.vector.tensor_copy(agg_t[:, q], turned_view(ps_at)).then_inc(agg_t_ready, 1)
                if live(5):
                    g, q = n - 5, (r - 5) % R
                    dve.wait_ge(x1_ready, g + 1)
                    nc.vector.bn_stats(st6[0:BIN, q, :], x1[0:BIN, q, :]).then_inc(stats_part, 1)
                if live(6):
                    g, q = n - 6, (r - 6) % R
                    dve.wait_ge(rstd_ready, g + 1)
                    if live(6 + R):
                        dve.wait_ge(h2_turned, g - R + 1)
                        dve.wait_ge(sum_ready, g - R + 1)
                    nc.vector.tensor_scalar(h2[0:BIN, q, :], x1[0:BIN, q, :], mv[0:BIN, q, 0:1], rstd[0:BIN, q, :],
                                            ALU.subtract, ALU.mult).then_inc(h2_ready, 1)
                if live(2):
                    g, q = n - 2, (r - 2) % R
                    dve.wait_ge(v_ready, g + 1)
                    if live(2 + R):
                        dve.wait_ge(act_turned, g - R + 1)
                    dve.wait_ge(u_in[q], 16 * (j + (r >= 2)))
                    nc.vector.tensor_tensor(act1[0:BIN, q, :], ps_v[r % 2][0:BIN, 0:D], u_row[0:BIN, q, :], ALU.add
                                            ).then_inc(v_added, 1)
                if live(5):
                    g, q = n - 5, (r - 5) % R
                    hold(dve, stats_part, g + 1)
                    nc.vector.bn_aggr(mv[0:BIN, q, :], st6[0:BIN, q, :]).then_inc(stats_ready, 1)
                if live(4):
                    g, q = n - 4, (r - 4) % R
                    dve.wait_ge(y_ready, g + 1)
                    if live(4 + R):
                        dve.wait_ge(sum_ready, g - R + 1)
                    dve.wait_ge(xh_in[q], 16 * j)
                    nc.vector.tensor_tensor(x1[0:BIN, q, :], ps_y[r % 2][0:BIN, 0:D], xh_row[0:BIN, q, :], ALU.add
                                            ).then_inc(x1_ready, 1)

            pipeline(dve, step)


def route(nc, t, ps_logits, combine, w):
    with ExitStack() as ctx:
        def sb(name, shape):
            return ctx.enter_context(nc.sbuf_tensor(name, shape, F32))

        prob = sb("prob", [P, BINS, EXPERTS])
        index = sb("index", [P, BINS, EXPERTS])
        work = sb("work_r", [P, BINS, EXPERTS])
        hot = [sb("hot0", [P, BINS, EXPERTS]), sb("hot1", [P, BINS, EXPERTS])]
        low = sb("low", [P, BINS])
        best = [sb("best0", [P, BINS]), sb("best1", [P, BINS])]
        first = sb("first", [P, BINS])
        total = sb("total", [P, BINS])
        index_ready = ctx.enter_context(nc.semaphore("index_ready"))
        shifted = ctx.enter_context(nc.semaphore("shifted"))
        exp_ready = ctx.enter_context(nc.semaphore("exp_ready"))
        done = ctx.enter_context(nc.semaphore("route_step"))
        b2 = ctx.enter_context(nc.sbuf_tensor("b2", [EXPERTS, 2, D], F32))
        b2_part = ctx.enter_context(nc.sbuf_tensor("b2_part", [EXPERTS, 3, D], BF16))
        b2_dram = nc.dram_tensor("b2_dram", (3, EXPERTS, D), BF16).ap()
        biases_in = ctx.enter_context(nc.semaphore("biases_in"))
        b2_step = ctx.enter_context(nc.semaphore("b2_step"))
        b2_split = ctx.enter_context(nc.semaphore("b2_split"))
        b2_out = ctx.enter_context(nc.semaphore("b2_out"))
        b2_in = ctx.enter_context(nc.semaphore("b2_in"))
        rows_cleared = ctx.enter_context(nc.semaphore("rows_cleared"))
        hi_ready = ctx.enter_context(nc.semaphore("w_hi_ready"))
        block = ctx.enter_context(nc.Block())
        full = [BIN, BINS, EXPERTS]

        def wide(a):
            return a[0:BIN, :].rearrange("p (b o) -> p b o", o=1).broadcast_to(full)

        @block.sync
        def _(sp):
            sp.dma_start(b2[:, 0, :], t["L0_ffn_b2"]).then_inc(biases_in, 16)
            for c in range(KC):
                sp.dma_start(w["b1"][:, c, :], t["L0_ffn_b1"][:, c * P:(c + 1) * P].rearrange("e p -> p e")
                             ).then_inc(biases_in, 16)
            sp.wait_ge(b2_split, 1)
            sp.dma_start(b2_dram.rearrange("n e f -> e n f"), b2_part[:]).then_inc(b2_out, 16)
            sp.wait_ge(b2_out, 16)
            sp.wait_ge(rows_cleared, 1)
            sp.dma_start(w["b2_rows"][0:3, :, :], b2_dram).then_inc(b2_in, 16)
            sp.wait_ge(b2_in, 16)

        @block.gpsimd
        def _(pool):
            nc.gpsimd.iota(index[:], [[0, BINS], [1, EXPERTS]], base=0, channel_multiplier=0,
                           allow_small_or_imprecise_dtypes=True).then_inc(index_ready, 1)
            nc.gpsimd.memset(w["ones3"][:], 1.0)
            nc.gpsimd.memset(w["b2_rows"][:], 0.0).then_inc(rows_cleared, 1)
            pool.wait_ge(biases_in, 16 * (1 + KC))
            for m in range(3):
                a, b = b2[:, m % 2, :], b2[:, (m + 1) % 2, :]
                if m:
                    pool.wait_ge(b2_step, 2 * m)
                part = nc.gpsimd.tensor_copy(b2_part[:, m, :], a)
                if m == 2:
                    part.then_inc(b2_split, 1)
                else:
                    part.then_inc(b2_step, 1)
                    pool.wait_ge(b2_step, 2 * m + 1)
                    nc.gpsimd.tensor_tensor(b, a, b2_part[:, m, :], ALU.subtract).then_inc(b2_step, 1)
            pool.wait_ge(hi_ready, 1)
            nc.gpsimd.tensor_tensor(w["lo"][0][:], w["raw"][0][:], w["hi"][0][:].bitcast(F32), ALU.subtract
                                    )

        @block.scalar
        def _(act):
            act.wait_ge(w["in"], 16 * 2)
            nc.scalar.activation(w["hi"][0][:], w["raw"][0][:], ACT.Copy).then_inc(hi_ready, 1)
            act.wait_ge(shifted, 1)
            nc.scalar.activation(prob[0:BIN], prob[0:BIN], ACT.Exp).then_inc(exp_ready, 1)
            nc.scalar.activation(w["hi"][1][:], w["raw"][1][:], ACT.Copy).then_inc(hi_ready, 1)

        @block.vector
        def _(dve):
            steps = [0]

            def then(ins):
                steps[0] += 1
                ins.then_inc(done, 1)
                dve.wait_ge(done, steps[0])

            c, p, a, idx = combine[0:BIN], prob[0:BIN], work[0:BIN], index[0:BIN]
            logits = ps_logits[0:BIN, 0:BINS * EXPERTS].rearrange("p (b e) -> p b e", e=EXPERTS)
            then(nc.vector.tensor_reduce(low[0:BIN, :], logits, AX_X, ALU.max))
            nc.vector.tensor_tensor(p, logits, wide(low), ALU.subtract).then_inc(shifted, 1)
            dve.wait_ge(exp_ready, 1)
            then(nc.vector.tensor_reduce(low[0:BIN, :], p, AX_X, ALU.add))
            then(nc.vector.reciprocal(total[0:BIN, :], low[0:BIN, :]))
            then(nc.vector.tensor_tensor(p, p, wide(total), ALU.mult))
            dve.wait_ge(index_ready, 1)
            for k in range(2):
                then(nc.vector.tensor_reduce(best[k][0:BIN, :], p, AX_X, ALU.max))
                then(nc.vector.tensor_tensor(a, p, wide(best[k]), ALU.is_lt))
                then(nc.vector.scalar_tensor_tensor(out=a, in0=a, scalar=float(EXPERTS), in1=idx, op0=ALU.mult,
                                                    op1=ALU.add))
                then(nc.vector.tensor_reduce(first[0:BIN, :], a, AX_X, ALU.min))
                then(nc.vector.tensor_tensor(hot[k][0:BIN], idx, wide(first), ALU.is_equal))
                if k == 0:
                    then(nc.vector.scalar_tensor_tensor(out=p, in0=hot[0][0:BIN], scalar=-2.0, in1=p, op0=ALU.mult,
                                                        op1=ALU.add))
                then(nc.vector.tensor_tensor(hot[k][0:BIN], hot[k][0:BIN], wide(best[k]), ALU.mult))
            then(nc.vector.tensor_tensor(total[0:BIN, :], best[0][0:BIN, :], best[1][0:BIN, :], ALU.add))
            then(nc.vector.tensor_scalar(total[0:BIN, :], total[0:BIN, :], 1e-12, None, ALU.max))
            then(nc.vector.reciprocal(low[0:BIN, :], total[0:BIN, :]))
            then(nc.vector.tensor_tensor(a, hot[0][0:BIN], hot[1][0:BIN], ALU.add))
            then(nc.vector.tensor_tensor(c, a, wide(low), ALU.mult))
            dve.wait_ge(hi_ready, 2)
            nc.vector.tensor_tensor(w["lo"][1][:], w["raw"][1][:], w["hi"][1][:].bitcast(F32), ALU.subtract
                                    )


def experts(nc, node_rows, tokens_t, combine, w, out):
    PAIR = 2 * BIN
    E = EXPERTS
    R = 4
    PAIRS = BINS // 2
    w_hi, w_lo, b1, b2_rows, ones3 = w["hi"], w["lo"], w["b1"], w["b2_rows"], w["ones3"]
    with ExitStack() as ctx:
        def sb(name, shape, dt=F32):
            return ctx.enter_context(nc.sbuf_tensor(name, shape, dt))

        def sem(name):
            return ctx.enter_context(nc.semaphore(name))

        tk_hi = sb("tk_hi", [P, KC, PAIR], F32R)
        tk_lo = sb("tk_lo", [P, KC, PAIR], F32R)
        g = sb("g", [P, R, KC, PAIR])
        g_hi = sb("g_hi", [P, R, KC, PAIR], F32R)
        g_lo = sb("g_lo", [P, R, KC, PAIR], F32R)
        ps_h = [ctx.enter_context(nc.psum_tensor(f"ps_h{k}", [P, 512], F32)) for k in range(2)]
        ps_y = [ctx.enter_context(nc.psum_tensor(f"ps_ye{k}", [P, 512], F32)) for k in range(2)]

        tk_split = sem("tk_split")
        tk_ready = sem("tk_ready")
        h_ready = sem("h_ready_e")
        g_ready = sem("g_ready")
        g_hi_ready = sem("g_hi_ready")
        g_lo_ready = sem("g_lo_ready")
        y_ready = sem("y_ready_e")
        added = sem("added_e")
        stored = sem("stored")
        block = ctx.enter_context(nc.Block())

        def pipeline(engine, step, last=0):
            for e in range(E):
                step(0, e, lambda d: e - d >= 0, True)
            with engine.Fori(1, PAIRS - 1) as c:
                for e in range(E):
                    step(c, e, lambda d: True, True)
            for n in range(E * (PAIRS - 1), E * PAIRS + last):
                step(n // E, n % E, lambda d: n - d < E * PAIRS, False)

        @block.sync
        def _(sp):
            with sp.Fori(0, PAIRS - 1) as c:
                sp.wait_ge(added, 2 * E * (c + 1))
                for i in range(2):
                    sp.dma_start(out[ds((2 * c + i) * BIN, BIN), :],
                                 node_rows[0:BIN, ds(2 * c + i, 1), :].rearrange("p o f -> p (o f)")
                                 ).then_inc(stored, 16)
            sp.wait_ge(added, 2 * E * PAIRS)
            sp.dma_start(out[(BINS - 2) * BIN:(BINS - 1) * BIN, :], node_rows[0:BIN, BINS - 2, :]).then_inc(stored, 16)
            sp.dma_start(out[(BINS - 1) * BIN:NODES, :], node_rows[0:LAST, BINS - 1, :]).then_inc(stored, 16)
            sp.wait_ge(stored, 16 * BINS)

        @block.scalar
        def _(act):
            nc.scalar.activation(tk_hi[:], tokens_t[:, :, 0:PAIR], ACT.Copy).then_inc(tk_split, 1)

            def step(c, e, live, more):
                n = E * c + e
                k, r = e % 2, e % R
                if more and e == E - 1:
                    hold(act, h_ready, n + 1)
                    nc.scalar.activation(tk_hi[:], tokens_t[:, :, ds((c + 1) * PAIR, PAIR)], ACT.Copy
                                         ).then_inc(tk_split, 1)
                act.wait_ge(h_ready, n + 1)
                if live(R):
                    act.wait_ge(g_lo_ready, n - R + 1)
                for m in range(KC):
                    gl = nc.scalar.activation(g[:, r, m, :], ps_h[k][:, m * PAIR:(m + 1) * PAIR], ACT.Gelu,
                                              bias=b1[:, m, e:e + 1])
                gl.then_inc(g_ready, 1)
                act.wait_ge(g_ready, n + 1)
                if live(R):
                    act.wait_ge(y_ready, n - R + 1)
                nc.scalar.activation(g_hi[:, r], g[:, r], ACT.Copy).then_inc(g_hi_ready, 1)

            pipeline(act, step)

        @block.tensor
        def _(pe):
            def step(c, e, live, more):
                n = E * c + e
                if live(0):
                    k = e % 2
                    if e == 0:
                        pe.wait_ge(tk_ready, c + 1)
                    if live(2):
                        pe.wait_ge(g_ready, n - 1)
                    for m in range(KC):
                        h = ps_h[k][:, m * PAIR:(m + 1) * PAIR]
                        i = 0
                        for a, tk in ((w_hi, tk_hi), (w_lo, tk_hi), (w_hi, tk_lo)):
                            for q in range(KC):
                                mm = pe.matmul(h, a[0][:, e, q, m * P:(m + 1) * P], tk[:, q, :], start=(i == 0),
                                               stop=(i == 3 * KC - 1))
                                i += 1
                    mm.then_inc(h_ready, 1)
                if live(2):
                    s, d, k, r = n - 2, (e - 2) % E, e % 2, (e - 2) % R
                    pe.wait_ge(g_lo_ready, s + 1)
                    if live(2 + 2):
                        pe.wait_ge(added, 2 * (s - 1))
                    for i in range(2):
                        y = ps_y[k][0:BIN, i * D:(i + 1) * D]
                        rows = slice(i * BIN, (i + 1) * BIN)
                        for q in range(KC):
                            pe.matmul(y, g_hi[:, r, q, rows], w_hi[1][:, d, q, :], start=(q == 0), stop=False)
                            pe.matmul(y, g_hi[:, r, q, rows], w_lo[1][:, d, q, :], start=False, stop=False)
                            pe.matmul(y, g_lo[:, r, q, rows], w_hi[1][:, d, q, :], start=False, stop=False)
                        mm = pe.matmul(y, ones3[:, 0:BIN], b2_rows[:, d, :], start=False, stop=True)
                    mm.then_inc(y_ready, 1)

            pipeline(pe, step, 2)

        @block.vector
        def _(dve):
            def split_tokens(c):
                dve.wait_ge(tk_split, c + 1)
                nc.vector.tensor_tensor(tk_lo[:], tokens_t[:, :, ds(c * PAIR, PAIR)], tk_hi[:].bitcast(F32),
                                        ALU.subtract).then_inc(tk_ready, 1)

            split_tokens(0)

            def step(c, e, live, more):
                n = E * c + e
                if more and e == E - 1:
                    split_tokens(c + 1)
                if live(0):
                    r = e % R
                    dve.wait_ge(g_hi_ready, n + 1)
                    nc.vector.tensor_tensor(g_lo[:, r], g[:, r], g_hi[:, r].bitcast(F32), ALU.subtract
                                            ).then_inc(g_lo_ready, 1)
                if live(2):
                    s, d, k = n - 2, (e - 2) % E, e % 2
                    pair = c if e >= 2 else c - 1
                    dve.wait_ge(y_ready, s + 1)
                    for i in range(2):
                        row = node_rows[0:BIN, ds(2 * pair + i, 1), :]
                        if d:
                            dve.wait_ge(added, 2 * (s - 1) + i + 1)
                        nc.vector.scalar_tensor_tensor(
                            out=row, in0=ps_y[k][0:BIN, i * D:(i + 1) * D].rearrange("p (o f) -> p o f", o=1),
                            scalar=combine[0:BIN, ds(2 * pair + i, 1), d:d + 1].rearrange("p o e -> p (o e)"),
                            in1=row, op0=ALU.mult, op1=ALU.add).then_inc(added, 1)

            pipeline(dve, step, 2)

_OUT = (NODES, D)


def kernel(**inputs):
    import numpy as _np
    import concourse.bacc as _bacc
    from concourse import mybir as _mybir
    from concourse.bass_utils import run_bass_kernel_spmd as _run

    nc = _bacc.Bacc("TRN2", target_bir_lowering=False, num_devices=1)
    arrays, t = {}, {}
    for name in NAMES:
        a = _np.ascontiguousarray(inputs[name])
        arrays[f"in_{name}"] = a
        t[name] = nc.dram_tensor(f"in_{name}", a.shape, _mybir.dt.from_np(a.dtype), kind="ExternalInput").ap()
    out = nc.dram_tensor("out_rows", _OUT, F32, kind="ExternalOutput").ap()
    gnn_ffn(nc, t, out)
    r = _run(nc, [arrays], core_ids=[0])
    return r.results[0]["out_rows"]
```

```python
from contextlib import ExitStack

import concourse.bass as bass
from concourse import mybir

F32 = mybir.dt.float32
F32R = mybir.dt.float32r
BF16 = mybir.dt.bfloat16
I32 = mybir.dt.int32
U32 = mybir.dt.uint32
ALU = mybir.AluOpType
ACT = mybir.ActivationFunctionType
AX_X = mybir.AxisListType.X
ds = bass.ds

P = 128
D = 256
KC = D // P
NODES = 6250
EDGES = 100000
EXPERTS = 8
LN_EPS = 1e-5

BIN = P - 2
BINS = -(-NODES // BIN)
LAST = NODES - (BINS - 1) * BIN

EP, EC = 125, 800
assert EP * EC == EDGES
TILES = (EDGES + (P - 1) * BINS) // P
GROUPS = -(-TILES // 2)
TILES = 2 * GROUPS
RING = 8
TABLE_P = P - 3
TABLE_C = -(-TILES // TABLE_P)
SLOTS = TILES * P
WORDS = 4
CHUNK = 40
ROUND = 1.5 * 2 ** 23

NAMES = ["x", "src", "dst", "edge_weight1", "L0_gnn_mW1", "L0_gnn_mb1", "L0_gnn_ln_g", "L0_gnn_ln_b", "L0_gnn_mW2",
         "L0_gnn_mb2", "L0_gnn_uW1", "L0_gnn_ub1", "L0_gnn_uW2", "L0_gnn_ub2", "L0_ffn_router_w", "L0_ffn_w1",
         "L0_ffn_b1", "L0_ffn_w2", "L0_ffn_b2"]


def hold(engine, semaphore, value):
    engine.wait_ge(semaphore, value)
    engine.nop(nofuse=True)


def by_chunks(w):
    return w.rearrange("(c p) n -> p c n", p=P)


def one_row(v):
    return v.rearrange("(o n) -> o n", o=1)


def gnn_ffn(nc, t, out):
    with ExitStack() as whole:
        whole.enter_context(nc.allow_non_contiguous_dma("small transposed parameters"))
        node_rows = whole.enter_context(nc.sbuf_tensor("node_rows", [P, BINS, D], F32))
        dram = {
            "b_rows": nc.dram_tensor("b_rows", (BINS * BIN, D), F32).ap(),
            "u_rows": nc.dram_tensor("u_rows", (BINS * BIN, D), F32).ap(),
            "xh_rows": nc.dram_tensor("xh_rows", (BINS * BIN, D), F32).ap(),
            "sorted_edges": nc.dram_tensor("sorted_edges", (SLOTS, WORDS), F32).ap(),
            "tile_bins": nc.dram_tensor("tile_bins", (TABLE_P * TABLE_C,), I32).ap(),
        }
        ident = whole.enter_context(nc.sbuf_tensor("ident", [P, P], F32))
        with ExitStack() as edges:
            kept = {
                "a_at": nc.sbuf_base,
                "a_hi": edges.enter_context(nc.sbuf_tensor("a_hi", [P, BINS, D], F32R)),
                "a_lo": edges.enter_context(nc.sbuf_tensor("a_lo", [P, BINS, D], F32R)),
                "slots": edges.enter_context(nc.sbuf_tensor("slots", [P, TILES, WORDS], F32)),
                "w2_hi": edges.enter_context(nc.sbuf_tensor("w2_hi", [P, KC, D], F32R)),
                "w2_lo": edges.enter_context(nc.sbuf_tensor("w2_lo", [P, KC, D], F32R)),
                "iota": edges.enter_context(nc.sbuf_tensor("iota", [P, P], F32)),
            }
            nodes_and_sort(nc, t, dram, node_rows, ident, kept)
            messages(nc, dram, node_rows, ident, kept)
        with ExitStack() as rest:
            turned = rest.enter_context(nc.sbuf_tensor("tokens_t", [P, KC, BINS * BIN], F32))
            combine = rest.enter_context(nc.sbuf_tensor("combine", [P, BINS, EXPERTS], F32))
            w = {"hi": [], "lo": [], "raw": [], "in": rest.enter_context(nc.semaphore("expert_weights_in"))}
            for m in (1, 2):
                shape = [P, EXPERTS, KC, D]
                w["hi"].append(rest.enter_context(nc.sbuf_tensor(f"w{m}_hi_e", shape, F32R)))
                at = nc.sbuf_base
                w["lo"].append(rest.enter_context(nc.sbuf_tensor(f"w{m}_lo_e", shape, F32R)))
                w["raw"].append(nc.alloc_sbuf_tensor_at(f"w{m}_raw", shape, F32, offset=at))
            with nc.psum_tensor("ps_logits", [P, 512], F32) as ps_logits:
                update(nc, t, dram, node_rows, ident, turned, ps_logits, w)
                w["b1"] = rest.enter_context(nc.sbuf_tensor("b1", [P, KC, EXPERTS], F32))
                w["b2_parts"] = rest.enter_context(nc.sbuf_tensor("b2_parts", [3 * EXPERTS, D], F32R))
                w["share_parts"] = rest.enter_context(nc.sbuf_tensor("share_parts", [P, BINS, 3, EXPERTS], F32R))
                route(nc, t, ps_logits, combine, w)
            experts(nc, node_rows, ident, turned, combine, w, out)
def nodes_and_sort(nc, t, dram, node_rows, ident, kept):
    a_hi, a_lo, slots = kept["a_hi"], kept["a_lo"], kept["slots"]
    with ExitStack() as ctx:
        def sb(name, shape, dt=F32):
            return ctx.enter_context(nc.sbuf_tensor(name, shape, dt))

        def sem(name):
            return ctx.enter_context(nc.semaphore(name))

        def psum(name):
            return ctx.enter_context(nc.psum_tensor(name, [P, 512], F32))

        pay = sb("pay", [P, EC, WORDS])
        row_of = sb("row_of", [P, EC], I32)
        stage_row = sb("stage_row", [P, 2, CHUNK], I32)
        stage_pay = sb("stage_pay", [P, 2, CHUNK, WORDS])
        bins_f = sb("bins_f", [P, TABLE_C])
        bins_i = sb("bins_i", [P, TABLE_C], I32)
        tile_no = sb("tile_no", [P, TABLE_C])
        before = sb("before", [P, P])
        ones = sb("ones", [P, P])
        w1a = sb("w1a", [P, KC, D])
        w1b = sb("w1b", [P, KC, D])
        u1a = sb("u1a", [P, KC, D])
        b1_all = sb("b1_all", [P, D])
        ub1_all = sb("ub1_all", [P, D])
        ub2_all = sb("ub2_all", [P, D])
        gcol = sb("gcol", [P, KC])
        bcol = sb("bcol", [P, KC])
        mv = sb("mv", [P, BINS, 2])
        rstd = sb("rstd", [P, BINS])
        half = sb("half", [P, BINS])
        st6 = sb("st6", [P, 6])
        st2 = sb("st2", [P, 2])
        h = sb("h", [P, 2, D])
        ht = sb("ht", [P, 2, KC, BIN])
        u_out = sb("u_out", [P, 2, D])
        xh_out = sb("xh_out", [P, 2, D])
        with ExitStack() as early:
            w2 = early.enter_context(nc.sbuf_tensor("w2", [P, KC, D], F32))
        b_out = sb("b_out", [P, 2, D])

        at = [kept["a_at"]]

        def early_sb(name, shape, dt=F32):
            size = 4
            for n in shape[1:]:
                size *= n
            where = at[0]
            at[0] += -(-size // 32) * 32
            return nc.alloc_sbuf_tensor_at(name, shape, dt, offset=where)

        b2_row = early_sb("b2_row", [1, D])
        minus_c = early_sb("minus_c", [1, D])
        wc = early_sb("wc", [1, D])
        wc_hi = early_sb("wc_hi", [1, D], F32R)
        wc_lo = early_sb("wc_lo", [1, D], F32R)
        at[0] = kept["a_at"] + 4 * BINS * D
        bin_of = early_sb("bin_of", [EP, EC])
        src_f = early_sb("src_f", [EP, EC])
        srci = early_sb("srci", [EP, EC], I32)
        dsti = early_sb("dsti", [EP, EC], I32)
        wgt = early_sb("wgt", [EP, EC])
        waste = [early_sb(f"waste{k}", [EP, EC], BF16) for k in range(2)]
        marks = early_sb("marks", [EP, BINS, CHUNK + 1])
        ranks = early_sb("ranks", [EP, BINS, CHUNK + 1])
        carry = early_sb("carry", [EP, BINS, CHUNK + 1])
        slot = early_sb("slot", [EP, CHUNK])
        tile_of = early_sb("tile_of", [EP, CHUNK])
        rounded = early_sb("rounded", [EP, CHUNK])
        counts = early_sb("counts", [EP, BINS])
        tiles = early_sb("tiles", [TABLE_P, BINS])
        ends = early_sb("ends", [TABLE_P, BINS])
        gtmp = early_sb("gtmp", [TABLE_P, BINS])
        gtmp2 = early_sb("gtmp2", [TABLE_P, BINS])
        ahead = early_sb("ahead", [TABLE_P, TABLE_C, BINS])

        ps_t = [psum("ps_t0"), psum("ps_t1")]
        ps_a, ps_b, ps_u, ps_n, ps_c = (psum(f"ps_{x}") for x in "abunc")

        edges_in = sem("edges_in")
        x_in = sem("x_in")
        params_in = sem("params_in")
        last_clear = sem("last_clear")
        pool_consts = sem("pool_consts")
        masks_cut = sem("masks_cut")
        prep = sem("prep")
        carry_one = sem("carry_one")
        counted = sem("counted")
        summed = sem("summed")
        base_ready = sem("base_ready")
        ranked = sem("ranked")
        chunk_ready = sem("chunk_ready")
        staged = sem("staged")
        scattered = [sem("scattered0"), sem("scattered1")]
        filled = sem("filled")
        cleared = sem("cleared")
        sorted_in = sem("sorted_in")
        table_ready = sem("table_ready")
        table_out = sem("table_out")
        wc_ready = sem("wc_ready")
        wc_out = sem("wc_out")
        c_mul = sem("c_mul")
        w2_centred = sem("w2_centred")
        w2_split = sem("w2_split")
        stats = sem("stats")
        var_ready = sem("var_ready")
        rstd_ready = sem("rstd_ready")
        h_ready = sem("h_ready")
        h_turned = sem("h_turned")
        ht_ready = sem("ht_ready")
        node_mul = sem("node_mul")
        a_hi_ready = sem("a_hi_ready")
        a_lo_ready = sem("a_lo_ready")
        xh_part = sem("xh_part")
        outs_ready = sem("outs_ready")
        outs_stored = [sem("outs_stored0"), sem("outs_stored1")]
        block = ctx.enter_context(nc.Block())
        n_params = 13
        STEPS = 10
        CHUNKS = EC // CHUNK
        FIRST = 9 * CHUNKS // 20

        @block.sync
        def _(sp):
            for dst, name in ((srci, "src"), (dsti, "dst")):
                sp.dma_start(dst[:], t[name].rearrange("(p c) -> p c", p=EP)).then_inc(edges_in, 16)
            sp.dma_start(wgt[:], t["edge_weight1"].rearrange("(p c) o -> p (c o)", p=EP)).then_inc(edges_in, 16)
            sp.dma_start(node_rows[0:BIN, 0:BINS - 1, :],
                         t["x"][0:(BINS - 1) * BIN, :].rearrange("(b p) f -> p b f", p=BIN)).then_inc(x_in, 16)
            sp.wait_ge(last_clear, 1)
            sp.dma_start(node_rows[0:LAST, BINS - 1, :], t["x"][(BINS - 1) * BIN:, :]).then_inc(x_in, 16)
            sp.wait_ge(cleared, 1)
            sp.dma_start(dram["sorted_edges"].rearrange("(p t) w -> p t w", p=P), slots[:]).then_inc(filled, 16)
            sp.wait_ge(table_ready, 1)
            sp.dma_start(dram["tile_bins"].rearrange("(p j) -> p j", p=TABLE_P), bins_i[0:TABLE_P, :]
                         ).then_inc(table_out, 16)
            sp.wait_ge(wc_ready, 1)
            for table, row in ((a_hi, wc_hi), (a_lo, wc_lo)):
                for p in (BIN, BIN + 1):
                    sp.dma_start(table[p:p + 1, :, :].bitcast(F32),
                                 row[0:1, :].bitcast(F32).rearrange("p (o f) -> p o f", o=1)
                                 .broadcast_to([1, BINS, D])).then_inc(wc_out, 16)
            with sp.Fori(0, BINS // 2) as j:
                for k in range(2):
                    i = 2 * j + k
                    sp.wait_ge(outs_ready, 3 * i + 3)
                    for buf, name in ((b_out, "b_rows"), (u_out, "u_rows"), (xh_out, "xh_rows")):
                        sp.dma_start(dram[name][ds(i * BIN, BIN), :], buf[0:BIN, k, :]).then_inc(outs_stored[k], 16)
            for k in range(2):
                sp.wait_ge(scattered[k], 16 * EC // 2)
            sp.dma_start(slots[:], dram["sorted_edges"].rearrange("(p t) w -> p t w", p=P)).then_inc(sorted_in, 16)
            sp.wait_ge(sorted_in, 16)
            for k in range(2):
                sp.wait_ge(outs_stored[k], 16 * 3 * BINS // 2)
            sp.wait_ge(wc_out, 16 * 4)
            sp.wait_ge(table_out, 16)

        @block.gpsimd
        def _(pool):
            nc.gpsimd.memset(ident[:], 0.0).then_inc(pool_consts, 1)
            nc.gpsimd.memset(before[:], 1.0).then_inc(pool_consts, 1)
            nc.gpsimd.memset(ones[:], 1.0).then_inc(pool_consts, 1)
            nc.gpsimd.memset(half[:], -0.5).then_inc(pool_consts, 1)
            nc.gpsimd.iota(kept["iota"][:], [[1, P]], base=0, channel_multiplier=0,
                           allow_small_or_imprecise_dtypes=True).then_inc(pool_consts, 1)
            nc.gpsimd.iota(tile_no[:], [[1, TABLE_C]], base=0, channel_multiplier=TABLE_C,
                           allow_small_or_imprecise_dtypes=True).then_inc(pool_consts, 1)
            pool.wait_ge(pool_consts, 6)
            nc.gpsimd.affine_select(out=ident[:], in_=ident[:], compare_op=ALU.not_equal, fill=1.0, base=0,
                                    pattern=[[-1, P]], channel_multiplier=1).then_inc(masks_cut, 1)
            nc.gpsimd.affine_select(out=before[:], in_=before[:], compare_op=ALU.is_ge, fill=0.0, base=-1,
                                    pattern=[[1, P]], channel_multiplier=-1).then_inc(masks_cut, 1)

            def stage_and_scatter(j, k, first):
                s = 2 * j + k
                if not first:
                    hold(pool, scattered[k], 16 * CHUNK * j)
                nc.gpsimd.tensor_copy(stage_row[0:EP, k, :], row_of[0:EP, ds(s * CHUNK, CHUNK)]).then_inc(staged, 1)
                nc.gpsimd.tensor_copy(stage_pay[0:EP, k], pay[0:EP, ds(s * CHUNK, CHUNK), :]).then_inc(staged, 1)
                hold(pool, staged, 2 * s + 2)
                for c in range(CHUNK):
                    nc.gpsimd.indirect_dma_start(
                        dram["sorted_edges"], bass.IndirectOffsetOnAxis(ap=stage_row[0:EP, k, c:c + 1], axis=0),
                        stage_pay[0:EP, k, c, :], None).then_inc(scattered[k], 16)

            pool.wait_ge(filled, 16)
            pool.wait_ge(chunk_ready, 1)
            stage_and_scatter(0, 0, True)
            pool.wait_ge(chunk_ready, 2)
            stage_and_scatter(0, 1, True)

            def scatter(first, last):
                with pool.Fori(first, last) as j:
                    for k in range(2):
                        hold(pool, chunk_ready, 2 * j + k + 1)
                        stage_and_scatter(j, k, False)

            scatter(1, FIRST // 2)
            pool.wait_ge(var_ready, 1)
            nc.gpsimd.tensor_tensor(rstd[0:BIN, :], mv[0:BIN, :, 1], half[0:BIN, :], ALU.pow).then_inc(rstd_ready, 1)
            scatter(FIRST // 2, CHUNKS // 2)

        @block.scalar
        def _(act):
            mw1, uw1 = t["L0_gnn_mW1"], t["L0_gnn_uW1"]
            for dst, src in ((w1a, by_chunks(mw1[0:D, :])), (w1b, by_chunks(mw1[D:2 * D, :])),
                             (u1a, by_chunks(uw1[0:D, :])), (w2, by_chunks(t["L0_gnn_mW2"]))):
                act.dma_start(dst[:], src).then_inc(params_in, 16)
            for dst, name in ((b1_all, "L0_gnn_mb1"), (ub1_all, "L0_gnn_ub1"), (ub2_all, "L0_gnn_ub2")):
                act.dma_start(dst[:], one_row(t[name]).broadcast_to([P, D])).then_inc(params_in, 16)
            act.dma_start(wc[:], mw1[2 * D:2 * D + 1, :]).then_inc(params_in, 16)
            act.dma_start(b2_row[:], one_row(t["L0_gnn_mb2"])).then_inc(params_in, 16)
            for dst, name in ((gcol, "L0_gnn_ln_g"), (bcol, "L0_gnn_ln_b")):
                for c in range(KC):
                    act.dma_start(dst[:, c:c + 1], t[name][c * P:(c + 1) * P].rearrange("(p o) -> p o", o=1)
                                  ).then_inc(params_in, 16)

            def copies(i, k, first):
                act.wait_ge(h_turned, i + 1)
                if not first:
                    act.wait_ge(node_mul, i - 1)
                nc.scalar.activation(ht[:, k], ps_t[k][:, 0:KC * BIN].rearrange("p (c n) -> p c n", c=KC),
                                     ACT.Copy).then_inc(ht_ready, 1)
                hold(act, node_mul, i + 1)
                nc.scalar.activation(a_hi[0:BIN, ds(i, 1), :], ps_a[0:BIN, 0:D].rearrange("p (o f) -> p o f", o=1),
                                     ACT.Copy).then_inc(a_hi_ready, 1)

            copies(0, 0, True)
            copies(1, 1, True)
            with act.Fori(1, BINS // 2) as j:
                for k in range(2):
                    copies(2 * j + k, k, False)

        @block.tensor
        def _(pe):
            pe.wait_ge(masks_cut, 2)
            pe.wait_ge(counted, BINS)
            pe.matmul(ps_n[:, 0:BINS], before[0:EP, :], counts[:], start=True, stop=True)
            pe.matmul(ps_n[:, BINS:2 * BINS], ones[0:EP, :], counts[:], start=True, stop=True).then_inc(summed, 1)
            pe.wait_ge(params_in, 16 * n_params)
            for c in range(KC):
                mm = pe.matmul(ps_c[0:1, 0:D], bcol[:, c:c + 1], w2[:, c, :], start=(c == 0), stop=(c == KC - 1))
            mm.then_inc(c_mul, 1)
            pe.wait_ge(w2_split, 4)
            for c in range(KC):
                pe.matmul(ps_n[:, 0:D], ones[:], w2[:, c, :], start=(c == 0), stop=False)
            pe.matmul(ps_n[:, 0:D], ones[0:1, :], minus_c[:], start=False, stop=True).then_inc(c_mul, 1)

            def products(i, k, first):
                pe.wait_ge(h_ready, i + 1)
                for c in range(KC):
                    tr = pe.transpose(ps_t[k][:, c * BIN:(c + 1) * BIN], h[0:BIN, k, c * P:(c + 1) * P],
                                      ident[0:BIN, 0:BIN])
                tr.then_inc(h_turned, 1)
                pe.wait_ge(ht_ready, i + 1)
                if not first:
                    pe.wait_ge(outs_ready, 3 * i)
                    pe.wait_ge(a_lo_ready, i)
                for ps, w in ((ps_a, w1a), (ps_b, w1b), (ps_u, u1a)):
                    for c in range(KC):
                        mm = pe.matmul(ps[0:BIN, 0:D], ht[:, k, c, :], w[:, c, :], start=(c == 0),
                                       stop=(c == KC - 1))
                mm.then_inc(node_mul, 1)

            products(0, 0, True)
            products(1, 1, False)
            with pe.Fori(1, BINS // 2) as j:
                for k in range(2):
                    products(2 * j + k, k, False)

        @block.vector
        def _(dve):
            nc.vector.memset(node_rows[:, BINS - 1, :], 0.0).then_inc(last_clear, 1)
            nc.vector.memset(slots[:], 0.0).then_inc(prep, 1)
            dve.wait_ge(prep, 1)
            nc.vector.memset(slots[:, :, 1:2], -1.0).then_inc(cleared, 1)
            nc.vector.memset(carry[:], 1.0).then_inc(carry_one, 1)
            dve.wait_ge(carry_one, 1)
            nc.vector.memset(carry[:, :, 0:1], 0.0).then_inc(ranked, 1)
            dve.wait_ge(edges_in, 16 * 3)
            nc.vector.tensor_copy(pay[0:EP, :, 0].bitcast(I32), dsti[:]).then_inc(prep, 1)
            nc.vector.tensor_copy(pay[0:EP, :, 2].bitcast(F32R), wgt[:]).then_inc(prep, 1)
            nc.vector.tensor_copy(src_f[:], srci[:]).then_inc(prep, 1)
            dve.wait_ge(prep, 4)
            nc.vector.tensor_tensor(pay[0:EP, :, 3].bitcast(F32R), wgt[:], pay[0:EP, :, 2],
                                    ALU.subtract).then_inc(prep, 1)
            nc.vector.tensor_scalar(bin_of[:], src_f[:], 1.0 / BIN, 0.5 / BIN - 0.5, ALU.mult,
                                    ALU.add).then_inc(prep, 1)
            dve.wait_ge(prep, 6)
            nc.vector.tensor_scalar(wgt[:], bin_of[:], ROUND, None, ALU.add).then_inc(prep, 1)
            dve.wait_ge(prep, 7)
            nc.vector.tensor_scalar(bin_of[:], wgt[:], -ROUND, None, ALU.add).then_inc(prep, 1)
            dve.wait_ge(prep, 8)
            nc.vector.scalar_tensor_tensor(out=pay[0:EP, :, 1], in0=bin_of[:], scalar=-float(BIN),
                                           in1=src_f[:], op0=ALU.mult, op1=ALU.add).then_inc(prep, 1)
            dve.wait_ge(pool_consts, 6)
            dve.wait_ge(prep, 9)

            def count(j, k, first):
                b = 2 * j + k
                if not first:
                    dve.wait_ge(counted, b - 1)
                nc.vector.tensor_scalar(waste[k][:], bin_of[:], kept["iota"][0:EP, ds(b, 1)], 0.0,
                                        ALU.is_equal, ALU.add, accum_out=counts[:, ds(b, 1)]).then_inc(counted, 1)

            count(0, 0, True)
            count(0, 1, True)
            with dve.Fori(1, BINS // 2) as j:
                for k in range(2):
                    count(j, k, False)
            dve.wait_ge(summed, 1)
            nc.vector.tensor_scalar(gtmp[:], ps_n[0:TABLE_P, BINS:2 * BINS], 1.0 / P,
                                    (P - 1.0) / P - 0.5 + 0.5 / P, ALU.mult, ALU.add
                                    ).then_inc(base_ready, 1)
            dve.wait_ge(base_ready, 1)
            nc.vector.tensor_scalar(gtmp2[:], gtmp[:], ROUND, None, ALU.add).then_inc(base_ready, 1)
            dve.wait_ge(base_ready, 2)
            nc.vector.tensor_scalar(tiles[:], gtmp2[:], -ROUND, None, ALU.add).then_inc(base_ready, 1)
            dve.wait_ge(base_ready, 3)
            nc.vector.tensor_tensor_scan(ends[:], tiles[:], tiles[:], 0.0, ALU.add, ALU.max
                                         ).then_inc(base_ready, 1)
            dve.wait_ge(base_ready, 4)
            nc.vector.tensor_tensor(gtmp[:], ends[:], tiles[:], ALU.subtract).then_inc(base_ready, 1)
            dve.wait_ge(base_ready, 5)
            nc.vector.scalar_tensor_tensor(out=ranks[:, :, CHUNK:CHUNK + 1],
                                           in0=gtmp[0:EP, :].rearrange("p (b o) -> p b o", o=1), scalar=float(P),
                                           in1=ps_n[0:EP, 0:BINS].rearrange("p (b o) -> p b o", o=1), op0=ALU.mult,
                                           op1=ALU.add).then_inc(base_ready, 1)
            table = [TABLE_P, TABLE_C, BINS]
            nc.vector.tensor_tensor(ahead[:], ends[:].rearrange("p (o b) -> p o b", o=1).broadcast_to(table),
                                    tile_no[0:TABLE_P, :].rearrange("p (j o) -> p j o", o=1).broadcast_to(table),
                                    ALU.is_le).then_inc(base_ready, 1)
            dve.wait_ge(base_ready, 7)
            nc.vector.tensor_reduce(bins_f[0:TABLE_P, :], ahead[:], AX_X, ALU.add).then_inc(base_ready, 1)
            dve.wait_ge(base_ready, 8)
            nc.vector.tensor_scalar(bins_i[0:TABLE_P, :], bins_f[0:TABLE_P, :], float(BINS - 1), None, ALU.min
                                    ).then_inc(table_ready, 1)

            with dve.Fori(0, CHUNKS) as n:
                cols = ds(n * CHUNK, CHUNK)
                step = STEPS * n + 1
                dve.wait_ge(ranked, step)
                nc.vector.tensor_tensor(
                    marks[:, :, 1:], bin_of[:, cols].rearrange("p (o c) -> p o c", o=1).broadcast_to([EP, BINS, CHUNK]),
                    kept["iota"][0:EP, 0:BINS].rearrange("p (b o) -> p b o", o=1).broadcast_to([EP, BINS, CHUNK]),
                    ALU.is_equal).then_inc(ranked, 1)
                nc.vector.tensor_scalar(marks[:, :, 0:1], ranks[:, :, CHUNK:], 0.0, None, ALU.add).then_inc(ranked, 1)
                dve.wait_ge(ranked, step + 2)
                nc.vector.tensor_tensor_scan(ranks[:].rearrange("p b c -> p (b c)"),
                                             carry[:].rearrange("p b c -> p (b c)"),
                                             marks[:].rearrange("p b c -> p (b c)"), 0.0, ALU.mult, ALU.add
                                             ).then_inc(ranked, 1)
                dve.wait_ge(ranked, step + 3)
                nc.vector.tensor_tensor(marks[:, :, 1:], marks[:, :, 1:], ranks[:, :, 1:], ALU.mult
                                        ).then_inc(ranked, 1)
                hold(dve, ranked, step + 4)
                nc.vector.tensor_reduce(slot[:], marks[:, :, 1:].rearrange("p b c -> p c b"), AX_X, ALU.add
                                        ).then_inc(ranked, 1)
                dve.wait_ge(ranked, step + 5)
                nc.vector.tensor_scalar(tile_of[:], slot[:], 1.0 / P, -1.0 / P - 0.5 + 0.5 / P, ALU.mult,
                                        ALU.add).then_inc(ranked, 1)
                dve.wait_ge(ranked, step + 6)
                nc.vector.tensor_scalar(rounded[:], tile_of[:], ROUND, None, ALU.add).then_inc(ranked, 1)
                dve.wait_ge(ranked, step + 7)
                nc.vector.tensor_scalar(tile_of[:], rounded[:], -ROUND, None, ALU.add).then_inc(ranked, 1)
                dve.wait_ge(ranked, step + 8)
                nc.vector.scalar_tensor_tensor(out=rounded[:], in0=tile_of[:], scalar=-float(P), in1=slot[:],
                                               op0=ALU.mult, op1=ALU.add).then_inc(ranked, 1)
                dve.wait_ge(ranked, step + 9)
                nc.vector.tensor_scalar(slot[:], rounded[:], float(TILES), -float(TILES), ALU.mult, ALU.add
                                        ).then_inc(ranked, 1)
                dve.wait_ge(ranked, step + 10)
                nc.vector.tensor_tensor(row_of[0:EP, cols], slot[:], tile_of[:], ALU.add).then_inc(chunk_ready, 1)

            dve.wait_ge(x_in, 32)
            with dve.Fori(0, BINS) as i:
                nc.vector.bn_stats(st6[0:BIN, :], node_rows[0:BIN, ds(i, 1), :].rearrange("p o f -> p (o f)")
                                   ).then_inc(stats, 1)
                hold(dve, stats, 3 * i + 1)
                nc.vector.bn_aggr(st2[0:BIN, :], st6[0:BIN, :]).then_inc(stats, 1)
                dve.wait_ge(stats, 3 * i + 2)
                nc.vector.tensor_scalar(mv[0:BIN, ds(i, 1), :], st2[0:BIN, :].rearrange("p (o f) -> p o f", o=1),
                                        0.0, None, ALU.add).then_inc(stats, 1)
                hold(dve, stats, 3 * i + 3)
            nc.vector.tensor_scalar(mv[0:BIN, :, 1], mv[0:BIN, :, 1], LN_EPS, None, ALU.add).then_inc(var_ready, 1)
            dve.wait_ge(params_in, 16 * n_params)
            nc.vector.tensor_copy(wc_hi[:], wc[:]).then_inc(w2_split, 1)
            dve.wait_ge(c_mul, 1)
            for c in range(KC):
                nc.vector.tensor_scalar(w2[:, c, :], w2[:, c, :], gcol[:, c:c + 1], None, ALU.mult
                                        ).then_inc(w2_split, 1)
            nc.vector.scalar_tensor_tensor(out=minus_c[:], in0=b2_row[:], scalar=-1.0, in1=ps_c[0:1, 0:D],
                                           op0=ALU.mult, op1=ALU.subtract).then_inc(w2_split, 1)
            dve.wait_ge(w2_split, 4)
            nc.vector.tensor_tensor(wc_lo[:], wc[:], wc_hi[:].bitcast(F32), ALU.subtract).then_inc(wc_ready, 1)
            dve.wait_ge(c_mul, 2)
            for c in range(KC):
                centred = nc.vector.scalar_tensor_tensor(out=w2[:, c, :], in0=ps_n[:, 0:D], scalar=-1.0 / D,
                                                         in1=w2[:, c, :], op0=ALU.mult, op1=ALU.add)
            centred.then_inc(w2_centred, 1)
            dve.wait_ge(w2_centred, 1)
            nc.vector.tensor_copy(kept["w2_hi"][:], w2[:]).then_inc(w2_split, 1)
            dve.wait_ge(w2_split, 5)
            nc.vector.tensor_tensor(kept["w2_lo"][:], w2[:], kept["w2_hi"][:].bitcast(F32), ALU.subtract)

            def node(j, k, first):
                i = 2 * j + k
                row = node_rows[0:BIN, ds(i, 1), :].rearrange("p o f -> p (o f)")
                if not first:
                    dve.wait_ge(h_turned, i - 1)
                    dve.wait_ge(outs_stored[k], 16 * 3 * j)
                nc.vector.tensor_scalar(h[0:BIN, k, :], row, mv[0:BIN, ds(i, 1), 0:1].rearrange("p o f -> p (o f)"),
                                        rstd[0:BIN, ds(i, 1)], ALU.subtract, ALU.mult).then_inc(h_ready, 1)
                dve.wait_ge(h_ready, i + 1)
                nc.vector.tensor_tensor(xh_out[0:BIN, k, :], h[0:BIN, k, :], row, ALU.add).then_inc(xh_part, 1)
                dve.wait_ge(xh_part, i + 1)
                nc.vector.tensor_tensor(xh_out[0:BIN, k, :], xh_out[0:BIN, k, :], ub2_all[0:BIN, :], ALU.add
                                        ).then_inc(outs_ready, 1)
                dve.wait_ge(node_mul, i + 1)
                nc.vector.tensor_tensor(b_out[0:BIN, k, :], ps_b[0:BIN, 0:D], b1_all[0:BIN, :], ALU.add
                                        ).then_inc(outs_ready, 1)
                nc.vector.tensor_tensor(u_out[0:BIN, k, :], ps_u[0:BIN, 0:D], ub1_all[0:BIN, :], ALU.add
                                        ).then_inc(outs_ready, 1)
                dve.wait_ge(a_hi_ready, i + 1)
                nc.vector.tensor_tensor(a_lo[0:BIN, ds(i, 1), :],
                                        ps_a[0:BIN, 0:D].rearrange("p (o f) -> p o f", o=1),
                                        a_hi[0:BIN, ds(i, 1), :].bitcast(F32), ALU.subtract).then_inc(a_lo_ready, 1)

            dve.wait_ge(rstd_ready, 1)
            dve.wait_ge(chunk_ready, CHUNKS)
            dve.wait_ge(wc_out, 16 * 4)
            node(0, 0, True)
            node(0, 1, True)
            with dve.Fori(1, BINS // 2) as j:
                for k in range(2):
                    node(j, k, False)

def messages(nc, dram, node_rows, ident, kept):
    a_hi, a_lo, slots, iota = kept["a_hi"], kept["a_lo"], kept["slots"], kept["iota"]
    w2_hi, w2_lo = kept["w2_hi"], kept["w2_lo"]
    with ExitStack() as ctx:
        def sb(name, shape, dt=F32):
            return ctx.enter_context(nc.sbuf_tensor(name, shape, dt))

        def sem(name):
            return ctx.enter_context(nc.semaphore(name))

        tile_bin = sb("tile_bin", [1, TABLE_P * TABLE_C], I32)
        dst_row = sb("dst_row", [P, RING, 2], I32)
        onehot = sb("onehot", [P, RING, 2, P])
        onehot_t = sb("onehot_t", [P, 2, 2, P], F32R)
        rows = [sb(f"rows{r}", [P, 2, D]) for r in range(RING)]
        st6 = sb("st6_m", [P, 2, 6])
        mv = sb("mv_m", [P, RING, 2, 2])
        rstd = sb("rstd_m", [P, RING, 2])
        shift = sb("shift", [P, RING, 2])
        half = sb("half_m", [P, 2])
        one = sb("one_m", [P, 1])
        t_hi = sb("t_hi", [P, 2, 2, KC, P], F32R)
        t_lo = sb("t_lo", [P, 2, 2, KC, P], F32R)

        def psum(name, n=2, width=512):
            return [ctx.enter_context(nc.psum_tensor(f"{name}{k}", [P, width], F32)) for k in range(n)]

        ps_oh = ctx.enter_context(nc.psum_tensor("ps_oh", [P, 512], F32))
        ps_pre = psum("ps_pre")
        ps_rt = psum("ps_rt")
        ps_z = psum("ps_z")
        ps_agg = ctx.enter_context(nc.psum_tensor("ps_agg", [P, 512], F32))

        table_in = sem("table_in")
        start = sem("start")
        dst_ready = sem("dst_ready")
        b_landed = [sem(f"b_landed{r}") for r in range(RING)]
        onehot_ready = sem("onehot_ready")
        onehot_turned = sem("onehot_turned")
        onehot_t_ready = sem("onehot_t_ready")
        a_gathered = sem("a_gathered")
        pre_ready = sem("pre_ready")
        silu_ready = sem("silu_ready")
        tile_stats = sem("tile_stats")
        stats_ready = sem("stats_ready")
        eps_added = sem("eps_added")
        rstd_ready = sem("rstd_ready")
        shift_ready = sem("shift_ready")
        norm_ready = sem("norm_ready")
        rows_turned = sem("rows_turned")
        hi_ready = sem("hi_ready")
        lo_ready = sem("lo_ready")
        z_ready = sem("z_ready")
        msg_ready = sem("msg_ready")
        part_ready = sem("part_ready")
        added = sem("added")
        block = ctx.enter_context(nc.Block())

        def pipeline(engine, step, last):
            for n in range(2 * RING):
                step(n // RING, n % RING, lambda d: n - d >= 0)
            with engine.Fori(1, GROUPS // (2 * RING)) as j:
                for turn in range(2):
                    for r in range(RING):
                        step(2 * j + turn, r, lambda d: True)
            for n in range(GROUPS // (2 * RING) * 2 * RING, GROUPS + last):
                step(n // RING, n % RING, lambda d: n - d < GROUPS)

        @block.sync
        def _(sp):
            sp.dma_start(tile_bin[:], one_row(dram["tile_bins"])).then_inc(table_in, 16)
            sp.wait_ge(table_in, 16)

        @block.gpsimd
        def _(pool):
            nc.gpsimd.memset(half[:], -0.5).then_inc(start, 1)
            pool.wait_ge(start, 1)

            def step(j, r, live):
                n = RING * j + r
                if live(0):
                    if live(RING):
                        hold(pool, part_ready, n - RING + 1)
                    hold(pool, dst_ready, n + 1)
                    for i in range(2):
                        nc.gpsimd.indirect_dma_start(
                            rows[r][:, i, :], None, dram["b_rows"],
                            bass.IndirectOffsetOnAxis(ap=dst_row[:, r, i:i + 1], axis=0)).then_inc(b_landed[r], 16)
                if live(2):
                    g, q = n - 2, (r - 2) % RING
                    hold(pool, stats_ready, g + 1)
                    nc.gpsimd.tensor_scalar(mv[:, q, :, 1], mv[:, q, :, 1], 1.0, LN_EPS, ALU.mult,
                                            ALU.add).then_inc(eps_added, 1)
                    pool.wait_ge(eps_added, g + 1)
                    nc.gpsimd.tensor_tensor(rstd[:, q, :], mv[:, q, :, 1], half[:], ALU.pow).then_inc(rstd_ready, 1)

            pipeline(pool, step, 2)

        @block.scalar
        def _(act):
            def place_rows(n, r):
                nc.scalar.activation(dst_row[:, r, :], slots[:, ds(2 * n, 2), 0].bitcast(I32), ACT.Copy
                                     ).then_inc(dst_ready, 1)

            place_rows(0, 0)

            def step(j, r, live):
                n = RING * j + r
                if live(-1):
                    place_rows(n + 1, (r + 1) % RING)
                if live(4):
                    g, q = n - 4, (r - 4) % RING
                    act.wait_ge(shift_ready, g + 1)
                    for i in range(2):
                        nm = nc.scalar.activation(rows[q][:, i, :], rows[q][:, i, :], ACT.Identity,
                                                  bias=shift[:, q, i:i + 1], scale=rstd[:, q, i:i + 1])
                    nm.then_inc(norm_ready, 1)
                if live(6):
                    g, k = n - 6, (r - 6) % 2
                    act.wait_ge(z_ready, g + 1)
                    nc.scalar.activation(rows[(r - 6) % RING][:], ps_z[k][:].rearrange("p (i n) -> p i n", i=2), ACT.Silu
                                         ).then_inc(msg_ready, 1)
                if live(0):
                    k = r % 2
                    act.wait_ge(onehot_turned, n + 1)
                    if live(2):
                        act.wait_ge(a_gathered, n - 1)
                    nc.scalar.activation(onehot_t[:, k], ps_oh[:, 0:2 * P].rearrange("p (i n) -> p i n", i=2),
                                         ACT.Copy).then_inc(onehot_t_ready, 1)
                if live(4):
                    g, k = n - 4, (r - 4) % 2
                    act.wait_ge(rows_turned, g + 1)
                    if live(4 + 2):
                        act.wait_ge(z_ready, g - 1)
                    nc.scalar.activation(t_hi[:, k].rearrange("p i c e -> p (i c e)"), ps_rt[k][:], ACT.Copy
                                         ).then_inc(hi_ready, 1)
                if live(1):
                    g, x = n - 1, rows[(r - 1) % RING]
                    act.wait_ge(pre_ready, g + 1)
                    nc.scalar.activation(x[:], x[:], ACT.Silu).then_inc(silu_ready, 1)

            pipeline(act, step, 6)

        @block.tensor
        def _(pe):
            pe.wait_ge(table_in, 16)

            def step(j, r, live):
                n = RING * j + r
                if live(1):
                    b = [pe.value_load(tile_bin[0:1, ds(2 * (n - 1) + i, 1)], min_val=0, max_val=BINS - 1)
                         for i in range(2)]
                if live(1):
                    g, k = n - 1, (r - 1) % 2
                    pe.wait_ge(onehot_t_ready, g + 1)
                    if live(1 + 2):
                        pe.wait_ge(pre_ready, g - 1)
                    for i in range(2):
                        pre = ps_pre[k][:, i * D:(i + 1) * D]
                        pe.matmul(pre, onehot_t[:, k, i, :], a_hi[:, ds(b[i], 1), :].rearrange("p o f -> p (o f)"),
                                  start=True, stop=False)
                        mm = pe.matmul(pre, onehot_t[:, k, i, :],
                                       a_lo[:, ds(b[i], 1), :].rearrange("p o f -> p (o f)"), start=False, stop=True)
                    mm.then_inc(a_gathered, 1)
                if live(0):
                    pe.wait_ge(onehot_ready, n + 1)
                    if live(1):
                        pe.wait_ge(onehot_t_ready, n)
                    for i in range(2):
                        tr = pe.transpose(ps_oh[:, i * P:(i + 1) * P], onehot[:, r, i, :], ident[:])
                    tr.then_inc(onehot_turned, 1)
                if live(4):
                    g, k, q = n - 4, (r - 4) % 2, (r - 4) % RING
                    pe.wait_ge(norm_ready, g + 1)
                    if live(4 + 2):
                        pe.wait_ge(lo_ready, g - 1)
                    for i in range(2):
                        for c in range(KC):
                            tr = pe.transpose(ps_rt[k][:, (i * KC + c) * P:(i * KC + c + 1) * P],
                                              rows[q][:, i, c * P:(c + 1) * P], ident[:])
                    tr.then_inc(rows_turned, 1)
                if live(6):
                    g, k, q = n - 6, (r - 6) % 2, (r - 6) % RING
                    pe.wait_ge(msg_ready, g + 1)
                    if live(6 + 1):
                        pe.wait_ge(added, 2 * g + 1)
                    for i in range(2):
                        mm = pe.matmul(ps_agg[0:BIN, i * D:(i + 1) * D], onehot[:, q, i, 0:BIN], rows[q][:, i, :],
                                       start=True, stop=True)
                    mm.then_inc(part_ready, 1)
                if live(5):
                    g, k = n - 5, (r - 5) % 2
                    pe.wait_ge(lo_ready, g + 1)
                    if live(5 + 2):
                        pe.wait_ge(msg_ready, g - 1)
                    for i in range(2):
                        z = ps_z[k][:, i * D:(i + 1) * D]
                        for c in range(KC):
                            pe.matmul(z, t_hi[:, k, i, c, :], w2_hi[:, c, :], start=(c == 0), stop=False)
                            pe.matmul(z, t_hi[:, k, i, c, :], w2_lo[:, c, :], start=False, stop=False)
                            mm = pe.matmul(z, t_lo[:, k, i, c, :], w2_hi[:, c, :], start=False, stop=(c == KC - 1))
                    mm.then_inc(z_ready, 1)

            pipeline(pe, step, 6)

        @block.vector
        def _(dve):
            nc.vector.memset(one[:], 1.0)
            nc.vector.memset(node_rows[:], 0.0).then_inc(added, 1)
            dve.wait_ge(table_in, 16)

            def step(j, r, live):
                n = RING * j + r
                b = {}
                if live(7):
                    b[0] = dve.value_load(tile_bin[0:1, ds(2 * (n - 7) + 0, 1)], min_val=0, max_val=BINS - 1)
                if live(7):
                    b[1] = dve.value_load(tile_bin[0:1, ds(2 * (n - 7) + 1, 1)], min_val=0, max_val=BINS - 1)

                def add_sums(i, d):
                    g = n - d
                    dve.wait_ge(part_ready, g + 1)
                    dve.wait_ge(added, 2 * g + i + 1)
                    sums = node_rows[0:BIN, ds(b[i], 1), :]
                    nc.vector.tensor_tensor(sums, sums, ps_agg[0:BIN, i * D:(i + 1) * D]
                                            .rearrange("p (o f) -> p o f", o=1), ALU.add).then_inc(added, 1)

                if live(4):
                    g, q = n - 4, (r - 4) % RING
                    dve.wait_ge(rstd_ready, g + 1)
                    for i in range(2):
                        sh = nc.vector.scalar_tensor_tensor(
                            out=shift[:, q, i:i + 1], in0=mv[:, q, i, 0:1], scalar=rstd[:, q, i:i + 1], in1=one[:],
                            op0=ALU.mult, op1=ALU.subtract, reverse1=True)
                    sh.then_inc(shift_ready, 1)
                if live(0):
                    if live(RING):
                        dve.wait_ge(part_ready, n - RING + 1)
                    tiles = slots[:, ds(2 * n, 2), :]
                    nc.vector.tensor_tensor(
                        onehot[:, r, :, 0:BIN],
                        iota[:, 0:BIN].rearrange("p (o n) -> p o n", o=1).broadcast_to([P, 2, BIN]),
                        tiles[:, :, 1:2].broadcast_to([P, 2, BIN]), ALU.is_equal)
                    nc.vector.tensor_copy(onehot[:, r, :, BIN:P], tiles[:, :, 2:4]).then_inc(onehot_ready, 1)
                if live(7):
                    add_sums(0, 7)
                if live(2):
                    g, q = n - 2, (r - 2) % RING
                    dve.wait_ge(silu_ready, g + 1)
                    for i in range(2):
                        nc.vector.bn_stats(st6[:, i, :], rows[q][:, i, :]).then_inc(tile_stats, 1)
                if live(7):
                    add_sums(1, 7)
                if live(5):
                    g, k = n - 5, (r - 5) % 2
                    dve.wait_ge(hi_ready, g + 1)
                    if live(2):
                        dve.wait_ge(tile_stats, 2 * (n - 2) + 2)
                    nc.vector.tensor_tensor(t_lo[:, k].rearrange("p i c e -> p (i c e)"), ps_rt[k][:],
                                            t_hi[:, k].rearrange("p i c e -> p (i c e)").bitcast(F32),
                                            ALU.subtract).then_inc(lo_ready, 1)
                if live(2):
                    g, q = n - 2, (r - 2) % RING
                    if not live(5):
                        dve.wait_ge(tile_stats, 2 * g + 2)
                    for i in range(2):
                        ag = nc.vector.bn_aggr(mv[:, q, i, :], st6[:, i, :])
                    ag.then_inc(stats_ready, 1)
                if live(1):
                    g, q = n - 1, (r - 1) % RING
                    dve.wait_ge(a_gathered, g + 1)
                    dve.wait_ge(b_landed[q], 32 * (j + (r >= 1)))
                    x = rows[q][:].rearrange("p i f -> p (i f)")
                    nc.vector.tensor_tensor(x, x, ps_pre[q % 2][:], ALU.add).then_inc(pre_ready, 1)

            pipeline(dve, step, 7)

def update(nc, t, dram, node_rows, ident, tokens_t, ps_logits, w):
    R = 4
    with ExitStack() as ctx:
        def sb(name, shape, dt=F32):
            return ctx.enter_context(nc.sbuf_tensor(name, shape, dt))

        def sem(name):
            return ctx.enter_context(nc.semaphore(name))

        def psum(name):
            return ctx.enter_context(nc.psum_tensor(name, [P, 512], F32))

        u1b = sb("u1b", [P, KC, D])
        u2 = sb("u2", [P, KC, D])
        rw = sb("rw", [P, KC, EXPERTS])
        u_row = sb("u_row", [P, R, D])
        xh_row = sb("xh_row", [P, R, D])
        agg = sb("agg", [P, R, D])
        agg_t = sb("agg_t", [P, R, KC, BIN])
        act1 = sb("act1", [P, R, D])
        act1_t = sb("act1_t", [P, R, KC, BIN])
        x1 = sb("x1", [P, R, D])
        h2 = sb("h2", [P, R, D])
        h2_t = sb("h2_t", [P, R, KC, BIN])
        st6 = sb("st6_u", [P, R, 6])
        mv = sb("mv_u", [P, R, 2])
        rstd = sb("rstd_u", [P, R, 1])
        half = sb("half_u", [P, 1])
        ps_at, ps_st, ps_ht = (psum(f"ps_{x}") for x in ("at", "st", "ht"))
        ps_v = [psum("ps_v0"), psum("ps_v1")]
        ps_y = [psum("ps_y0"), psum("ps_y1")]

        weights_in = sem("weights_in")
        u_in = [sem(f"u_in{r}") for r in range(R)]
        xh_in = [sem(f"xh_in{r}") for r in range(R)]
        agg_ready = sem("agg_ready")
        agg_turned = sem("agg_turned")
        agg_t_ready = sem("agg_t_ready")
        v_ready = sem("v_ready")
        v_added = sem("v_added")
        silu_ready = sem("silu_ready")
        act_turned = sem("act_turned")
        act_t_ready = sem("act_t_ready")
        y_ready = sem("y_ready")
        x1_ready = sem("x1_ready")
        stats_part = sem("stats_part")
        stats_ready = sem("stats_ready")
        eps_added = sem("eps_added")
        half_ready = sem("half_ready")
        rstd_ready = sem("rstd_ready")
        h2_ready = sem("h2_ready")
        sum_ready = sem("sum_ready")
        h2_turned = sem("h2_turned")
        h2_t_ready = sem("h2_t_ready")
        l_ready = sem("l_ready")
        w_hi_ready = sem("w_hi_ready")
        block = ctx.enter_context(nc.Block())

        def pipeline(engine, step, last=7):
            for n in range(3 * R):
                step(n // R, n % R, lambda d: n - d >= 0)
            with engine.Fori(3, BINS // R) as j:
                for r in range(R):
                    step(j, r, lambda d: True)
            for n in range(BINS // R * R, BINS + last):
                step(n // R, n % R, lambda d: n - d < BINS)

        def weights_step(n):
            e = n - BINS // R * R if isinstance(n, int) else -1
            return e if 0 <= e < EXPERTS else None

        def turned_view(ps):
            return ps[:, 0:KC * BIN].rearrange("p (c n) -> p c n", c=KC)

        @block.sync
        def _(sp):
            for dst, src in ((u1b, by_chunks(t["L0_gnn_uW1"][D:2 * D, :])), (u2, by_chunks(t["L0_gnn_uW2"]))):
                sp.dma_start(dst[:], src).then_inc(weights_in, 16)
            for c in range(KC):
                sp.dma_start(rw[:, c, :], t["L0_ffn_router_w"][:, c * P:(c + 1) * P].rearrange("e p -> p e")
                             ).then_inc(weights_in, 16)
            for m, name in enumerate(("L0_ffn_w1", "L0_ffn_w2")):
                sp.dma_start(w["raw"][m][:], t[name].rearrange("e (c p) n -> p e c n", p=P)).then_inc(w["in"], 16)

            def step(j, r, live):
                n = R * j + r
                if live(0):
                    if live(R):
                        sp.wait_ge(v_added, n - R + 1)
                    sp.dma_start(u_row[0:BIN, r, :], dram["u_rows"][ds(n * BIN, BIN), :]).then_inc(u_in[r], 16)
                    if live(R):
                        sp.wait_ge(x1_ready, n - R + 1)
                    sp.dma_start(xh_row[0:BIN, r, :], dram["xh_rows"][ds(n * BIN, BIN), :]).then_inc(xh_in[r], 16)

            pipeline(sp, step, 0)

        @block.gpsimd
        def _(pool):
            nc.gpsimd.memset(half[:], -0.5).then_inc(half_ready, 1)
            pool.wait_ge(half_ready, 1)

            def step(j, r, live):
                n = R * j + r
                if live(6):
                    g, q = n - 6, (r - 6) % R
                    hold(pool, h2_ready, g + 1)
                    nc.gpsimd.tensor_tensor(node_rows[0:BIN, ds(g, 1), :],
                                            h2[0:BIN, q, :].rearrange("p (o f) -> p o f", o=1),
                                            x1[0:BIN, q, :].rearrange("p (o f) -> p o f", o=1), ALU.add
                                            ).then_inc(sum_ready, 1)
                if live(5):
                    q = (r - 5) % R
                    hold(pool, stats_ready, n - 4)
                    nc.gpsimd.tensor_scalar(mv[0:BIN, q, 1:2], mv[0:BIN, q, 1:2], 1.0, LN_EPS, ALU.mult,
                                            ALU.add).then_inc(eps_added, 1)
                if live(5):
                    q = (r - 5) % R
                    pool.wait_ge(eps_added, n - 4)
                    nc.gpsimd.tensor_tensor(rstd[0:BIN, q, :], mv[0:BIN, q, 1:2], half[0:BIN, :], ALU.pow
                                            ).then_inc(rstd_ready, 1)

            pipeline(pool, step)

        @block.scalar
        def _(act):
            def step(j, r, live):
                n = R * j + r
                if live(4):
                    g, q = n - 4, (r - 4) % R
                    act.wait_ge(act_turned, g + 1)
                    if live(4 + R):
                        act.wait_ge(y_ready, g - R + 1)
                    nc.scalar.activation(act1_t[:, q], turned_view(ps_st), ACT.Copy).then_inc(act_t_ready, 1)
                if live(0):
                    if live(R):
                        hold(act, agg_turned, n - R + 1)
                    nc.scalar.activation(agg[0:BIN, r, :], node_rows[0:BIN, ds(n, 1), :].rearrange("p o f -> p (o f)"),
                                         ACT.Copy).then_inc(agg_ready, 1)
                if live(8):
                    g, q = n - 8, (r - 8) % R
                    hold(act, h2_t_ready, g + 1)
                    nc.scalar.activation(tokens_t[:, :, ds(g * BIN, BIN)], h2_t[:, q], ACT.Copy)
                if live(7):
                    g, q = n - 7, (r - 7) % R
                    act.wait_ge(h2_turned, g + 1)
                    if live(7 + R):
                        act.wait_ge(l_ready, g - R + 1)
                    nc.scalar.activation(h2_t[:, q], turned_view(ps_ht), ACT.Copy).then_inc(h2_t_ready, 1)
                if live(2):
                    g, q = n - 2, (r - 2) % R
                    act.wait_ge(v_added, g + 1)
                    nc.scalar.activation(act1[0:BIN, q, :], act1[0:BIN, q, :], ACT.Silu).then_inc(silu_ready, 1)
                e = weights_step(n)
                if e is not None:
                    if e == 0:
                        act.wait_ge(w["in"], 16 * 2)
                    for m in range(2):
                        nc.scalar.activation(w["hi"][m][:, e], w["raw"][m][:, e], ACT.Copy).then_inc(w_hi_ready, 1)

            pipeline(act, step, 8)

        @block.tensor
        def _(pe):
            pe.wait_ge(weights_in, 16 * 4)

            def turn(ps, rows):
                for c in range(KC):
                    tr = pe.transpose(ps[:, c * BIN:(c + 1) * BIN], rows[:, c * P:(c + 1) * P], ident[0:BIN, 0:BIN])
                return tr

            def product(ps, rows_t, w):
                for c in range(KC):
                    mm = pe.matmul(ps, rows_t[:, c, :], w[:, c, :], start=(c == 0), stop=(c == KC - 1))
                return mm

            def step(j, r, live):
                n = R * j + r
                if live(2):
                    g, q = n - 2, (r - 2) % R
                    pe.wait_ge(agg_t_ready, g + 1)
                    if live(2 + 2):
                        pe.wait_ge(v_added, g - 1)
                    product(ps_v[r % 2][0:BIN, 0:D], agg_t[:, q], u1b).then_inc(v_ready, 1)
                if live(3):
                    g, q = n - 3, (r - 3) % R
                    pe.wait_ge(silu_ready, g + 1)
                    if live(3 + 1):
                        pe.wait_ge(act_t_ready, g)
                    turn(ps_st, act1[0:BIN, q, :]).then_inc(act_turned, 1)
                if live(4):
                    g, q = n - 4, (r - 4) % R
                    pe.wait_ge(act_t_ready, g + 1)
                    if live(4 + 2):
                        pe.wait_ge(x1_ready, g - 1)
                    product(ps_y[r % 2][0:BIN, 0:D], act1_t[:, q], u2).then_inc(y_ready, 1)
                if live(7):
                    g, q = n - 7, (r - 7) % R
                    pe.wait_ge(h2_t_ready, g + 1)
                    product(ps_logits[0:BIN, ds(g * EXPERTS, EXPERTS)], h2_t[:, q], rw).then_inc(l_ready, 1)
                if live(6):
                    g, q = n - 6, (r - 6) % R
                    pe.wait_ge(h2_ready, g + 1)
                    if live(6 + 1):
                        pe.wait_ge(h2_t_ready, g)
                    turn(ps_ht, h2[0:BIN, q, :]).then_inc(h2_turned, 1)
                if live(0):
                    pe.wait_ge(agg_ready, n + 1)
                    if live(1):
                        pe.wait_ge(agg_t_ready, n)
                    turn(ps_at, agg[0:BIN, r, :]).then_inc(agg_turned, 1)

            pipeline(pe, step)

        @block.vector
        def _(dve):
            def step(j, r, live):
                n = R * j + r
                if live(1):
                    g, q = n - 1, (r - 1) % R
                    dve.wait_ge(agg_turned, g + 1)
                    if live(1 + R):
                        dve.wait_ge(v_ready, g - R + 1)
                    nc.vector.tensor_copy(agg_t[:, q], turned_view(ps_at)).then_inc(agg_t_ready, 1)
                if live(5):
                    g, q = n - 5, (r - 5) % R
                    dve.wait_ge(x1_ready, g + 1)
                    nc.vector.bn_stats(st6[0:BIN, q, :], x1[0:BIN, q, :]).then_inc(stats_part, 1)
                if live(6):
                    g, q = n - 6, (r - 6) % R
                    dve.wait_ge(rstd_ready, g + 1)
                    if live(6 + R):
                        dve.wait_ge(h2_turned, g - R + 1)
                        dve.wait_ge(sum_ready, g - R + 1)
                    nc.vector.tensor_scalar(h2[0:BIN, q, :], x1[0:BIN, q, :], mv[0:BIN, q, 0:1], rstd[0:BIN, q, :],
                                            ALU.subtract, ALU.mult).then_inc(h2_ready, 1)
                if live(2):
                    g, q = n - 2, (r - 2) % R
                    dve.wait_ge(v_ready, g + 1)
                    if live(2 + R):
                        dve.wait_ge(act_turned, g - R + 1)
                    dve.wait_ge(u_in[q], 16 * (j + (r >= 2)))
                    nc.vector.tensor_tensor(act1[0:BIN, q, :], ps_v[r % 2][0:BIN, 0:D], u_row[0:BIN, q, :], ALU.add
                                            ).then_inc(v_added, 1)
                if live(5):
                    g, q = n - 5, (r - 5) % R
                    hold(dve, stats_part, g + 1)
                    nc.vector.bn_aggr(mv[0:BIN, q, :], st6[0:BIN, q, :]).then_inc(stats_ready, 1)
                if live(4):
                    g, q = n - 4, (r - 4) % R
                    dve.wait_ge(y_ready, g + 1)
                    if live(4 + R):
                        dve.wait_ge(sum_ready, g - R + 1)
                    dve.wait_ge(xh_in[q], 16 * j)
                    nc.vector.tensor_tensor(x1[0:BIN, q, :], ps_y[r % 2][0:BIN, 0:D], xh_row[0:BIN, q, :], ALU.add
                                            ).then_inc(x1_ready, 1)
                e = weights_step(n)
                if e is not None:
                    for m in range(2):
                        dve.wait_ge(w_hi_ready, 2 * e + m + 1)
                        nc.vector.tensor_tensor(w["lo"][m][:, e], w["raw"][m][:, e], w["hi"][m][:, e].bitcast(F32),
                                                ALU.subtract)

            pipeline(dve, step)


def route(nc, t, ps_logits, combine, w):
    with ExitStack() as ctx:
        def sb(name, shape):
            return ctx.enter_context(nc.sbuf_tensor(name, shape, F32))

        prob = sb("prob", [P, BINS, EXPERTS])
        index = sb("index", [P, BINS, EXPERTS])
        work = sb("work_r", [P, BINS, EXPERTS])
        hot = [sb("hot0", [P, BINS, EXPERTS]), sb("hot1", [P, BINS, EXPERTS])]
        low = sb("low", [P, BINS])
        best = [sb("best0", [P, BINS]), sb("best1", [P, BINS])]
        first = sb("first", [P, BINS])
        total = sb("total", [P, BINS])
        index_ready = ctx.enter_context(nc.semaphore("index_ready"))
        shifted = ctx.enter_context(nc.semaphore("shifted"))
        exp_ready = ctx.enter_context(nc.semaphore("exp_ready"))
        done = ctx.enter_context(nc.semaphore("route_step"))
        b2 = ctx.enter_context(nc.sbuf_tensor("b2", [EXPERTS, D], F32))
        b2_lo = ctx.enter_context(nc.sbuf_tensor("b2_lo", [EXPERTS, D], F32R))
        biases_in = ctx.enter_context(nc.semaphore("biases_in"))
        b2_split = ctx.enter_context(nc.semaphore("b2_split"))
        b2_placed = ctx.enter_context(nc.semaphore("b2_placed"))
        block = ctx.enter_context(nc.Block())
        full = [BIN, BINS, EXPERTS]
        E = EXPERTS

        def wide(a):
            return a[0:BIN, :].rearrange("p (b o) -> p b o", o=1).broadcast_to(full)

        @block.sync
        def _(sp):
            sp.dma_start(b2[:], t["L0_ffn_b2"]).then_inc(biases_in, 16)
            for c in range(KC):
                sp.dma_start(w["b1"][:, c, :], t["L0_ffn_b1"][:, c * P:(c + 1) * P].rearrange("e p -> p e")
                             ).then_inc(biases_in, 16)
            sp.wait_ge(b2_split, 2)
            sp.dma_start(w["b2_parts"][E:2 * E, :].bitcast(F32), w["b2_parts"][0:E, :].bitcast(F32)
                         ).then_inc(b2_placed, 16)
            sp.dma_start(w["b2_parts"][2 * E:3 * E, :].bitcast(F32), b2_lo[:].bitcast(F32)).then_inc(b2_placed, 16)
            sp.wait_ge(b2_placed, 32)

        @block.gpsimd
        def _(pool):
            nc.gpsimd.iota(index[:], [[0, BINS], [1, EXPERTS]], base=0, channel_multiplier=0,
                           allow_small_or_imprecise_dtypes=True).then_inc(index_ready, 1)
            pool.wait_ge(biases_in, 16 * (1 + KC))
            nc.gpsimd.tensor_copy(w["b2_parts"][0:E, :], b2[:]).then_inc(b2_split, 1)
            pool.wait_ge(b2_split, 1)
            nc.gpsimd.tensor_tensor(b2_lo[:], b2[:], w["b2_parts"][0:E, :].bitcast(F32), ALU.subtract
                                    ).then_inc(b2_split, 1)

        @block.scalar
        def _(act):
            act.wait_ge(shifted, 1)
            nc.scalar.activation(prob[0:BIN], prob[0:BIN], ACT.Exp).then_inc(exp_ready, 1)

        @block.vector
        def _(dve):
            steps = [0]

            def then(ins):
                steps[0] += 1
                ins.then_inc(done, 1)
                dve.wait_ge(done, steps[0])

            c, p, a, idx = combine[0:BIN], prob[0:BIN], work[0:BIN], index[0:BIN]
            logits = ps_logits[0:BIN, 0:BINS * EXPERTS].rearrange("p (b e) -> p b e", e=EXPERTS)
            then(nc.vector.tensor_reduce(low[0:BIN, :], logits, AX_X, ALU.max))
            nc.vector.tensor_tensor(p, logits, wide(low), ALU.subtract).then_inc(shifted, 1)
            dve.wait_ge(exp_ready, 1)
            then(nc.vector.tensor_reduce(low[0:BIN, :], p, AX_X, ALU.add))
            then(nc.vector.reciprocal(total[0:BIN, :], low[0:BIN, :]))
            then(nc.vector.tensor_tensor(p, p, wide(total), ALU.mult))
            dve.wait_ge(index_ready, 1)
            for k in range(2):
                then(nc.vector.tensor_reduce(best[k][0:BIN, :], p, AX_X, ALU.max))
                then(nc.vector.tensor_tensor(a, p, wide(best[k]), ALU.is_lt))
                then(nc.vector.scalar_tensor_tensor(out=a, in0=a, scalar=float(EXPERTS), in1=idx, op0=ALU.mult,
                                                    op1=ALU.add))
                then(nc.vector.tensor_reduce(first[0:BIN, :], a, AX_X, ALU.min))
                then(nc.vector.tensor_tensor(hot[k][0:BIN], idx, wide(first), ALU.is_equal))
                if k == 0:
                    then(nc.vector.scalar_tensor_tensor(out=p, in0=hot[0][0:BIN], scalar=-2.0, in1=p, op0=ALU.mult,
                                                        op1=ALU.add))
                then(nc.vector.tensor_tensor(hot[k][0:BIN], hot[k][0:BIN], wide(best[k]), ALU.mult))
            then(nc.vector.tensor_tensor(total[0:BIN, :], best[0][0:BIN, :], best[1][0:BIN, :], ALU.add))
            then(nc.vector.tensor_scalar(total[0:BIN, :], total[0:BIN, :], 1e-12, None, ALU.max))
            then(nc.vector.reciprocal(low[0:BIN, :], total[0:BIN, :]))
            then(nc.vector.tensor_tensor(a, hot[0][0:BIN], hot[1][0:BIN], ALU.add))
            then(nc.vector.tensor_tensor(c, a, wide(low), ALU.mult))
            parts = w["share_parts"][0:BIN]
            nc.vector.tensor_copy(parts[:, :, 2, :], c)
            then(nc.vector.tensor_copy(parts[:, :, 0, :], c))
            nc.vector.tensor_tensor(parts[:, :, 1, :], c, parts[:, :, 0, :].bitcast(F32), ALU.subtract)


def experts(nc, node_rows, ident, tokens_t, combine, w, out):
    PAIR = 2 * BIN
    E = EXPERTS
    R = 4
    PAIRS = BINS // 2
    w_hi, w_lo, b1, b2_parts, share_parts = w["hi"], w["lo"], w["b1"], w["b2_parts"], w["share_parts"]
    with ExitStack() as ctx:
        def sb(name, shape, dt=F32):
            return ctx.enter_context(nc.sbuf_tensor(name, shape, dt))

        def sem(name):
            return ctx.enter_context(nc.semaphore(name))

        tk_hi = sb("tk_hi", [P, KC, PAIR], F32R)
        tk_lo = sb("tk_lo", [P, KC, PAIR], F32R)
        g = sb("g", [P, R, KC, PAIR])
        g_hi = sb("g_hi", [P, R, KC, PAIR], F32R)
        g_lo = sb("g_lo", [P, R, KC, PAIR], F32R)
        ps_h = [ctx.enter_context(nc.psum_tensor(f"ps_h{k}", [P, 512], F32)) for k in range(2)]
        ps_y = [ctx.enter_context(nc.psum_tensor(f"ps_ye{k}", [P, 512], F32)) for k in range(2)]
        ps_s = ctx.enter_context(nc.psum_tensor("ps_s", [P, 512], F32))
        ps_b2 = ctx.enter_context(nc.psum_tensor("ps_b2", [P, 512], F32))
        shares = sb("shares", [P, 2, 3 * E])
        shares_t = sb("shares_t", [3 * E, PAIR], F32R)

        tk_split = sem("tk_split")
        tk_ready = sem("tk_ready")
        h_ready = sem("h_ready_e")
        g_ready = sem("g_ready")
        g_hi_ready = sem("g_hi_ready")
        g_lo_ready = sem("g_lo_ready")
        y_ready = sem("y_ready_e")
        shares_ready = sem("shares_ready")
        shares_turned = sem("shares_turned")
        shares_t_ready = sem("shares_t_ready")
        b2_ready = sem("b2_ready")
        b2_added = sem("b2_added")
        added = sem("added_e")
        stored = sem("stored")
        block = ctx.enter_context(nc.Block())

        def pipeline(engine, step, last=0):
            for e in range(E):
                step(0, e, lambda d: e - d >= 0, True)
            with engine.Fori(1, PAIRS - 1) as c:
                for e in range(E):
                    step(c, e, lambda d: True, True)
            for n in range(E * (PAIRS - 1), E * PAIRS + last):
                step(n // E, n % E, lambda d: n - d < E * PAIRS, False)

        @block.sync
        def _(sp):
            with sp.Fori(0, PAIRS - 1) as c:
                sp.wait_ge(added, 2 * E * (c + 1))
                for i in range(2):
                    sp.dma_start(out[ds((2 * c + i) * BIN, BIN), :],
                                 node_rows[0:BIN, ds(2 * c + i, 1), :].rearrange("p o f -> p (o f)")
                                 ).then_inc(stored, 16)
            sp.wait_ge(added, 2 * E * PAIRS)
            sp.dma_start(out[(BINS - 2) * BIN:(BINS - 1) * BIN, :], node_rows[0:BIN, BINS - 2, :]).then_inc(stored, 16)
            sp.dma_start(out[(BINS - 1) * BIN:NODES, :], node_rows[0:LAST, BINS - 1, :]).then_inc(stored, 16)
            sp.wait_ge(stored, 16 * BINS)

        @block.scalar
        def _(act):
            nc.scalar.activation(tk_hi[:], tokens_t[:, :, 0:PAIR], ACT.Copy).then_inc(tk_split, 1)

            def step(c, e, live, more):
                n = E * c + e
                k, r = e % 2, e % R
                if more and e == E - 1:
                    hold(act, h_ready, n + 1)
                    nc.scalar.activation(tk_hi[:], tokens_t[:, :, ds((c + 1) * PAIR, PAIR)], ACT.Copy
                                         ).then_inc(tk_split, 1)
                act.wait_ge(h_ready, n + 1)
                if live(R):
                    act.wait_ge(g_lo_ready, n - R + 1)
                for m in range(KC):
                    gl = nc.scalar.activation(g[:, r, m, :], ps_h[k][:, m * PAIR:(m + 1) * PAIR], ACT.Gelu,
                                              bias=b1[:, m, e:e + 1])
                gl.then_inc(g_ready, 1)
                act.wait_ge(g_ready, n + 1)
                if live(R):
                    act.wait_ge(y_ready, n - R + 1)
                nc.scalar.activation(g_hi[:, r], g[:, r], ACT.Copy).then_inc(g_hi_ready, 1)
                if e == 0:
                    nc.scalar.activation(shares[0:BIN], share_parts[0:BIN, ds(2 * c, 2), :, :].bitcast(F32)
                                         .rearrange("p i n e -> p i (n e)"), ACT.Copy).then_inc(shares_ready, 1)
                if e == 2:
                    act.wait_ge(shares_turned, c + 1)
                    nc.scalar.activation(shares_t[:], ps_s[0:3 * E, 0:PAIR], ACT.Copy).then_inc(shares_t_ready, 1)

            pipeline(act, step)

        @block.tensor
        def _(pe):
            def step(c, e, live, more):
                n = E * c + e
                if live(0):
                    k = e % 2
                    if e == 0:
                        pe.wait_ge(tk_ready, c + 1)
                    if live(2):
                        pe.wait_ge(g_ready, n - 1)
                    for m in range(KC):
                        h = ps_h[k][:, m * PAIR:(m + 1) * PAIR]
                        i = 0
                        for a, tk in ((w_hi, tk_hi), (w_lo, tk_hi), (w_hi, tk_lo)):
                            for q in range(KC):
                                mm = pe.matmul(h, a[0][:, e, q, m * P:(m + 1) * P], tk[:, q, :], start=(i == 0),
                                               stop=(i == 3 * KC - 1))
                                i += 1
                    mm.then_inc(h_ready, 1)
                if live(0) and e == 1:
                    pe.wait_ge(shares_ready, c + 1)
                    for i in range(2):
                        tr = pe.transpose(ps_s[0:3 * E, i * BIN:(i + 1) * BIN], shares[0:BIN, i, :],
                                          ident[0:BIN, 0:BIN])
                    tr.then_inc(shares_turned, 1)
                if live(0) and e == 3:
                    pe.wait_ge(shares_t_ready, c + 1)
                    if live(E):
                        pe.wait_ge(b2_added, 2 * c)
                    for i in range(2):
                        mm = pe.matmul(ps_b2[0:BIN, i * D:(i + 1) * D], shares_t[:, i * BIN:(i + 1) * BIN],
                                       b2_parts[:], start=True, stop=True)
                    mm.then_inc(b2_ready, 1)
                if live(2):
                    s, d, k, r = n - 2, (e - 2) % E, e % 2, (e - 2) % R
                    pe.wait_ge(g_lo_ready, s + 1)
                    if live(2 + 2):
                        pe.wait_ge(added, 2 * (s - 1))
                    for i in range(2):
                        y = ps_y[k][0:BIN, i * D:(i + 1) * D]
                        rows = slice(i * BIN, (i + 1) * BIN)
                        for q in range(KC):
                            pe.matmul(y, g_hi[:, r, q, rows], w_hi[1][:, d, q, :], start=(q == 0), stop=False)
                            pe.matmul(y, g_hi[:, r, q, rows], w_lo[1][:, d, q, :], start=False, stop=False)
                            mm = pe.matmul(y, g_lo[:, r, q, rows], w_hi[1][:, d, q, :], start=False,
                                           stop=(q == KC - 1))
                    mm.then_inc(y_ready, 1)

            pipeline(pe, step, 2)

        @block.vector
        def _(dve):
            def split_tokens(c):
                dve.wait_ge(tk_split, c + 1)
                nc.vector.tensor_tensor(tk_lo[:], tokens_t[:, :, ds(c * PAIR, PAIR)], tk_hi[:].bitcast(F32),
                                        ALU.subtract).then_inc(tk_ready, 1)

            split_tokens(0)

            def step(c, e, live, more):
                n = E * c + e
                if more and e == E - 1:
                    split_tokens(c + 1)
                if live(0):
                    r = e % R
                    dve.wait_ge(g_hi_ready, n + 1)
                    nc.vector.tensor_tensor(g_lo[:, r], g[:, r], g_hi[:, r].bitcast(F32), ALU.subtract
                                            ).then_inc(g_lo_ready, 1)
                if live(2):
                    s, d, k = n - 2, (e - 2) % E, e % 2
                    pair = c if e >= 2 else c - 1
                    dve.wait_ge(y_ready, s + 1)
                    for i in range(2):
                        row = node_rows[0:BIN, ds(2 * pair + i, 1), :]
                        if d:
                            dve.wait_ge(added, 2 * (s - 1) + i + 1)
                        if d == 3:
                            dve.wait_ge(b2_added, 2 * c + i + 1)
                        nc.vector.scalar_tensor_tensor(
                            out=row, in0=ps_y[k][0:BIN, i * D:(i + 1) * D].rearrange("p (o f) -> p o f", o=1),
                            scalar=combine[0:BIN, ds(2 * pair + i, 1), d:d + 1].rearrange("p o e -> p (o e)"),
                            in1=row, op0=ALU.mult, op1=ALU.add).then_inc(added, 1)
                    if d == 2:
                        for i in range(2):
                            row = node_rows[0:BIN, ds(2 * pair + i, 1), :]
                            dve.wait_ge(b2_ready, c + 1)
                            dve.wait_ge(added, 2 * s + i + 1)
                            nc.vector.tensor_tensor(row, row, ps_b2[0:BIN, i * D:(i + 1) * D]
                                                    .rearrange("p (o f) -> p o f", o=1), ALU.add
                                                    ).then_inc(b2_added, 1)

            pipeline(dve, step, 2)

_OUT = (NODES, D)


def kernel(**inputs):
    import numpy as _np
    import concourse.bacc as _bacc
    from concourse import mybir as _mybir
    from concourse.bass_utils import run_bass_kernel_spmd as _run

    nc = _bacc.Bacc("TRN2", target_bir_lowering=False, num_devices=1)
    arrays, t = {}, {}
    for name in NAMES:
        a = _np.ascontiguousarray(inputs[name])
        arrays[f"in_{name}"] = a
        t[name] = nc.dram_tensor(f"in_{name}", a.shape, _mybir.dt.from_np(a.dtype), kind="ExternalInput").ap()
    out = nc.dram_tensor("out_rows", _OUT, F32, kind="ExternalOutput").ap()
    gnn_ffn(nc, t, out)
    r = _run(nc, [arrays], core_ids=[0])
    return r.results[0]["out_rows"]
```
